# Optimizing a Trainium2 kernel written in Bass

```python
import numpy as np
import jax
import jax.numpy as jnp

def _softmax(x, axis=-1):
    return jax.nn.softmax(x, axis=axis)

def _gelu(x):
    return jax.nn.gelu(x, approximate=True)

def _silu(x):
    return jax.nn.silu(x)

def _sigmoid(x):
    return jax.nn.sigmoid(x)

def _layernorm(x, axis=-1, eps=1e-05):
    m = jnp.mean(x, axis=axis, keepdims=True)
    v = jnp.var(x, axis=axis, keepdims=True)
    return (x - m) / jnp.sqrt(v + eps)

def _scatter_add(tgt, idx, src, axis=0):
    return tgt.at[idx].add(src)

def _segment_sum(src, seg, n):
    return jax.ops.segment_sum(src, seg, n)
kernel_name = 'mk_prb_d1_jaxref_r8_68b791'

def setup_inputs(seed: int=0):
    np.random.seed(seed)
    _w = jnp.asarray

    def _L0_attn_setup():
        import jax, jax.numpy as jnp
        import numpy as np
        D_MODEL = 256
        N_HEADS = 16
        HEAD_DIM = D_MODEL // N_HEADS
        B, T = (2, 256)
        key = jax.random.key(seed)
        ks = jax.random.split(key, 9)
        s = 0.02
        x = jax.random.normal(ks[0], (B, T, D_MODEL), dtype=jnp.float32)
        Wq = jax.random.normal(ks[1], (N_HEADS, D_MODEL, HEAD_DIM), dtype=jnp.float32) * s
        bq = jax.random.normal(ks[2], (N_HEADS, HEAD_DIM), dtype=jnp.float32) * s
        Wk = jax.random.normal(ks[3], (N_HEADS, D_MODEL, HEAD_DIM), dtype=jnp.float32) * s
        bk = jax.random.normal(ks[4], (N_HEADS, HEAD_DIM), dtype=jnp.float32) * s
        Wv = jax.random.normal(ks[5], (N_HEADS, D_MODEL, HEAD_DIM), dtype=jnp.float32) * s
        bv = jax.random.normal(ks[6], (N_HEADS, HEAD_DIM), dtype=jnp.float32) * s
        Wo = jax.random.normal(ks[7], (D_MODEL, D_MODEL), dtype=jnp.float32) * s
        bo = jax.random.normal(ks[8], (D_MODEL,), dtype=jnp.float32) * s
        return {'x': x, 'Wq': Wq, 'bq': bq, 'Wk': Wk, 'bk': bk, 'Wv': Wv, 'bv': bv, 'Wo': Wo, 'bo': bo}
    _L0_attn_in = _L0_attn_setup()

    def _L0_ffn_setup():
        import jax, jax.numpy as jnp
        import numpy as np
        B, S, H, I, E, F, K, R, TOPK = (1, 128, 256, 176, 64, 8, 8, 8, 6)
        ISH = 2 * I

        def _fused_linear(x, W, qa, qb, scale, w):
            out = x @ W.T
            a = jnp.einsum('th,krh->tkr', x, qa)
            b = jnp.einsum('tkr,khr->tkh', a, qb)
            mix = jnp.einsum('tkh,tk->th', b, w)
            return out + scale[None, :] * mix

        def _moe_forward(hidden_states, gate_weight, inv_mapping, mask_up_W, gate_W, gate_qa, gate_qb, gate_scale, up_W, up_qa, up_qb, up_scale, down_W, down_qa, down_qb, down_scale, sh_gate_W, sh_up_W, sh_down_W):
            b, s, h = hidden_states.shape
            x = hidden_states.reshape(-1, h)
            T = x.shape[0]
            scores = jax.nn.softmax(x @ gate_weight.T, axis=-1)
            topk_w, topk_idx = jax.lax.top_k(scores, TOPK)
            w_dense = jnp.zeros((T, E), x.dtype).at[jnp.arange(T)[:, None], topk_idx].add(topk_w)
            flat = w_dense[:, inv_mapping]
            scalar = flat.sum(-1)
            soft = jax.nn.softmax(jnp.where(flat == 0, -1000000000.0, flat), axis=-1)

            def expert(muW, gW, gqa, gqb, gs, uW, uqa, uqb, us, dW, dqa, dqb, ds, w):
                xe = x + w @ muW.T
                gate = jax.nn.silu(_fused_linear(xe, gW, gqa, gqb, gs, w))
                up = _fused_linear(xe, uW, uqa, uqb, us, w)
                return _fused_linear(gate * up, dW, dqa, dqb, ds, w)
            outs = jax.vmap(expert, in_axes=(0,) * 13 + (1,))(mask_up_W, gate_W, gate_qa, gate_qb, gate_scale, up_W, up_qa, up_qb, up_scale, down_W, down_qa, down_qb, down_scale, soft)
            y = jnp.einsum('fth,tf->th', outs, scalar).reshape(b, s, h)
            sh = jax.nn.silu(hidden_states @ sh_gate_W.T) * (hidden_states @ sh_up_W.T) @ sh_down_W.T
            return y + sh
        key = jax.random.key(seed)
        ks = jax.random.split(key, 20)
        g = lambda k, shape, s=0.02: jax.random.normal(k, shape, jnp.float32) * s
        return {'hidden_states': jax.random.normal(ks[0], (B, S, H), jnp.float32), 'gate_weight': g(ks[1], (E, H)), 'inv_mapping': jnp.arange(E, dtype=jnp.int32).reshape(F, K), 'mask_up_W': g(ks[2], (F, H, K)), 'gate_W': g(ks[3], (F, I, H)), 'gate_qa': g(ks[4], (F, K, R, H)), 'gate_qb': g(ks[5], (F, K, I, R)), 'gate_scale': jnp.full((F, I), 0.1, jnp.float32), 'up_W': g(ks[6], (F, I, H)), 'up_qa': g(ks[7], (F, K, R, H)), 'up_qb': g(ks[8], (F, K, I, R)), 'up_scale': jnp.full((F, I), 0.1, jnp.float32), 'down_W': g(ks[9], (F, H, I)), 'down_qa': g(ks[10], (F, K, R, I)), 'down_qb': g(ks[11], (F, K, H, R)), 'down_scale': jnp.full((F, H), 0.1, jnp.float32), 'sh_gate_W': g(ks[12], (ISH, H)), 'sh_up_W': g(ks[13], (ISH, H)), 'sh_down_W': g(ks[14], (H, ISH))}
    _L0_ffn_in = _L0_ffn_setup()
    _d = {'L0_attn_x': _L0_attn_in['x'], 'L0_attn_Wq': _L0_attn_in['Wq'], 'L0_attn_bq': _L0_attn_in['bq'], 'L0_attn_Wk': _L0_attn_in['Wk'], 'L0_attn_bk': _L0_attn_in['bk'], 'L0_attn_Wv': _L0_attn_in['Wv'], 'L0_attn_bv': _L0_attn_in['bv'], 'L0_attn_Wo': _L0_attn_in['Wo'], 'L0_attn_bo': _L0_attn_in['bo'], 'L0_ffn_gate_weight': _L0_ffn_in['gate_weight'], 'L0_ffn_inv_mapping': _L0_ffn_in['inv_mapping'], 'L0_ffn_mask_up_W': _L0_ffn_in['mask_up_W'], 'L0_ffn_gate_W': _L0_ffn_in['gate_W'], 'L0_ffn_gate_qa': _L0_ffn_in['gate_qa'], 'L0_ffn_gate_qb': _L0_ffn_in['gate_qb'], 'L0_ffn_gate_scale': _L0_ffn_in['gate_scale'], 'L0_ffn_up_W': _L0_ffn_in['up_W'], 'L0_ffn_up_qa': _L0_ffn_in['up_qa'], 'L0_ffn_up_qb': _L0_ffn_in['up_qb'], 'L0_ffn_up_scale': _L0_ffn_in['up_scale'], 'L0_ffn_down_W': _L0_ffn_in['down_W'], 'L0_ffn_down_qa': _L0_ffn_in['down_qa'], 'L0_ffn_down_qb': _L0_ffn_in['down_qb'], 'L0_ffn_down_scale': _L0_ffn_in['down_scale'], 'L0_ffn_sh_gate_W': _L0_ffn_in['sh_gate_W'], 'L0_ffn_sh_up_W': _L0_ffn_in['sh_up_W'], 'L0_ffn_sh_down_W': _L0_ffn_in['sh_down_W']}
    _x0 = _d['L0_attn_x']
    _d['L0_attn_x'] = jax.random.normal(jax.random.fold_in(jax.random.key(seed), 1), (8, 512, 256), dtype=_x0.dtype)
    del _x0
    return _d

def reference(L0_attn_x, L0_attn_Wq, L0_attn_bq, L0_attn_Wk, L0_attn_bk, L0_attn_Wv, L0_attn_bv, L0_attn_Wo, L0_attn_bo, L0_ffn_gate_weight, L0_ffn_inv_mapping, L0_ffn_mask_up_W, L0_ffn_gate_W, L0_ffn_gate_qa, L0_ffn_gate_qb, L0_ffn_gate_scale, L0_ffn_up_W, L0_ffn_up_qa, L0_ffn_up_qb, L0_ffn_up_scale, L0_ffn_down_W, L0_ffn_down_qa, L0_ffn_down_qb, L0_ffn_down_scale, L0_ffn_sh_gate_W, L0_ffn_sh_up_W, L0_ffn_sh_down_W):

    def _L0_attn_ref(x, Wq, bq, Wk, bk, Wv, bv, Wo, bo):
        import jax, jax.numpy as jnp
        import numpy as np
        D_MODEL = 256
        N_HEADS = 16
        HEAD_DIM = D_MODEL // N_HEADS
        B, T = (2, 256)
        Bn, Tn, C = x.shape
        H, _, D = Wq.shape
        scale = D ** (-0.5)
        q = jnp.einsum('btc,hcd->bhtd', x, Wq) + bq[None, :, None, :]
        k = jnp.einsum('btc,hcd->bhtd', x, Wk) + bk[None, :, None, :]
        v = jnp.einsum('btc,hcd->bhtd', x, Wv) + bv[None, :, None, :]
        scores = jnp.einsum('bhtd,bhsd->bhts', q, k) * scale
        neg = jnp.finfo(scores.dtype).min
        causal = jnp.triu(jnp.full((Tn, Tn), neg, dtype=scores.dtype), k=1)
        probs = jax.nn.softmax(scores + causal, axis=-1)
        y = jnp.einsum('bhts,bhsd->bhtd', probs, v)
        y = y.transpose(0, 2, 1, 3).reshape(Bn, Tn, H * D)
        return y @ Wo + bo

    def _L0_ffn_ref(hidden_states, gate_weight, inv_mapping, mask_up_W, gate_W, gate_qa, gate_qb, gate_scale, up_W, up_qa, up_qb, up_scale, down_W, down_qa, down_qb, down_scale, sh_gate_W, sh_up_W, sh_down_W):
        import jax, jax.numpy as jnp
        import numpy as np
        B, S, H, I, E, F, K, R, TOPK = (1, 128, 256, 176, 64, 8, 8, 8, 6)
        ISH = 2 * I

        def _fused_linear(x, W, qa, qb, scale, w):
            out = x @ W.T
            a = jnp.einsum('th,krh->tkr', x, qa)
            b = jnp.einsum('tkr,khr->tkh', a, qb)
            mix = jnp.einsum('tkh,tk->th', b, w)
            return out + scale[None, :] * mix

        def _moe_forward(hidden_states, gate_weight, inv_mapping, mask_up_W, gate_W, gate_qa, gate_qb, gate_scale, up_W, up_qa, up_qb, up_scale, down_W, down_qa, down_qb, down_scale, sh_gate_W, sh_up_W, sh_down_W):
            b, s, h = hidden_states.shape
            x = hidden_states.reshape(-1, h)
            T = x.shape[0]
            scores = jax.nn.softmax(x @ gate_weight.T, axis=-1)
            topk_w, topk_idx = jax.lax.top_k(scores, TOPK)
            w_dense = jnp.zeros((T, E), x.dtype).at[jnp.arange(T)[:, None], topk_idx].add(topk_w)
            flat = w_dense[:, inv_mapping]
            scalar = flat.sum(-1)
            soft = jax.nn.softmax(jnp.where(flat == 0, -1000000000.0, flat), axis=-1)

            def expert(muW, gW, gqa, gqb, gs, uW, uqa, uqb, us, dW, dqa, dqb, ds, w):
                xe = x + w @ muW.T
                gate = jax.nn.silu(_fused_linear(xe, gW, gqa, gqb, gs, w))
                up = _fused_linear(xe, uW, uqa, uqb, us, w)
                return _fused_linear(gate * up, dW, dqa, dqb, ds, w)
            outs = jax.vmap(expert, in_axes=(0,) * 13 + (1,))(mask_up_W, gate_W, gate_qa, gate_qb, gate_scale, up_W, up_qa, up_qb, up_scale, down_W, down_qa, down_qb, down_scale, soft)
            y = jnp.einsum('fth,tf->th', outs, scalar).reshape(b, s, h)
            sh = jax.nn.silu(hidden_states @ sh_gate_W.T) * (hidden_states @ sh_up_W.T) @ sh_down_W.T
            return y + sh
        return _moe_forward(hidden_states, gate_weight, inv_mapping, mask_up_W, gate_W, gate_qa, gate_qb, gate_scale, up_W, up_qa, up_qb, up_scale, down_W, down_qa, down_qb, down_scale, sh_gate_W, sh_up_W, sh_down_W)
    x = L0_attn_x
    xn = _layernorm(x, axis=-1)
    x = x + _L0_attn_ref(xn, L0_attn_Wq, L0_attn_bq, L0_attn_Wk, L0_attn_bk, L0_attn_Wv, L0_attn_bv, L0_attn_Wo, L0_attn_bo) + _L0_ffn_ref(xn, L0_ffn_gate_weight, L0_ffn_inv_mapping, L0_ffn_mask_up_W, L0_ffn_gate_W, L0_ffn_gate_qa, L0_ffn_gate_qb, L0_ffn_gate_scale, L0_ffn_up_W, L0_ffn_up_qa, L0_ffn_up_qb, L0_ffn_up_scale, L0_ffn_down_W, L0_ffn_down_qa, L0_ffn_down_qb, L0_ffn_down_scale, L0_ffn_sh_gate_W, L0_ffn_sh_up_W, L0_ffn_sh_down_W)
    return x

_drawn_inputs = setup_inputs


def setup_inputs(seed=0):
    import zlib

    import numpy as np

    out = dict(_drawn_inputs(seed))
    spreads = {'L0_ffn_gate_scale': (0.10000000149011612, 0.6),
     'L0_ffn_up_scale': (0.10000000149011612, 0.6),
     'L0_ffn_down_scale': (0.10000000149011612, 0.6)}
    factors = {'L0_attn_Wq': 8.0,
     'L0_attn_bq': 8.0,
     'L0_attn_Wk': 8.0,
     'L0_attn_bk': 64.0,
     'L0_attn_Wv': 4.715,
     'L0_attn_bv': 8.0,
     'L0_attn_Wo': 4.091,
     'L0_attn_bo': 16.511,
     'L0_ffn_gate_weight': 8.0,
     'L0_ffn_mask_up_W': 8.0,
     'L0_ffn_gate_W': 8.0,
     'L0_ffn_gate_qa': 8.0,
     'L0_ffn_gate_qb': 8.0,
     'L0_ffn_up_W': 8.0,
     'L0_ffn_up_qa': 8.0,
     'L0_ffn_up_qb': 8.0,
     'L0_ffn_down_W': 8.0,
     'L0_ffn_down_qa': 8.0,
     'L0_ffn_down_qb': 8.0,
     'L0_ffn_sh_gate_W': 2.863,
     'L0_ffn_sh_up_W': 2.827,
     'L0_ffn_sh_down_W': 2.817}
    for name, (base, spread) in spreads.items():
        noise = np.random.default_rng([zlib.crc32(name.encode()), seed]).standard_normal(out[name].shape)
        drawn = base * np.exp(spread * noise) if base else spread * noise
        out[name] = jnp.asarray(drawn.astype(out[name].dtype))
    for name, factor in factors.items():
        out[name] = (out[name] * factor).astype(out[name].dtype)
    return out
```

```python
from contextlib import ExitStack

import numpy as np
import concourse.bass as bass
from concourse import mybir

F32 = mybir.dt.float32
F32R = mybir.dt.float32r
BF16 = mybir.dt.bfloat16
I32 = mybir.dt.int32
ALU = mybir.AluOpType
ACT = mybir.ActivationFunctionType
AX = mybir.AxisListType.X
ds = bass.ds

P = 128
C = 256
KC = C // P
B, TT = 8, 512
T = B * TT
BLK = TT // P
NBLK = T // P
H, D = 16, 16
HQ = 4
NQ = H // HQ
NQUAD = B * NQ
E, F, K, R, TOPK = 64, 8, 8, 8, 6
I = 176
IR = I - P
GW = 7
EPS = 1e-5
SCALE = float(D) ** -0.5
NEG = -3e38

WX = KC * 4 * P
WS = 3 * P
WD = 2 * 3 * P
WE = WX + WS + WD
WM = KC * P
WCAT = 4 * P
WALL = 2 * WE + WCAT
SW = E + F
SG = KC * 6 * P
SD = 3 * C
SO = KC * C
SALL = SG + SD + SO
PW = KC * GW * P

Q_PART = [0, 0, 0, 1, 1, 2]
K_PART = [0, 1, 2, 0, 1, 0]
KS = 6 * D
KM = KS + 3
P_OFF = [0, TT, 1024, 896]
P_W = 1280


def prepare(nc, a, g):
    with ExitStack() as ctx:
        sb = lambda n, s, d: ctx.enter_context(nc.sbuf_tensor(n, s, d))
        sem = lambda n: ctx.enter_context(nc.semaphore(n))
        pw = sb("pw_raw", [P, PW], F32)
        sw = sb("shared_raw", [P, SALL], F32)
        raw = [sb(f"expert_raw{s}", [P, WE + WM], F32) for s in range(2)]
        sh_hi, sh_lo = sb("shared_hi", [P, SALL], F32R), sb("shared_lo", [P, SALL], F32R)
        scl = [sb(f"expert_scale{s}", [P, WS + C], F32) for s in range(2)]
        done = sb("expert_done", [P, WALL], F32R)
        cat_hi = sb("cat_hi", [P, WCAT], F32R)
        cat_ps = [ctx.enter_context(nc.psum_tensor(f"cat_ps{s}", [P, WCAT], F32)) for s in range(2)]
        const_in, pw_in, sw_in = sem("const_in"), sem("pw_in"), sem("sw_in")
        raw_in = [sem(f"raw_in{s}") for s in range(2)]
        stored = sem("expert_stored")
        base_hi, base_lo, shared_kept = sem("base_hi"), sem("base_lo"), sem("shared_kept")
        scaled, part_hi, part_lo = sem("scaled"), sem("part_hi"), sem("part_lo")
        cat_mm, cat_rounded = sem("cat_mm"), sem("cat_rounded")
        with nc.Block() as block:
            @block.sync
            def _(sp):
                sp.dma_start(pw[:], a["pw"]).then_inc(pw_in, 16)
                sp.dma_start(sw[:], a["shared"]).then_inc(sw_in, 16)
                for n, (dst, src) in enumerate(g["consts"]):
                    sp.dma_start(dst, src).then_inc(const_in, 16)
                sp.dma_start(g["y"][:], a["x_t"].rearrange("(c p) t -> p c t", p=P)).then_inc(const_in, 16)
                sp.wait_ge(base_lo, 2)
                for half, v in enumerate((sh_hi, sh_lo)):
                    sp.dma_start(g["sh_scr"][:, half * SALL:(half + 1) * SALL], v[:].bitcast(F32)).then_inc(shared_kept, 16)
                sp.sem_inc(stored, 16)
                sp.sem_inc(part_lo, 2)
                with sp.Fori(0, F // 2) as i:
                    for s in range(2):
                        sp.wait_ge(part_lo, 2 * i + s + 1)
                        sp.dma_start(raw[s][:], a["experts"][ds(2 * i + s, 1)].rearrange("e p n -> (e p) n")).then_inc(raw_in[s], 16)
                        sp.dma_start(scl[s][:], a["scales"][ds(2 * i + s, 1)].to_broadcast([P, WS + C])).then_inc(raw_in[s], 16)
                        sp.wait_ge(part_lo, 2 * i + s + 3)
                        sp.dma_start(g["wall"][ds(2 * i + s, 1)].rearrange("e p n -> (e p) n"), done[:].bitcast(F32)).then_inc(stored, 16)
                sp.wait_ge(stored, 16 * F + 16)
                sp.wait_ge(shared_kept, 32)
                sp.wait_ge(const_in, 16 * len(g["consts"]) + 16)

            @block.scalar
            def _(act):
                act.wait_ge(pw_in, 16)
                nc.scalar.activation(g["pw_hi"][:], pw[:], ACT.Copy).then_inc(base_hi, 1)
                act.wait_ge(sw_in, 16)
                nc.scalar.activation(sh_hi[:], sw[:], ACT.Copy).then_inc(base_hi, 1)
                with act.Fori(0, F // 2) as i:
                    for s in range(2):
                        act.wait_ge(scaled, 2 * i + s + 1)
                        act.wait_ge(stored, 32 * i + 16 * s + 16)
                        nc.scalar.activation(done[:, 0:WE], raw[s][:, 0:WE], ACT.Copy).then_inc(part_hi, 1)
                        act.wait_ge(cat_mm, 2 * i + s + 1)
                        nc.scalar.activation(cat_hi[:], cat_ps[s][:], ACT.Copy).then_inc(cat_rounded, 1)

            @block.vector
            def _(dve):
                dve.wait_ge(base_hi, 1)
                nc.vector.tensor_tensor(g["pw_lo"][:], pw[:], g["pw_hi"][:].bitcast(F32), ALU.subtract).then_inc(base_lo, 1)
                dve.wait_ge(base_hi, 2)
                nc.vector.tensor_tensor(sh_lo[:], sw[:], sh_hi[:].bitcast(F32), ALU.subtract).then_inc(base_lo, 1)
                dve.wait_ge(const_in, 16 * len(g["consts"]) + 16)
                nc.vector.tensor_copy(g["ident_bf"][:], g["ident"][:]).then_inc(base_lo, 1)
                with dve.Fori(0, F // 2) as i:
                    for s in range(2):
                        dve.wait_ge(raw_in[s], 32 * i + 32)
                        v = raw[s][:, WX:WX + WS]
                        nc.vector.tensor_tensor(v, v, scl[s][:, 0:WS], ALU.mult)
                        v = raw[s][64:P, WX + WS + 3 * P + P:WE]
                        nc.vector.tensor_tensor(v, v, scl[s][64:P, WS:WS + C], ALU.mult).then_inc(scaled, 1)
                        dve.wait_ge(part_hi, 2 * i + s + 1)
                        nc.vector.tensor_tensor(done[:, WE:2 * WE], raw[s][:, 0:WE],
                                                done[:, 0:WE].bitcast(F32), ALU.subtract)
                        dve.wait_ge(cat_rounded, 2 * i + s + 1)
                        nc.vector.scalar_tensor_tensor(done[:, 2 * WE:WALL], cat_hi[:].bitcast(F32), g["cat_sign"][:, 0:1],
                                                       cat_ps[s][:], ALU.mult, ALU.add).then_inc(part_lo, 1)

            @block.tensor
            def _(pe):
                with pe.Fori(0, F // 2) as i:
                    for s in range(2):
                        pe.wait_ge(raw_in[s], 32 * i + 32)
                        for c in range(KC):
                            last = nc.tensor.matmul(cat_ps[s][:], raw[s][:, WE + c * P:WE + (c + 1) * P],
                                                    raw[s][:, c * 4 * P:(c + 1) * 4 * P], start=(c == 0), stop=(c == KC - 1))
                        last.then_inc(cat_mm, 1)


def wait_first(eng, passed, sem, value):
    eng.wait_ge(sem, value)
    eng.sem_inc(passed, 1)


def three_passes(nc, out, w_hi, w_lo, x_hi, x_lo, start, stop):
    nc.tensor.matmul(out, w_hi, x_hi, start=start, stop=False)
    nc.tensor.matmul(out, w_hi, x_lo, start=False, stop=False)
    return nc.tensor.matmul(out, w_lo, x_hi, start=False, stop=stop)



def project(nc, a, g):
    with ExitStack() as ctx:
        sb = lambda n, s, d: ctx.enter_context(nc.sbuf_tensor(n, s, d))
        psum = lambda n, s, d: ctx.enter_context(nc.psum_tensor(n, s, d))
        sem = lambda n: ctx.enter_context(nc.semaphore(n))
        xin = [sb(f"xin{s}", [P, BLK, C], F32) for s in range(2)]
        stat = [sb(f"stat{s}", [P, BLK, 6], F32) for s in range(2)]
        mv = [sb(f"mv{s}", [P, BLK, 2], F32) for s in range(2)]
        std = [sb(f"std{s}", [P, BLK], F32) for s in range(2)]
        rstd = [sb(f"rstd{s}", [P, BLK], F32) for s in range(2)]
        xc_hi = [sb(f"xc_hi{s}", [P, KC, TT], F32R) for s in range(2)]
        xc_lo = [sb(f"xc_lo{s}", [P, KC, TT], F32R) for s in range(2)]
        lgt = sb("logits_t", [E, TT], F32)
        vf = [sb(f"v_f{c}", [P, TT], F32) for c in range(2)]
        vt = [sb(f"v_tok{s}", [P, BLK, H, 32], F32) for s in range(2)]
        qf = [sb(f"qk_f{j}", [P, TT], F32) for j in range(4)]
        rest = [sb(f"qk_rest{j}", [P, TT], F32) for j in range(4)]
        qs = [sb(f"qk_split{s}", [P, 4, 3, TT], BF16) for s in range(2)]
        tp = psum("x_turned_ps", [P, KC, TT], F32)
        gp = [psum(f"group_ps{j}", [P, TT], F32) for j in range(4)]
        lp = psum("logits_ps", [P, BLK, E], F32)
        vp = psum("v_ps", [P, BLK, P], F32)
        x_in = [sem(f"x_in{s}") for s in range(2)]
        x_kept = [sem(f"x_kept{s}") for s in range(2)]
        qkv_kept = [sem(f"qkv_kept{s}") for s in range(2)]
        stats, aggregated, eps_added, root, rooted, normed = map(sem, "stats aggregated eps_added root rooted normed".split())
        turned, x_rounded, x_rest = map(sem, "x_turned x_rounded x_rest".split())
        groups, evacuated = sem("groups_done"), sem("groups_evacuated")
        logits_turned, logits_kept, v_turned, v_kept = map(sem, "logits_turned logits_kept v_turned v_kept".split())
        rest1, part2, part3 = map(sem, "qk_rest1 qk_part2 qk_part3".split())
        passed = sem("passed")
        EV, EV_TILE = [1, 2, 3, 5, 7, 9, 11], 11
        with nc.Block() as block:
            @block.sync
            def _(sp):
                for s in range(2):
                    sp.sem_inc(x_kept[s], 32)
                    sp.sem_inc(qkv_kept[s], 80)
                sp.sem_inc(x_rest, 1)
                sp.sem_inc(evacuated, EV_TILE)
                sp.sem_inc(logits_turned, 1)
                sp.sem_inc(logits_kept, 1)
                sp.sem_inc(v_turned, 2)
                sp.sem_inc(v_kept, 1)
                sp.sem_inc(rest1, 4)
                sp.sem_inc(part3, 4)
                for s in range(2):
                    sp.dma_start(xin[s][:], a["x"][s].rearrange("(b p) c -> p b c", p=P)).then_inc(x_in[s], 16)

                def tile(t, s, more):
                    if more:
                        sp.wait_ge(turned, t + 1)
                        sp.dma_start(xin[s][:], a["x"][ds(t + 2, 1)].rearrange("o (b p) c -> p (o b) c", p=P)).then_inc(x_in[s], 16)
                    sp.wait_ge(x_rest, t + 2)
                    sp.dma_start(g["x_hi"][:, :, ds(t * TT, TT)].bitcast(F32), xc_hi[s][:].bitcast(F32)).then_inc(x_kept[s], 16)
                    sp.dma_start(g["x_lo"][:, :, ds(t * TT, TT)].bitcast(F32), xc_lo[s][:].bitcast(F32)).then_inc(x_kept[s], 16)
                    sp.wait_ge(v_kept, 2 * t + 3)
                    sp.dma_start(g["v_scr"][ds(t, 1)].rearrange("b p n -> (b p) n"), vt[s][:].rearrange("p b h d -> p (b h d)")).then_inc(qkv_kept[s], 16)
                    for j in range(4):
                        wait_first(sp, passed, part3, 4 * t + j + 5)
                        sp.dma_start(g["qk_scr"][j, :, :, ds(t * TT, TT)].rearrange("s p t -> p s t"), qs[s][:, j]).then_inc(qkv_kept[s], 16)

                with sp.Fori(0, B // 2 - 1) as i:
                    for s in range(2):
                        tile(2 * i + s, s, True)
                for s in range(2):
                    tile(B - 2 + s, s, False)
                for s in range(2):
                    sp.wait_ge(x_kept[s], 16 * B + 32)
                    sp.wait_ge(qkv_kept[s], 40 * B + 80)

            @block.vector
            def _(dve):
                for s in range(2):
                    nc.vector.memset(vt[s][:, :, :, D:D + 1], 1.0)
                    nc.vector.memset(vt[s][:, :, :, D + 1:32], 0.0)

                def norm(t, i, s):
                    dve.wait_ge(x_in[s], 16 * i + 16)
                    for b in range(BLK):
                        nc.vector.bn_stats(stat[s][:, b], xin[s][:, b]).then_inc(stats, 1)
                    for b in range(BLK):
                        wait_first(dve, passed, stats, BLK * t + b + 1)
                        nc.vector.bn_aggr(mv[s][:, b], stat[s][:, b]).then_inc(aggregated, 1)
                    dve.wait_ge(aggregated, BLK * t + BLK)
                    nc.vector.tensor_scalar_add(std[s][:], mv[s][:, :, 1], EPS).then_inc(eps_added, 1)
                    dve.wait_ge(root, t + 1)
                    nc.vector.reciprocal(rstd[s][:], std[s][:]).then_inc(rooted, 1)
                    dve.wait_ge(rooted, t + 1)
                    for b in range(BLK):
                        last = nc.vector.tensor_scalar(xin[s][:, b], xin[s][:, b], mv[s][:, b, 0:1], rstd[s][:, b:b + 1],
                                                       ALU.subtract, ALU.mult)
                    last.then_inc(normed, 1)

                def x_low(t, s):
                    dve.wait_ge(x_rounded, t + 1)
                    nc.vector.tensor_tensor(xc_lo[s][:], tp[:], xc_hi[s][:].bitcast(F32), ALU.subtract).then_inc(x_rest, 1)

                def split(t, s, j):
                    dve.wait_ge(evacuated, EV_TILE * t + EV_TILE + EV[3 + j])
                    dve.wait_ge(part3, 4 * t + j + 1)
                    nc.vector.tensor_tensor(rest[j][:], qf[j][:], qs[s][:, j, 0], ALU.subtract).then_inc(rest1, 1)
                    dve.wait_ge(rest1, 4 * t + j + 5)
                    nc.vector.tensor_copy(qs[s][:, j, 1], rest[j][:]).then_inc(part2, 1)

                def tile(t, i, s, more):
                    if more:
                        norm(t + 1, i + s, 1 - s)
                    dve.wait_ge(logits_turned, t + 2)
                    nc.vector.tensor_copy(g["logits"][:, ds(t * BLK, BLK), :], lp[:]).then_inc(logits_kept, 1)
                    dve.wait_ge(qkv_kept[s], 80 * i + 80)
                    for c in range(2):
                        dve.wait_ge(v_turned, 2 * t + c + 3)
                        nc.vector.tensor_copy(vt[s][:, :, 8 * c:8 * c + 8, 0:D],
                                              vp[:].rearrange("p b (h d) -> p b h d", d=D)).then_inc(v_kept, 1)
                    split(t, s, 0)
                    split(t, s, 1)
                    if more:
                        x_low(t + 1, 1 - s)
                    split(t, s, 2)
                    split(t, s, 3)

                norm(0, 0, 0)
                x_low(0, 0)
                with dve.Fori(0, B // 2 - 1) as i:
                    for s in range(2):
                        tile(2 * i + s, i, s, True)
                for s in range(2):
                    tile(B - 2 + s, B // 2 - 1, s, s == 0)

            @block.gpsimd
            def _(pool):
                with pool.Fori(0, B // 2) as i:
                    for s in range(2):
                        for j in range(4):
                            pool.wait_ge(part2, 8 * i + 4 * s + j + 1)
                            nc.gpsimd.tensor_tensor(qs[s][:, j, 2], rest[j][:], qs[s][:, j, 1], ALU.subtract).then_inc(part3, 1)

            @block.scalar
            def _(act):
                def x_high(t, i, s):
                    act.wait_ge(turned, t + 1)
                    act.wait_ge(x_kept[s], 32 * i + 32)
                    nc.scalar.activation(xc_hi[s][:], tp[:], ACT.Copy).then_inc(x_rounded, 1)

                def take_root(t, s):
                    act.wait_ge(eps_added, t + 1)
                    nc.scalar.activation(std[s][:], std[s][:], ACT.Sqrt).then_inc(root, 1)

                def evacuate(t, i, s, n):
                    act.wait_ge(groups, GW * t + n + 1)
                    bank = gp[n % 4]
                    if n == 0:
                        act.wait_ge(logits_turned, t + 1)
                        nc.scalar.activation(lgt[:], bank[0:E], ACT.Copy).then_inc(evacuated, 1)
                    elif n <= 2:
                        act.wait_ge(v_turned, 2 * t + n)
                        nc.scalar.activation(vf[n - 1][:], bank[:], ACT.Identity, bias=g["bias"][:, n:n + 1]).then_inc(evacuated, 1)
                    else:
                        j = n - 3
                        act.wait_ge(rest1, 4 * t + j + 1)
                        act.wait_ge(qkv_kept[s], 80 * i + 80)
                        nc.scalar.activation(qf[j][:], bank[:], ACT.Identity, bias=g["bias"][:, n:n + 1]).then_inc(evacuated, 1)
                        nc.scalar.activation(qs[s][:, j, 0], bank[:], ACT.Identity, bias=g["bias"][:, n:n + 1]).then_inc(evacuated, 1)

                def tile(t, i, s, more):
                    if more:
                        take_root(t + 1, 1 - s)
                    for n in range(5):
                        evacuate(t, i, s, n)
                    if more:
                        x_high(t + 1, i + s, 1 - s)
                    for n in range(5, GW):
                        evacuate(t, i, s, n)

                take_root(0, 0)
                x_high(0, 0, 0)
                with act.Fori(0, B // 2 - 1) as i:
                    for s in range(2):
                        tile(2 * i + s, i, s, True)
                for s in range(2):
                    tile(B - 2 + s, B // 2 - 1, s, s == 0)

            @block.tensor
            def _(pe):
                def turn_x(t, s):
                    pe.wait_ge(normed, t + 1)
                    pe.wait_ge(x_rest, t + 1)
                    for c in range(KC):
                        for b in range(BLK):
                            last = nc.tensor.transpose(tp[:, c, b * P:(b + 1) * P], xin[s][:, b, c * P:(c + 1) * P], g["ident"][:])
                    last.then_inc(turned, 1)

                def group(t, s, n):
                    before = EV[n - 4] + EV_TILE if n >= 4 else EV[n + 4] if n < 3 else EV[3]
                    pe.wait_ge(evacuated, EV_TILE * t + before)
                    for c in range(KC):
                        w = slice((c * GW + n) * P, (c * GW + n + 1) * P)
                        last = three_passes(nc, gp[n % 4][:], g["pw_hi"][:, w], g["pw_lo"][:, w],
                                            xc_hi[s][:, c], xc_lo[s][:, c], c == 0, c == KC - 1)
                    last.then_inc(groups, 1)

                def turn_v(t, c):
                    pe.wait_ge(evacuated, EV_TILE * t + EV_TILE + EV[1 + c])
                    pe.wait_ge(v_kept, 2 * t + c + 1)
                    for b in range(BLK):
                        last = nc.tensor.transpose(vp[:, b], vf[c][:, b * P:(b + 1) * P], g["ident"][:])
                    last.then_inc(v_turned, 1)

                def tile(t, s, more):
                    pe.wait_ge(x_rest, t + 2)
                    for n in range(3):
                        group(t, s, n)
                    pe.wait_ge(evacuated, EV_TILE * t + EV_TILE + EV[0])
                    wait_first(pe, passed, logits_kept, t + 1)
                    for b in range(BLK):
                        last = nc.tensor.transpose(lp[:, b], lgt[:, b * P:(b + 1) * P], g["ident"][0:E, 0:E])
                    last.then_inc(logits_turned, 1)
                    group(t, s, 3)
                    turn_v(t, 0)
                    group(t, s, 4)
                    turn_v(t, 1)
                    if more:
                        turn_x(t + 1, 1 - s)
                    group(t, s, 5)
                    group(t, s, 6)

                turn_x(0, 0)
                with pe.Fori(0, B // 2 - 1) as i:
                    for s in range(2):
                        tile(2 * i + s, s, True)
                for s in range(2):
                    tile(B - 2 + s, s, s == 0)


def route(nc, a, g):
    with ExitStack() as ctx:
        sb = lambda n, s, d: ctx.enter_context(nc.sbuf_tensor(n, s, d))
        psum = lambda n, s, d: ctx.enter_context(nc.psum_tensor(n, s, d))
        sem = lambda n: ctx.enter_context(nc.semaphore(n))
        CAND = E + 8
        work = sb("route_work", [P, NBLK, E], F32)
        scores = sb("scores", [P, NBLK, CAND], F32)
        marked = sb("marked", [P, NBLK, CAND], F32)
        top = sb("top", [P, NBLK, 8], F32)
        row = sb("row", [P, NBLK], F32)
        dense_t = sb("dense_t", [E, NBLK, P], F32)
        flat = sb("flat", [P, NBLK, E], F32)
        f8 = sb("per_expert", [P, NBLK * F], F32)
        soft = sb("soft", [P, NBLK, SW], F32)
        inv_i = sb("inv_i", [E, E], I32)
        pick = sb("pick", [E, E], F32)
        sw_t = sb("soft_t", [SW, 2, TT], F32)
        sw_hi = sb("soft_hi", [E, 2, TT], F32R)
        sw_lo = sb("soft_lo", [E, 2, TT], F32R)
        turn_ps = [psum(f"route_turn{j}", [SW, BLK, P], F32) for j in range(2)]
        flat_ps = [psum(f"flat_ps{j}", [P, 8, E], F32) for j in range(4)]
        inv_in = sem("inv_in")
        kept = [sem(f"soft_kept{s}") for s in range(2)]
        chain = sem("route_step")
        act_step, dense_ready, soft_ready = sem("route_act"), sem("dense_ready"), sem("soft_ready")
        dense_turned, dense_copied, picked, soft_turned, soft_copied = map(
            sem, "dense_turned dense_copied picked soft_turned soft_copied".split())
        split_hi, split_lo = sem("soft_split_hi"), sem("soft_split_lo")
        steps = []
        with nc.Block() as block:
            @block.vector
            def _(dve):
                def step(ins):
                    steps.append(1)
                    ins.then_inc(chain, 1)
                    dve.wait_ge(chain, len(steps))

                bc = lambda v, m: v.unsqueeze(2).broadcast_to([P, v.shape[1], m])
                logits = g["logits"]
                step(nc.vector.tensor_reduce(row[:], logits[:], AX, ALU.max))
                step(nc.vector.tensor_tensor(work[:], logits[:], bc(row[:], E), ALU.subtract))
                step(nc.vector.memset(scores[:, :, E:CAND], -1.0))
                dve.wait_ge(act_step, 1)
                step(nc.vector.tensor_reduce(row[:], work[:], AX, ALU.add))
                step(nc.vector.reciprocal(row[:], row[:]))
                step(nc.vector.tensor_tensor(scores[:, :, 0:E], work[:], bc(row[:], E), ALU.mult))
                for b in range(NBLK):
                    last = nc.vector.max(top[:, b], scores[:, b, 0:E])
                step(last)
                step(nc.vector.memset(top[:, :, TOPK:8], -1.0))
                for b in range(NBLK):
                    last = nc.vector.match_replace(marked[:, b], top[:, b], scores[:, b], -2.0)
                step(last)
                step(nc.vector.scalar_tensor_tensor(work[:], marked[:, :, 0:E], -2.0, scores[:, :, 0:E], ALU.is_equal, ALU.mult))
                dve.wait_ge(inv_in, 16)
                step(nc.vector.tensor_copy(pick[:], inv_i[:]))
                nc.vector.tensor_scalar(pick[:], pick[:], g["entry"][0:E, 0:1], None, ALU.is_equal).then_inc(dense_ready, 1)
                for j in range(4):
                    dve.wait_ge(picked, j + 1)
                    last = nc.vector.tensor_copy(flat[:, 8 * j:8 * j + 8], flat_ps[j][:])
                step(last)
                v = flat[:].rearrange("p b (f k) -> p (b f) k", k=K)
                w = work[:].rearrange("p b (f k) -> p (b f) k", k=K)
                scalars = soft[:, :, E:SW]
                step(nc.vector.tensor_reduce(scalars, flat[:].rearrange("p b (f k) -> p b f k", k=K), AX, ALU.add))
                step(nc.vector.tensor_scalar(work[:], flat[:], 0.0, -1e9, ALU.is_equal, ALU.mult))
                step(nc.vector.tensor_tensor(work[:], work[:], flat[:], ALU.add))
                step(nc.vector.tensor_reduce(f8[:], w, AX, ALU.max))
                step(nc.vector.tensor_tensor(w, w, bc(f8[:], K), ALU.subtract))
                dve.wait_ge(act_step, 2)
                step(nc.vector.tensor_reduce(f8[:], w, AX, ALU.add))
                step(nc.vector.reciprocal(f8[:], f8[:]))
                nc.vector.tensor_tensor(soft[:, :, 0:E].rearrange("p b (f k) -> p b f k", k=K),
                                        work[:].rearrange("p b (f k) -> p b f k", k=K),
                                        f8[:].rearrange("p (b f) -> p b f", f=F).unsqueeze(3).broadcast_to([P, NBLK, F, K]),
                                        ALU.mult).then_inc(soft_ready, 1)
                for t in range(B):
                    dve.wait_ge(split_hi, t + 1)
                    nc.vector.tensor_tensor(sw_lo[:, t % 2], sw_t[0:E, t % 2], sw_hi[:, t % 2].bitcast(F32), ALU.subtract).then_inc(split_lo, 1)

            @block.scalar
            def _(act):
                act.wait_ge(chain, 2)
                nc.scalar.activation(work[:], work[:], ACT.Exp).then_inc(act_step, 1)
                for t in range(B):
                    act.wait_ge(dense_turned, t + 1)
                    nc.scalar.activation(dense_t[:, t * BLK:(t + 1) * BLK], turn_ps[t % 2][0:E], ACT.Copy).then_inc(dense_copied, 1)
                act.wait_ge(chain, 17)
                nc.scalar.activation(work[:], work[:], ACT.Exp).then_inc(act_step, 1)
                for t in range(B):
                    act.wait_ge(soft_turned, t + 1)
                    if t >= 2:
                        act.wait_ge(kept[t % 2], 64 * (t // 2))
                    nc.scalar.activation(sw_t[:, t % 2], turn_ps[t % 2][:].rearrange("p b t -> p (b t)"), ACT.Copy).then_inc(soft_copied, 1)
                    nc.scalar.activation(sw_hi[:, t % 2], turn_ps[t % 2][0:E].rearrange("p b t -> p (b t)"), ACT.Copy).then_inc(split_hi, 1)

            @block.tensor
            def _(pe):
                pe.wait_ge(dense_ready, 1)
                for t in range(B):
                    if t >= 2:
                        pe.wait_ge(dense_copied, t - 1)
                    for b in range(BLK):
                        last = nc.tensor.transpose(turn_ps[t % 2][0:E, b], work[:, t * BLK + b], g["ident"][:])
                    last.then_inc(dense_turned, 1)
                for j in range(4):
                    pe.wait_ge(dense_copied, 2 * j + 2)
                    for b in range(8):
                        last = nc.tensor.matmul(flat_ps[j][:, b], dense_t[:, 8 * j + b], pick[:], start=True, stop=True)
                    last.then_inc(picked, 1)
                pe.wait_ge(soft_ready, 1)
                for t in range(B):
                    if t >= 2:
                        pe.wait_ge(split_hi, t - 1)
                    for b in range(BLK):
                        last = nc.tensor.transpose(turn_ps[t % 2][:, b], soft[:, t * BLK + b], g["ident"][:])
                    last.then_inc(soft_turned, 1)

            @block.sync
            def _(sp):
                sp.dma_start(inv_i[:], a["inv"].to_broadcast([E, E])).then_inc(inv_in, 16)
                for t in range(B):
                    tok = slice(t * TT, (t + 1) * TT)
                    sp.wait_ge(soft_copied, t + 1)
                    sp.dma_start(g["sw_scr"][:, tok], sw_t[:, t % 2]).then_inc(kept[t % 2], 16)
                    sp.wait_ge(split_lo, t + 1)
                    for part, src in enumerate((sw_hi, sw_lo, sw_hi)):
                        sp.dma_start(g["cat_scr"][:, part * K:(part + 1) * K, tok], src[:, t % 2].bitcast(F32)).then_inc(kept[t % 2], 16)
                for s in range(2):
                    sp.wait_ge(kept[s], 32 * B)


def attend(nc, a, g):
    with ExitStack() as ctx:
        sb = lambda n, s, d: ctx.enter_context(nc.sbuf_tensor(n, s, d))
        psum = lambda n, s, d: ctx.enter_context(nc.psum_tensor(n, s, d))
        sem = lambda n: ctx.enter_context(nc.semaphore(n))
        q_st = [sb(f"q_stack{s}", [P, HQ, TT], BF16) for s in range(2)]
        k_st = [sb(f"k_stack{s}", [P, HQ, TT], BF16) for s in range(2)]
        v_st = [sb(f"v_stack{s}", [P, BLK, HQ * 32], F32) for s in range(2)]
        junk = [sb(f"junk{s}", [P, TT], F32) for s in range(2)]
        mx = sb("row_max", [P, HQ * BLK], F32)
        mrest = sb("row_max_rest", [P, HQ * BLK], F32)
        mparts = sb("row_max_parts", [P, 3, HQ * BLK], BF16)
        m_t = [sb(f"row_max_t{s}", [3 * HQ * BLK, P], BF16) for s in range(2)]
        prob = [sb(f"prob{s}", [P, HQ, P_W], F32) for s in range(2)]
        y_out = [sb(f"y_out{s}", [P, TT], F32) for s in range(2)]
        ma_ps = [psum(f"max_ps{j}", [P, TT], F32) for j in range(2)]
        s_ps = [psum(f"score_ps{j}", [P, 2, TT], F32) for j in range(2)]
        s2_ps = psum("score2_ps", [P, 2, 256], F32)
        y_ps = psum("y_ps", [P, TT], F32)
        qk_in = [sem(f"qk_in{s}") for s in range(2)]
        m_in = [sem(f"m_in{s}") for s in range(2)]
        y_kept = [sem(f"y_kept{s}") for s in range(2)]
        ones_set, passed = sem("ones_set"), sem("passed")
        row_scored, maxed, m_part, m_turned, m_copied = map(sem, "row_scored maxed m_part m_turned m_copied".split())
        scored, exped, masked, mixed, y_copied = map(sem, "scored exped masked mixed y_copied".split())
        NLOAD = 13 * 16
        with nc.Block() as block:
            def quads(eng, step):
                with eng.Fori(0, B - 1) as b:
                    for q in range(NQ):
                        step(NQ * b + q, b, q, True)
                for q in range(NQ):
                    step(NQ * (B - 1) + q, B - 1, q, q < NQ - 1)

            @block.sync
            def _(sp):
                sp.sem_inc(maxed, 2)
                sp.sem_inc(m_copied, 1)
                sp.sem_inc(exped, 3)
                sp.sem_inc(mixed, 2)
                sp.sem_inc(y_copied, 1)
                for s in range(2):
                    sp.sem_inc(y_kept[s], 16)
                sp.wait_ge(ones_set, 1)

                def load(n, b, q):
                    s = q % 2
                    sp.wait_ge(mixed, n + 1)
                    tok = ds(b * TT, TT)
                    rows = slice((q % 2) * HQ * D, (q % 2 + 1) * HQ * D)
                    for st, j, parts in ((q_st, q // 2, Q_PART), (k_st, 2 + q // 2, K_PART)):
                        for slot, part in enumerate(parts):
                            src = g["qk_scr"][j, part, rows, tok].rearrange("(h d) t -> d h t", d=D)
                            sp.dma_start(st[s][slot * D:(slot + 1) * D], src).then_inc(qk_in[s], 16)
                    sp.dma_start(v_st[s][:], g["v_scr"][ds(b, 1)].rearrange("o p (k n) -> p (o k) n", k=BLK)[:, :, q * HQ * 32:(q + 1) * HQ * 32]).then_inc(qk_in[s], 16)

                def max_rows(n, s):
                    sp.wait_ge(m_copied, n + 2)
                    sp.dma_start(q_st[s][KS:KM].rearrange("j h t -> j (h t)").rearrange("j (n t) -> j n t", t=P), m_t[s][:]).then_inc(m_in[s], 16)

                def step(n, b, q, more):
                    s = q % 2
                    if more:
                        max_rows(n + 1, 1 - s)
                    if more and q < NQ - 2:
                        load(n + 2, b, q + 2)
                    elif b is not B - 1 and q >= NQ - 2:
                        load(n + 2, b + 1, q - 2)
                    wait_first(sp, passed, y_copied, n + 2)
                    sp.dma_start(g["y_scr"][ds(b, 1), q].rearrange("o p t -> (o p) t"), y_out[s][:]).then_inc(y_kept[s], 16)

                load(0, 0, 0)
                load(1, 0, 1)
                max_rows(0, 0)
                quads(sp, step)
                for s in range(2):
                    sp.wait_ge(y_kept[s], 16 * (NQUAD // 2) + 16)

            @block.vector
            def _(dve):
                for s in range(2):
                    last = nc.vector.memset(k_st[s][KS:KM], 1.0)
                last.then_inc(ones_set, 1)

                def maxima(n):
                    for x in range(HQ * BLK):
                        w = (x % BLK + 1) * P
                        dve.wait_ge(row_scored, 16 * n + x + 1)
                        wait_first(dve, passed, maxed, 16 * n + x + 1)
                        nc.vector.tensor_tensor_reduce(out=junk[x % 2][:, 0:w], in0=ma_ps[x % 2][:, 0:w], in1=g["causal"][:, TT - w:TT],
                                                       scale=1.0, scalar=NEG, op0=ALU.add, op1=ALU.max,
                                                       accum_out=mx[:, x:x + 1]).then_inc(maxed, 1)

                def split_max(n, s):
                    dve.wait_ge(maxed, 16 * n + 18)
                    nc.vector.tensor_scalar(mparts[:, 0], mx[:], -1.0, None, ALU.mult).then_inc(m_part, 1)
                    dve.wait_ge(m_part, 4 * n + 1)
                    nc.vector.scalar_tensor_tensor(mrest[:], mx[:], -1.0, mparts[:, 0], ALU.mult, ALU.subtract).then_inc(m_part, 1)
                    dve.wait_ge(m_part, 4 * n + 2)
                    nc.vector.tensor_copy(mparts[:, 1], mrest[:]).then_inc(m_part, 1)
                    dve.wait_ge(m_part, 4 * n + 3)
                    nc.vector.tensor_tensor(mparts[:, 2], mrest[:], mparts[:, 1], ALU.subtract).then_inc(m_part, 1)
                    dve.wait_ge(m_turned, n + 1)
                    nc.vector.tensor_copy(m_t[s][:], ma_ps[0][0:3 * HQ * BLK, 0:P // 2].bitcast(BF16)).then_inc(m_copied, 1)

                def step(n, b, q, more):
                    s = q % 2
                    if more:
                        maxima(n + 1)
                    dve.wait_ge(mixed, n + 3)
                    dve.wait_ge(y_kept[s], 16 * (2 * b + q // 2) + 16)
                    nc.vector.tensor_copy(y_out[s][:], y_ps[:]).then_inc(y_copied, 1)
                    if more:
                        split_max(n + 1, 1 - s)

                maxima(0)
                split_max(0, 0)
                quads(dve, step)

            @block.scalar
            def _(act):
                def step(n, b, q, more):
                    s = q % 2
                    act.wait_ge(mixed, n + 1)
                    for pair in range(2):
                        for j in range(2):
                            act.wait_ge(scored, 6 * n + 3 * pair + j + 1)
                            nc.scalar.activation(prob[s][:, 2 * pair + j, 0:1024], s_ps[j][:].rearrange("p b t -> p (b t)"), ACT.Exp,
                                                 scale=SCALE).then_inc(exped, 1)
                        act.wait_ge(scored, 6 * n + 3 * pair + 3)
                        nc.scalar.activation(prob[s][:, 2 * pair:2 * pair + 2, 1024:P_W], s2_ps[:], ACT.Exp, scale=SCALE).then_inc(exped, 1)
                quads(act, step)

            @block.gpsimd
            def _(pool):
                def step(n, b, q, more):
                    s = q % 2
                    for pair in range(2):
                        v = prob[s][:, 2 * pair:2 * pair + 2]
                        wait_first(pool, passed, exped, 6 * n + 3 * pair + 6)
                        for i in range(BLK):
                            w = v[:, :, P_OFF[i]:P_OFF[i] + P]
                            nc.gpsimd.affine_select(out=w, in_=w, compare_op=ALU.is_ge, fill=0.0, base=0,
                                                    pattern=[[0, 2], [1, P]], channel_multiplier=-1).then_inc(masked, 1)
                quads(pool, step)

            @block.tensor
            def _(pe):
                def row_scores(n, b, q, h):
                    s = q % 2
                    if h == 0:
                        pe.wait_ge(qk_in[s], NLOAD * (2 * b + q // 2 + 1))
                        pe.wait_ge(m_copied, n + 1)
                    for x in range(h * BLK, (h + 1) * BLK):
                        blk = x % BLK
                        pe.wait_ge(maxed, 16 * n + x + 1)
                        nc.tensor.matmul(ma_ps[x % 2][:, 0:(blk + 1) * P], q_st[s][0:KS, h, blk * P:(blk + 1) * P],
                                         k_st[s][0:KS, h, 0:(blk + 1) * P], start=True, stop=True).then_inc(row_scored, 1)

                def turn_max(n):
                    wait_first(pe, passed, m_part, 4 * n + 4)
                    nc.tensor.transpose(ma_ps[0][0:3 * HQ * BLK, 0:P // 2].bitcast(BF16), mparts[:].rearrange("p j n -> p (j n)"),
                                        g["ident_bf"][:]).then_inc(m_turned, 1)

                def key_scores(n, b, q, h):
                    s, pair, j = q % 2, h // 2, h % 2
                    if h == 0:
                        pe.wait_ge(m_in[s], 16 * (2 * b + q // 2 + 1))
                    score = lambda out, i: nc.tensor.matmul(out, k_st[s][0:KM, h, i * P:(i + 1) * P], q_st[s][0:KM, h, i * P:TT],
                                                            start=True, stop=True)
                    pe.wait_ge(exped, 6 * n + 3 * pair + 1 + j)
                    score(s_ps[j][:, 0, :], 0)
                    score(s_ps[j][:, 1, 0:384], 1)
                    score(s_ps[j][:, 1, 384:512], 3).then_inc(scored, 1)
                    pe.wait_ge(exped, 6 * n + 3 * pair + 3)
                    last = score(s2_ps[:, j], 2)
                    if j == 1:
                        last.then_inc(scored, 1)

                def mix(n, q):
                    s = q % 2
                    pe.wait_ge(masked, 8 * n + 8)
                    pe.wait_ge(y_copied, n + 1)
                    for i in range(BLK):
                        for h in range(HQ):
                            last = nc.tensor.matmul(y_ps[32 * h:32 * h + 32, i * P:TT], v_st[s][:, i, 32 * h:32 * h + 32],
                                                    prob[s][:, h, P_OFF[i]:P_OFF[i] + TT - i * P], start=(i == 0), stop=(i == BLK - 1))
                    last.then_inc(mixed, 1)

                def step(n, b, q, more):
                    for h in range(HQ):
                        if more:
                            row_scores(n + 1, b + (q + 1) // NQ, (q + 1) % NQ, h)
                        key_scores(n, b, q, h)
                    mix(n, q)
                    if more:
                        turn_max(n + 1)

                for h in range(HQ):
                    row_scores(0, 0, 0, h)
                turn_max(0)
                quads(pe, step)


def share(nc, a, g):
    with ExitStack() as ctx:
        sb = lambda n, s, d: ctx.enter_context(nc.sbuf_tensor(n, s, d))
        psum = lambda n, s, d: ctx.enter_context(nc.psum_tensor(n, s, d))
        sem = lambda n: ctx.enter_context(nc.semaphore(n))
        sh_hi, sh_lo = sb("sh_hi", [P, SALL], F32R), sb("sh_lo", [P, SALL], F32R)
        sh_in = sem("sh_in")
        yp = [sb(f"y_packed{s}", [P, KC, TT], F32) for s in range(2)]
        den = [sb(f"sums{s}", [P, H * TT // P], F32) for s in range(2)]
        rden = [sb(f"sums_rep{s}", [P, KC, TT], F32) for s in range(2)]
        yn_hi = [sb(f"yn_hi{s}", [P, KC, TT], F32R) for s in range(2)]
        yn_lo = [sb(f"yn_lo{s}", [P, KC, TT], F32R) for s in range(2)]
        sg = [sb(f"silu{s}", [P, TT], F32) for s in range(2)]
        h_hi = [sb(f"h_hi{s}", [P, TT], F32R) for s in range(3)]
        h_lo = [sb(f"h_lo{s}", [P, TT], F32R) for s in range(3)]
        gu = [[psum(f"gu{j}{s}", [P, TT], F32) for s in range(2)] for j in range(2)]
        out_ps = psum("out_ps", [P, KC, TT], F32)
        y_in = [sem(f"y_in{s}") for s in range(2)]
        r_in = [sem(f"r_in{s}") for s in range(2)]
        r_kept = sem("r_kept")
        inverted, normed, yn_rounded, yn_ready = map(sem, "sums_inverted y_normed yn_rounded yn_ready".split())
        gate_up, gated, product, h_rounded, h_ready, summed, added = map(
            sem, "sh_gate_up sh_gated sh_product sh_rounded sh_ready sh_summed sh_added".split())
        W1 = lambda c, m: slice((c * 6 + m) * P, (c * 6 + m + 1) * P)
        W2 = lambda i, m: slice(SG + i * C + m * P, SG + i * C + (m + 1) * P)
        WO = lambda c, m: slice(SG + SD + c * C + m * P, SG + SD + c * C + (m + 1) * P)
        with nc.Block() as block:
            def tiles(eng, tile):
                with eng.Fori(0, B // 2) as i:
                    for s in range(2):
                        tile(2 * i + s, i, s)

            @block.sync
            def _(sp):
                for half, v in enumerate((sh_hi, sh_lo)):
                    sp.dma_start(v[:].bitcast(F32), g["sh_scr"][:, half * SALL:(half + 1) * SALL]).then_inc(sh_in, 16)
                sp.sem_inc(yn_ready, 2)
                sp.sem_inc(summed, 1)
                sp.sem_inc(gated, 2)
                sp.sem_inc(product, 2)
                sp.sem_inc(added, 1)

                def tile(t, i, s):
                    sp.wait_ge(yn_ready, t + 1)
                    for c in range(KC):
                        sp.dma_start(yp[s][:, c], g["y_heads"][ds(t, 1), c * 8:c * 8 + 8, 0:D].rearrange("o h d t -> (o h) d t")).then_inc(y_in[s], 16)
                    sp.dma_start(den[s][:], g["y_heads"][ds(t, 1), :, D].rearrange("o h (k n) -> (o h) k n", n=H * TT // P)).then_inc(y_in[s], 16)
                    sp.wait_ge(inverted, t + 1)
                    sp.dma_start(g["r_scr"][ds(t, 1)].rearrange("o h (k n) -> (o h k) n", n=H * TT // P), den[s][:]).then_inc(r_kept, 16)
                    sp.wait_ge(r_kept, 16 * t + 16)
                    for c in range(KC):
                        sp.dma_start(rden[s][:, c], g["r_scr"][ds(t, 1), c * 8:c * 8 + 8].rearrange("o h t -> (o h) t").unsqueeze(1)
                                     .broadcast_to([8, D, TT])).then_inc(r_in[s], 16)
                tiles(sp, tile)

            @block.vector
            def _(dve):
                def invert(t, i, s):
                    dve.wait_ge(y_in[s], 48 * i + 48)
                    nc.vector.reciprocal(den[s][:], den[s][:]).then_inc(inverted, 1)

                def tile(t, i, s):
                    invert(t, i, s)
                    for j in range(3):
                        if j == 1:
                            dve.wait_ge(r_in[s], 32 * i + 32)
                            nc.vector.tensor_tensor(yp[s][:], yp[s][:], rden[s][:], ALU.mult).then_inc(normed, 1)
                        if j == 2:
                            dve.wait_ge(yn_rounded, t + 1)
                            nc.vector.tensor_tensor(yn_lo[s][:], yp[s][:], yn_hi[s][:].bitcast(F32), ALU.subtract).then_inc(yn_ready, 1)
                        n = 3 * t + j
                        dve.wait_ge(gated, n + 3)
                        slot = (3 * s + j) % 2
                        nc.vector.tensor_tensor(sg[slot][:], sg[slot][:], gu[slot][1][:], ALU.mult).then_inc(product, 1)
                        dve.wait_ge(h_rounded, n + 1)
                        nc.vector.tensor_tensor(h_lo[j][:], sg[slot][:], h_hi[j][:].bitcast(F32), ALU.subtract).then_inc(h_ready, 1)
                    dve.wait_ge(summed, t + 2)
                    for c in range(KC):
                        v = g["y"][:, c, ds(t * TT, TT)]
                        last = nc.vector.scalar_tensor_tensor(v, out_ps[:, c], g["bias"][:, GW + c:GW + c + 1], v, ALU.add, ALU.add)
                    last.then_inc(added, 1)
                tiles(dve, tile)

            @block.scalar
            def _(act):
                def tile(t, i, s):
                    for j in range(3):
                        n = 3 * t + j
                        slot = (3 * s + j) % 2
                        act.wait_ge(gate_up, n + 1)
                        act.wait_ge(h_ready, n - 1) if False else None
                        act.wait_ge(product, n + 1)
                        nc.scalar.activation(sg[slot][:], gu[slot][0][:], ACT.Silu).then_inc(gated, 1)
                        if j == 1:
                            act.wait_ge(normed, t + 1)
                            nc.scalar.activation(yn_hi[s][:], yp[s][:], ACT.Copy).then_inc(yn_rounded, 1)
                        act.wait_ge(product, n + 3)
                        if j == 0:
                            act.wait_ge(summed, t + 1)
                        nc.scalar.activation(h_hi[j][:], sg[slot][:], ACT.Copy).then_inc(h_rounded, 1)
                tiles(act, tile)

            @block.tensor
            def _(pe):
                def gates(t, s, j):
                    n = 3 * t + j
                    slot = (3 * s + j) % 2
                    pe.wait_ge(product, n + 1)
                    for r in range(2):
                        for c in range(KC):
                            w = W1(c, 2 * j + r)
                            tok = ds(t * TT, TT)
                            last = three_passes(nc, gu[slot][r][:], sh_hi[:, w], sh_lo[:, w],
                                                g["x_hi"][:, c, tok], g["x_lo"][:, c, tok], c == 0, c == KC - 1)
                    last.then_inc(gate_up, 1)

                def down(t, j):
                    pe.wait_ge(h_ready, 3 * t + j + 1)
                    if j == 0:
                        pe.wait_ge(added, t + 1)
                    for m in range(KC):
                        last = three_passes(nc, out_ps[:, m], sh_hi[:, W2(j, m)], sh_lo[:, W2(j, m)],
                                            h_hi[j][:], h_lo[j][:], j == 0, j == 2)
                    if j == 2:
                        last.then_inc(summed, 1)

                def project_out(t, s):
                    pe.wait_ge(yn_ready, t + 3)
                    for m in range(KC):
                        for c in range(KC):
                            three_passes(nc, out_ps[:, m], sh_hi[:, WO(c, m)], sh_lo[:, WO(c, m)],
                                         yn_hi[s][:, c], yn_lo[s][:, c], False, False)

                def tile(t, i, s):
                    gates(t, s, 0)
                    gates(t, s, 1)
                    down(t, 0)
                    gates(t, s, 2)
                    down(t, 1)
                    project_out(t, s)
                    down(t, 2)
                pe.wait_ge(sh_in, 32)
                tiles(pe, tile)


def walk(eng, tile):
    def expert(e, ws, first=False, last=False):
        tile(e, 0, 0, 0, ws, first=first, last=False)
        with eng.Fori(0, B // 2 - 1) as j:
            for r in (1, 2):
                tile(e, 2 * j + r, j + r - 1, r % 2, ws, first=False, last=False)
        tile(e, B - 1, B // 2 - 1, 1, ws, first=False, last=last)

    expert(0, 0, first=True)
    with eng.Fori(0, F // 2 - 1) as i:
        expert(2 * i + 1, 1)
        expert(2 * i + 2, 0)
    expert(F - 1, 1, last=True)


def experts(nc, a, g):
    with ExitStack() as ctx:
        sb = lambda n, s, d: ctx.enter_context(nc.sbuf_tensor(n, s, d))
        psum = lambda n, s, d: ctx.enter_context(nc.psum_tensor(n, s, d))
        sem = lambda n: ctx.enter_context(nc.semaphore(n))
        w = [sb(f"expert_w{s}", [P, WALL], F32R) for s in range(2)]
        wrep = [sb(f"soft_rep{s}", [P, TT], F32) for s in range(2)]
        srep = [sb(f"scalar_rep{s}", [P, TT], F32) for s in range(2)]
        cat = [sb(f"soft_stack{s}", [P, TT], F32R) for s in range(2)]
        low, low_hi, low_lo = sb("low", [P, TT], F32), sb("low_hi", [P, TT], F32R), sb("low_lo", [P, TT], F32R)
        low2 = sb("low2", [P, TT], F32)
        sg = [sb(f"gate{c}", [P, TT], F32) for c in range(2)]
        h = [sb(f"h{c}", [P, TT], F32) for c in range(2)]
        h_hi = [[sb(f"eh_hi{c}{s}", [P, TT], F32R) for s in range(2)] for c in range(2)]
        h_lo = [[sb(f"eh_lo{c}{s}", [P, TT], F32R) for s in range(2)] for c in range(2)]
        low_ps = psum("low_ps", [P, TT], F32)
        gu_ps = [psum(f"expert_gu{m}", [P, TT], F32) for m in range(3)]
        out_ps = psum("expert_out", [P, TT], F32)
        w_in = [sem(f"expert_w_in{s}") for s in range(2)]
        tile_in = [sem(f"tile_in{s}") for s in range(2)]
        zeroed, y_stored = sem("zeroed"), sem("y_stored")
        low_done, weighted, low_rounded, low_ready = map(sem, "low_done weighted low_rounded low_ready".split())
        gu_done, gated, product, scaled, h_rounded, h_ready = map(
            sem, "gu_done gated product scaled h_rounded h_ready".split())
        low2_done, weighted2, low2_rounded, low2_ready = map(sem, "low2_done weighted2 low2_rounded low2_ready".split())
        out_done, added = sem("expert_out_done"), sem("expert_added")
        WLO = WE
        WXS = lambda c, m: slice((c * 4 + m) * P, (c * 4 + m + 1) * P)
        WSS = lambda m: slice(WX + m * P, WX + (m + 1) * P)
        WDS = lambda c, m: slice(WX + WS + (c * 3 + m) * P, WX + WS + (c * 3 + m + 1) * P)
        CATS = lambda m: slice(2 * WE + m * P, 2 * WE + (m + 1) * P)
        lo = lambda sl: slice(sl.start + WLO, sl.stop + WLO)
        IRP = 64

        with nc.Block() as block:
            @block.sync
            def _(sp):
                sp.sem_inc(weighted2, 2)
                sp.sem_inc(gated, 2)
                sp.sem_inc(product, 2)
                sp.sem_inc(h_ready, 2)
                sp.sem_inc(out_done, 4)
                sp.sem_inc(added, 2)
                sp.wait_ge(zeroed, 1)

                def tile(e, t, i, s, ws, first, last):
                    n = 8 * e + t
                    tok = ds(t * TT, TT)
                    sp.wait_ge(weighted2, n + 1)
                    for half in range(2):
                        sp.dma_start(wrep[s][half * 64:half * 64 + 64], g["sw_scr"][ds(e * K, K), tok].unsqueeze(1).broadcast_to([K, R, TT])).then_inc(tile_in[s], 16)
                    sp.dma_start(srep[s][:], g["sw_scr"][ds(e + E, 1), tok].to_broadcast([P, TT])).then_inc(tile_in[s], 16)
                    sp.dma_start(cat[s][0:3 * K].bitcast(F32), g["cat_scr"][ds(e, 1), :, tok].rearrange("o k t -> (o k) t")).then_inc(tile_in[s], 16)
                walk(sp, tile)
                for t in range(B):
                    sp.wait_ge(added, 2 * (8 * F - 8 + t) + 4)
                    sp.dma_start(g["out"].rearrange("(c p) t -> p c t", p=P)[:, :, t * TT:(t + 1) * TT], g["y"][:, :, t * TT:(t + 1) * TT]).then_inc(y_stored, 16)
                sp.wait_ge(y_stored, 16 * B)

            @block.vector
            def _(dve):
                for s in range(2):
                    nc.vector.memset(cat[s][:].bitcast(F32), 0.0)
                    nc.vector.memset(h_hi[1][s][:].bitcast(F32), 0.0)
                    last = nc.vector.memset(h_lo[1][s][:].bitcast(F32), 0.0)
                last.then_inc(zeroed, 1)

                def weight(n, i, s):
                    dve.wait_ge(low_done, n + 1)
                    dve.wait_ge(tile_in[s], 64 * i + 64)
                    nc.vector.tensor_tensor(low[:], low_ps[:], wrep[s][:], ALU.mult).then_inc(weighted, 1)

                def weight2(n, s):
                    dve.wait_ge(low2_done, n + 1)
                    nc.vector.tensor_tensor(low2[IRP:P], low_ps[IRP:P], wrep[s][IRP:P], ALU.mult).then_inc(weighted2, 1)
                    dve.wait_ge(low2_rounded, n + 1)
                    nc.vector.tensor_tensor(h_lo[1][s][IRP:P], low2[IRP:P], h_hi[1][s][IRP:P].bitcast(F32), ALU.subtract).then_inc(low2_ready, 1)

                def add(n, t, c):
                    dve.wait_ge(out_done, 2 * n + c + 5)
                    v = g["y"][:, c, ds(t * TT, TT)]
                    nc.vector.tensor_tensor(v, out_ps[:], v, ALU.add).then_inc(added, 1)

                def tile(e, t, i, s, ws, first, last):
                    n = 8 * e + t
                    tp = t - 1 if t is not 0 else B - 1
                    if first:
                        weight(n, 0, s)
                    dve.wait_ge(low_rounded, n + 1)
                    nc.vector.tensor_tensor(low_lo[:], low[:], low_hi[:].bitcast(F32), ALU.subtract).then_inc(low_ready, 1)
                    if not first:
                        weight2(n - 1, 1 - s)
                    dve.wait_ge(h_ready, 2 * n + 2)
                    dve.wait_ge(gated, 2 * n + 3)
                    dve.wait_ge(gu_done, 3 * n + 2)
                    nc.vector.tensor_tensor(h[0][:], sg[0][:], gu_ps[1][:], ALU.mult).then_inc(product, 1)
                    dve.wait_ge(gated, 2 * n + 4)
                    nc.vector.tensor_tensor(h[1][0:IR], sg[1][64:64 + IR], gu_ps[2][64:64 + IR], ALU.mult).then_inc(product, 1)
                    if not first:
                        add(n - 1, tp, 0)
                    if not last:
                        weight(n + 1, 4 * e + i + (1 if s else 0), 1 - s)
                    if not first:
                        add(n - 1, tp, 1)
                walk(dve, tile)
                weight2(8 * F - 1, 1)
                add(8 * F - 1, B - 1, 0)
                add(8 * F - 1, B - 1, 1)

            @block.scalar
            def _(act):
                def round_h(n, s):
                    act.wait_ge(out_done, 2 * n + 2)
                    for c, rows in ((0, slice(0, P)), (1, slice(0, IR))):
                        act.wait_ge(scaled, 2 * n + c + 1)
                        nc.scalar.activation(h_hi[c][s][rows], h[c][rows], ACT.Copy).then_inc(h_rounded, 1)

                def round_low2(n, s):
                    act.wait_ge(weighted2, n + 3)
                    nc.scalar.activation(h_hi[1][s][IRP:P], low2[IRP:P], ACT.Copy).then_inc(low2_rounded, 1)

                def tile(e, t, i, s, ws, first, last):
                    n = 8 * e + t
                    act.wait_ge(weighted, n + 1)
                    nc.scalar.activation(low_hi[:], low[:], ACT.Copy).then_inc(low_rounded, 1)
                    if not first:
                        round_h(n - 1, 1 - s)
                        round_low2(n - 1, 1 - s)
                    act.wait_ge(gu_done, 3 * n + 1)
                    nc.scalar.activation(sg[0][:], gu_ps[0][:], ACT.Silu).then_inc(gated, 1)
                    act.wait_ge(gu_done, 3 * n + 3)
                    nc.scalar.activation(sg[1][64:64 + IR], gu_ps[2][0:IR], ACT.Silu).then_inc(gated, 1)
                walk(act, tile)
                round_h(8 * F - 1, 1)
                round_low2(8 * F - 1, 1)

            @block.gpsimd
            def _(pool):
                def rest_h(n, s):
                    for c, rows in ((0, slice(0, P)), (1, slice(0, IR))):
                        pool.wait_ge(h_rounded, 2 * n + c + 1)
                        nc.gpsimd.tensor_tensor(h_lo[c][s][rows], h[c][rows], h_hi[c][s][rows].bitcast(F32), ALU.subtract).then_inc(h_ready, 1)

                def tile(e, t, i, s, ws, first, last):
                    n = 8 * e + t
                    if not first:
                        rest_h(n - 1, 1 - s)
                    for c, rows in ((0, slice(0, P)), (1, slice(0, IR))):
                        pool.wait_ge(product, 2 * n + c + 3)
                        nc.gpsimd.tensor_tensor(h[c][rows], h[c][rows], srep[s][rows], ALU.mult).then_inc(scaled, 1)
                    if t is 0 and e is not F - 1:
                        pool.wait_ge(out_done, 2 * n + 4)
                        pool.dma_start(w[1 - ws][:].bitcast(F32), g["wall"][ds(e + 1, 1)].rearrange("o p n -> (o p) n")).then_inc(w_in[1 - ws], 16)
                pool.dma_start(w[0][:].bitcast(F32), g["wall"][0]).then_inc(w_in[0], 16)
                walk(pool, tile)
                rest_h(8 * F - 1, 1)

            @block.tensor
            def _(pe):
                def from_x(out, m, t, s, ws, stop):
                    tok = ds(t * TT, TT)
                    for c in range(KC):
                        three_passes(nc, out, w[ws][:, WXS(c, m)], w[ws][:, lo(WXS(c, m))], g["x_hi"][:, c, tok], g["x_lo"][:, c, tok], c == 0, False)
                    return nc.tensor.matmul(out, w[ws][:, CATS(m)], cat[s][:], start=False, stop=stop)

                def low_rank(n, t, i, s, ws, freed):
                    pe.wait_ge(tile_in[s], 64 * i + 64)
                    pe.wait_ge(weighted2, freed)
                    from_x(low_ps[:], 0, t, s, ws, True).then_inc(low_done, 1)

                def low_rank2(n, s, ws):
                    pe.wait_ge(h_ready, 2 * n + 4)
                    pe.wait_ge(weighted, n + 2 if n is not 8 * F - 1 else n + 1)
                    for c in range(2):
                        last = three_passes(nc, low_ps[:], w[ws][:, WDS(c, 0)], w[ws][:, lo(WDS(c, 0))], h_hi[c][s][:], h_lo[c][s][:], c == 0, c == 1)
                    last.then_inc(low2_done, 1)

                def out(n, s, ws, m):
                    pe.wait_ge(added, 2 * n + m + 2)
                    three_passes(nc, out_ps[:], w[ws][:, WDS(0, 1 + m)], w[ws][:, lo(WDS(0, 1 + m))], h_hi[0][s][:], h_lo[0][s][:], True, False)
                    pe.wait_ge(low2_ready, n + 1)
                    three_passes(nc, out_ps[:], w[ws][:, WDS(1, 1 + m)], w[ws][:, lo(WDS(1, 1 + m))], h_hi[1][s][:], h_lo[1][s][:],
                                 False, True).then_inc(out_done, 1)

                def tile(e, t, i, s, ws, first, last):
                    n = 8 * e + t
                    wp = 1 - ws if t is 0 else ws
                    if first:
                        pe.wait_ge(w_in[0], 16)
                        low_rank(0, 0, 0, 0, 0, 1)
                    for m in range(3):
                        pe.wait_ge(*((gated, 2 * n + 1), (product, 2 * n + 1), (product, 2 * n + 2))[m])
                        from_x(gu_ps[m][:], m + 1, t, s, ws, False)
                    if not first:
                        low_rank2(n - 1, 1 - s, wp)
                    pe.wait_ge(low_ready, n + 1)
                    for m in range(3):
                        three_passes(nc, gu_ps[m][:], w[ws][:, WSS(m)], w[ws][:, lo(WSS(m))], low_hi[:], low_lo[:], False, True).then_inc(gu_done, 1)
                    if not first:
                        out(n - 1, 1 - s, wp, 0)
                    if not last:
                        if t is B - 1:
                            pe.wait_ge(w_in[1 - ws], 8 * (e + 1) + 16 - 8 * ((e + 1) % 2 if not isinstance(e, int) else 0)) if False else None
                            wait_weights(e, ws)
                            low_rank(n + 1, 0, 4 * e + 4, 0, 1 - ws, n + 2)
                        else:
                            low_rank(n + 1, t + 1, 4 * e + i + (1 if s else 0), 1 - s, ws, n + 2)
                    if not first:
                        out(n - 1, 1 - s, wp, 1)

                def wait_weights(e, ws):
                    pe.wait_ge(w_in[1 - ws], 8 * e + (16 if ws == 0 else 24))

                walk(pe, tile)
                low_rank2(8 * F - 1, 1, 1)
                out(8 * F - 1, 1, 1, 0)
                out(8 * F - 1, 1, 1, 1)


INPUTS = {
    "x": (B, TT, C), "x_t": (C, T), "pw": (P, PW), "shared": (P, SALL), "bias": (P, GW + KC), "inv": (1, E),
    "experts": (F, P, WE + WM), "scales": (F, WS + C),
    "ident": (P, P), "causal": (P, TT), "cat_sign": (P, 1), "entry": (P, 1),
}


def build(nc, a, out):
    g = {"out": out}
    scratch = lambda n, s, d: nc.dram_tensor(n, s, d, kind="Internal").ap()
    g["wall"] = scratch("wall_scr", [F, P, WALL], F32)
    g["sh_scr"] = scratch("sh_scr", [P, 2 * SALL], F32)
    g["qk_scr"] = scratch("qk_scr", [4, 3, P, T], BF16)
    g["v_scr"] = scratch("v_scr", [B, P, BLK * H * 32], F32)
    g["y_scr"] = scratch("y_scr", [B, NQ, P, TT], F32)
    g["y_heads"] = g["y_scr"].rearrange("b q (h d) t -> b (q h) d t", d=32)
    g["r_scr"] = scratch("r_scr", [B, H, TT], F32)
    g["sw_scr"] = scratch("sw_scr", [SW, T], F32)
    g["cat_scr"] = scratch("cat_scr", [F, 3 * K, T], F32)
    with ExitStack() as ctx:
        sb = lambda n, s, d: ctx.enter_context(nc.sbuf_tensor(n, s, d))
        for n, s, d in (("y", [P, KC, T], F32), ("x_hi", [P, KC, T], F32R), ("x_lo", [P, KC, T], F32R),
                        ("bias", [P, GW + KC], F32), ("ident", [P, P], F32), ("ident_bf", [P, P], BF16),
                        ("causal", [P, TT], F32), ("cat_sign", [P, 1], F32), ("entry", [P, 1], F32)):
            g[n] = sb(n, s, d)
        g["consts"] = [(g[n][:], a[n]) for n in ("bias", "ident", "causal", "cat_sign", "entry")]
        with ExitStack() as before_attention:
            sba = lambda n, s, d: before_attention.enter_context(nc.sbuf_tensor(n, s, d))
            g["logits"] = sba("logits", [P, NBLK, E], F32)
            with ExitStack() as for_projection:
                sbp = lambda n, s, d: for_projection.enter_context(nc.sbuf_tensor(n, s, d))
                g["pw_hi"], g["pw_lo"] = sbp("pw_hi", [P, PW], F32R), sbp("pw_lo", [P, PW], F32R)
                prepare(nc, a, g)
                project(nc, a, g)
            route(nc, a, g)
        attend(nc, a, g)
        share(nc, a, g)
        experts(nc, a, g)


def lay_out(inputs):
    k = {n.replace("L0_attn_", "at_").replace("L0_ffn_", ""): np.asarray(v) for n, v in inputs.items()}
    z = lambda *s: np.zeros(s, np.float32)
    chunks = lambda m: m.reshape(-1, P, m.shape[1]).transpose(1, 0, 2)
    heads = lambda m: m.transpose(1, 0, 2).reshape(C, H * D)
    pad = lambda m, cols: np.concatenate([m, z(m.shape[0], cols - m.shape[1])], 1)
    o = {"x": k["at_x"], "x_t": k["at_x"].reshape(T, C).T}
    groups = [pad(k["gate_weight"].T, P)]
    bias = [z(P)]
    for n in ("v", "q", "k"):
        m, b = heads(k["at_W" + n]), k["at_b" + n].reshape(H * D)
        groups += [m[:, c * P:(c + 1) * P] for c in range(2)]
        bias += [b[c * P:(c + 1) * P] for c in range(2)]
    o["pw"] = chunks(np.concatenate(groups, 1)).reshape(P, PW)
    bias += [k["at_bo"][c * P:(c + 1) * P] for c in range(KC)]
    o["bias"] = np.stack(bias, 1)
    pairs = []
    for i in range(3):
        pairs += [pad(k[n][i * P:(i + 1) * P].T, P) for n in ("sh_gate_W", "sh_up_W")]
    down = np.concatenate([k["sh_down_W"].T, z(3 * P - 2 * I, C)], 0)
    o["shared"] = np.concatenate([chunks(np.concatenate(pairs, 1)).reshape(P, SG), chunks(down).reshape(P, SD),
                                  chunks(k["at_Wo"]).reshape(P, SO)], 1)
    o["inv"] = k["inv_mapping"].reshape(1, E)
    third = lambda gate, up: np.concatenate([pad(gate, 64), pad(up, 64)], 1)
    ex, sc = [], []
    for f in range(F):
        gw, uw = k["gate_W"][f].T, k["up_W"][f].T
        low = np.concatenate([k["gate_qa"][f].reshape(K * R, C).T, k["up_qa"][f].reshape(K * R, C).T], 1)
        wx = chunks(np.concatenate([low, gw[:, :P], uw[:, :P], third(gw[:, P:], uw[:, P:])], 1)).reshape(P, WX)
        qb = [k[n][f].transpose(0, 2, 1).reshape(K * R, -1) for n in ("gate_qb", "up_qb", "down_qb")]
        ws = np.concatenate([
            np.concatenate([qb[0][:, :P], z(64, P), third(qb[0][:, P:], z(64, IR))], 1),
            np.concatenate([z(64, P), qb[1][:, :P], third(z(64, IR), qb[1][:, P:])], 1)], 0)
        dw, da = k["down_W"][f].T, k["down_qa"][f].reshape(K * R, I).T
        inner = np.concatenate([z(I, 64), da, dw], 1)
        wd = np.concatenate([inner, z(64 - IR, 3 * P), np.concatenate([z(64, P), qb[2]], 1)], 0)
        mu = k["mask_up_W"][f]
        spread = np.concatenate([mu, mu, mu, z(C, P - 3 * K)], 1)
        ex.append(np.concatenate([wx, ws, chunks(wd).reshape(P, WD), chunks(spread).reshape(P, WM)], 1))
        gs, us = k["gate_scale"][f][None], k["up_scale"][f][None]
        sc.append(np.concatenate([gs[:, :P], us[:, :P], third(gs[:, P:], us[:, P:]), k["down_scale"][f][None]], 1)[0])
    o["experts"], o["scales"] = np.stack(ex), np.stack(sc)
    o["ident"] = np.eye(P, dtype=np.float32)
    causal = z(P, TT)
    causal[:, TT - P:][np.triu_indices(P, 1)] = NEG
    o["causal"] = causal
    sign = z(P, 1)
    sign[2 * K:3 * K] = -1.0
    o["cat_sign"] = sign
    o["entry"] = np.arange(P, dtype=np.float32)[:, None]
    return {n: np.ascontiguousarray(v) for n, v in o.items()}


def kernel(**inputs):
    import concourse.bacc as bacc
    from concourse.bass_utils import run_bass_kernel_spmd

    nc = bacc.Bacc("TRN2", target_bir_lowering=False, num_devices=1)
    arrays = lay_out(inputs)
    a = {n: nc.dram_tensor("in_" + n, v.shape, mybir.dt.from_np(v.dtype), kind="ExternalInput").ap() for n, v in arrays.items()}
    out = nc.dram_tensor("out_t", (C, T), F32, kind="ExternalOutput").ap()
    build(nc, a, out)
    r = run_bass_kernel_spmd(nc, [{"in_" + n: v for n, v in arrays.items()}], core_ids=[0])
    return np.ascontiguousarray(r.results[0]["out_t"].T).reshape(B, TT, C)
```

```python
from contextlib import ExitStack

import numpy as np
import concourse.bass as bass
from concourse import mybir

F32 = mybir.dt.float32
F32R = mybir.dt.float32r
BF16 = mybir.dt.bfloat16
I32 = mybir.dt.int32
ALU = mybir.AluOpType
ACT = mybir.ActivationFunctionType
AX = mybir.AxisListType.X
ds = bass.ds

P = 128
C = 256
KC = C // P
B, TT = 8, 512
T = B * TT
BLK = TT // P
NBLK = T // P
H, D = 16, 16
HQ = 4
NQ = H // HQ
NQUAD = B * NQ
E, F, K, R, TOPK = 64, 8, 8, 8, 6
I = 176
IR = I - P
GW = 7
EPS = 1e-5
SCALE = float(D) ** -0.5
NEG = -3e38

WX = KC * 4 * P
WS = 3 * P
WD = 2 * 3 * P
WE = WX + WS + WD
WM = KC * P
WCAT = 4 * P
WALL = 2 * WE + WCAT
SW = E + F
SG = KC * 6 * P
SD = 3 * C
SO = KC * C
SALL = SG + SD + SO
PW = KC * GW * P

Q_PART = [0, 0, 0, 1, 1, 2]
K_PART = [0, 1, 2, 0, 1, 0]
KS = 6 * D
KM = KS + 3
P_OFF = [0, TT, 1024, 896]
P_W = 1280


def prepare(nc, a, g):
    with ExitStack() as ctx:
        sb = lambda n, s, d: ctx.enter_context(nc.sbuf_tensor(n, s, d))
        sem = lambda n: ctx.enter_context(nc.semaphore(n))
        pw = sb("pw_raw", [P, PW], F32)
        sw = sb("shared_raw", [P, SALL], F32)
        raw = [sb(f"expert_raw{s}", [P, WE + WM], F32) for s in range(2)]
        sh_hi, sh_lo = sb("shared_hi", [P, SALL], F32R), sb("shared_lo", [P, SALL], F32R)
        scl = [sb(f"expert_scale{s}", [P, WS + C], F32) for s in range(2)]
        done = sb("expert_done", [P, WALL], F32R)
        cat_hi = sb("cat_hi", [P, WCAT], F32R)
        causal = sb("causal", [P, TT], F32)
        cat_ps = [ctx.enter_context(nc.psum_tensor(f"cat_ps{s}", [P, WCAT], F32)) for s in range(2)]
        const_in, pw_in, sw_in = sem("const_in"), sem("pw_in"), sem("sw_in")
        raw_in = [sem(f"raw_in{s}") for s in range(2)]
        stored = sem("expert_stored")
        base_hi, base_lo, shared_kept = sem("base_hi"), sem("base_lo"), sem("shared_kept")
        scaled, part_hi, part_lo = sem("scaled"), sem("part_hi"), sem("part_lo")
        cat_mm, cat_rounded = sem("cat_mm"), sem("cat_rounded")
        with nc.Block() as block:
            @block.sync
            def _(sp):
                sp.dma_start(pw[:], a["pw"]).then_inc(pw_in, 16)
                sp.dma_start(sw[:], a["shared"]).then_inc(sw_in, 16)
                for n, (dst, src) in enumerate(g["consts"]):
                    sp.dma_start(dst, src).then_inc(const_in, 16)
                sp.dma_start(g["y"][:], a["x_t"].rearrange("(c p) t -> p c t", p=P)).then_inc(const_in, 16)
                sp.dma_start(causal[:], a["causal"]).then_inc(const_in, 16)
                sp.wait_ge(base_lo, 2)
                for half, v in enumerate((sh_hi, sh_lo)):
                    sp.dma_start(g["sh_scr"][:, half * SALL:(half + 1) * SALL], v[:].bitcast(F32)).then_inc(shared_kept, 16)
                sp.sem_inc(stored, 16)
                sp.sem_inc(part_lo, 2)
                with sp.Fori(0, F // 2) as i:
                    for s in range(2):
                        sp.wait_ge(part_lo, 2 * i + s + 1)
                        sp.dma_start(raw[s][:], a["experts"][ds(2 * i + s, 1)].rearrange("e p n -> (e p) n")).then_inc(raw_in[s], 16)
                        sp.dma_start(scl[s][:], a["scales"][ds(2 * i + s, 1)].to_broadcast([P, WS + C])).then_inc(raw_in[s], 16)
                        sp.wait_ge(part_lo, 2 * i + s + 3)
                        sp.dma_start(g["wall"][ds(2 * i + s, 1)].rearrange("e p n -> (e p) n"), done[:].bitcast(F32)).then_inc(stored, 16)
                sp.wait_ge(stored, 16 * F + 16)
                sp.wait_ge(shared_kept, 32)
                sp.wait_ge(const_in, 16 * len(g["consts"]) + 32)

            @block.scalar
            def _(act):
                act.wait_ge(pw_in, 16)
                nc.scalar.activation(g["pw_hi"][:], pw[:], ACT.Copy).then_inc(base_hi, 1)
                act.wait_ge(sw_in, 16)
                nc.scalar.activation(sh_hi[:], sw[:], ACT.Copy).then_inc(base_hi, 1)
                with act.Fori(0, F // 2) as i:
                    for s in range(2):
                        act.wait_ge(scaled, 2 * i + s + 1)
                        act.wait_ge(stored, 32 * i + 16 * s + 16)
                        nc.scalar.activation(done[:, 0:WE], raw[s][:, 0:WE], ACT.Copy).then_inc(part_hi, 1)
                        act.wait_ge(cat_mm, 2 * i + s + 1)
                        nc.scalar.activation(cat_hi[:], cat_ps[s][:], ACT.Copy).then_inc(cat_rounded, 1)

            @block.vector
            def _(dve):
                dve.wait_ge(base_hi, 1)
                nc.vector.tensor_tensor(g["pw_lo"][:], pw[:], g["pw_hi"][:].bitcast(F32), ALU.subtract).then_inc(base_lo, 1)
                dve.wait_ge(base_hi, 2)
                nc.vector.tensor_tensor(sh_lo[:], sw[:], sh_hi[:].bitcast(F32), ALU.subtract).then_inc(base_lo, 1)
                dve.wait_ge(const_in, 16 * len(g["consts"]) + 32)
                nc.vector.tensor_copy(g["ident_bf"][:], g["ident"][:]).then_inc(base_lo, 1)
                nc.vector.tensor_copy(g["causal_bf"][:], causal[:]).then_inc(base_lo, 1)
                with dve.Fori(0, F // 2) as i:
                    for s in range(2):
                        dve.wait_ge(raw_in[s], 32 * i + 32)
                        v = raw[s][:, WX:WX + WS]
                        nc.vector.tensor_tensor(v, v, scl[s][:, 0:WS], ALU.mult)
                        v = raw[s][64:P, WX + WS + 3 * P + P:WE]
                        nc.vector.tensor_tensor(v, v, scl[s][64:P, WS:WS + C], ALU.mult).then_inc(scaled, 1)
                        dve.wait_ge(part_hi, 2 * i + s + 1)
                        nc.vector.tensor_tensor(done[:, WE:2 * WE], raw[s][:, 0:WE],
                                                done[:, 0:WE].bitcast(F32), ALU.subtract)
                        dve.wait_ge(cat_rounded, 2 * i + s + 1)
                        nc.vector.scalar_tensor_tensor(done[:, 2 * WE:WALL], cat_hi[:].bitcast(F32), g["cat_sign"][:, 0:1],
                                                       cat_ps[s][:], ALU.mult, ALU.add).then_inc(part_lo, 1)

            @block.tensor
            def _(pe):
                with pe.Fori(0, F // 2) as i:
                    for s in range(2):
                        pe.wait_ge(raw_in[s], 32 * i + 32)
                        for c in range(KC):
                            last = nc.tensor.matmul(cat_ps[s][:], raw[s][:, WE + c * P:WE + (c + 1) * P],
                                                    raw[s][:, c * 4 * P:(c + 1) * 4 * P], start=(c == 0), stop=(c == KC - 1))
                        last.then_inc(cat_mm, 1)


def wait_first(eng, passed, sem, value):
    eng.wait_ge(sem, value)
    eng.sem_inc(passed, 1)


def three_passes(nc, out, w_hi, w_lo, x_hi, x_lo, start, stop):
    nc.tensor.matmul(out, w_hi, x_hi, start=start, stop=False)
    nc.tensor.matmul(out, w_hi, x_lo, start=False, stop=False)
    return nc.tensor.matmul(out, w_lo, x_hi, start=False, stop=stop)



def project(nc, a, g):
    with ExitStack() as ctx:
        sb = lambda n, s, d: ctx.enter_context(nc.sbuf_tensor(n, s, d))
        psum = lambda n, s, d: ctx.enter_context(nc.psum_tensor(n, s, d))
        sem = lambda n: ctx.enter_context(nc.semaphore(n))
        xin = [sb(f"xin{s}", [P, BLK, C], F32) for s in range(2)]
        stat = [sb(f"stat{s}", [P, BLK, 6], F32) for s in range(2)]
        mv = [sb(f"mv{s}", [P, BLK, 2], F32) for s in range(2)]
        std = [sb(f"std{s}", [P, BLK], F32) for s in range(2)]
        rstd = [sb(f"rstd{s}", [P, BLK], F32) for s in range(2)]
        xc_hi = [sb(f"xc_hi{s}", [P, KC, TT], F32R) for s in range(2)]
        xc_lo = [sb(f"xc_lo{s}", [P, KC, TT], F32R) for s in range(2)]
        lgt = sb("logits_t", [E, TT], F32)
        vf = [sb(f"v_f{c}", [P, TT], F32) for c in range(2)]
        vt = [sb(f"v_tok{s}", [P, BLK, H, 32], F32) for s in range(2)]
        qf = [sb(f"qk_f{j}", [P, TT], F32) for j in range(4)]
        rest = [sb(f"qk_rest{j}", [P, TT], F32) for j in range(4)]
        qs = [sb(f"qk_split{s}", [P, 4, 3, TT], BF16) for s in range(2)]
        tp = psum("x_turned_ps", [P, KC, TT], F32)
        gp = [psum(f"group_ps{j}", [P, TT], F32) for j in range(4)]
        lp = psum("logits_ps", [P, BLK, E], F32)
        vp = psum("v_ps", [P, BLK, P], F32)
        x_in = [sem(f"x_in{s}") for s in range(2)]
        x_kept = [sem(f"x_kept{s}") for s in range(2)]
        qkv_kept = [sem(f"qkv_kept{s}") for s in range(2)]
        stats, aggregated, eps_added, root, rooted, normed = map(sem, "stats aggregated eps_added root rooted normed".split())
        turned, x_rounded, x_rest = map(sem, "x_turned x_rounded x_rest".split())
        groups, evacuated = sem("groups_done"), sem("groups_evacuated")
        logits_turned, logits_kept, v_turned, v_kept = map(sem, "logits_turned logits_kept v_turned v_kept".split())
        rest1, part2, part3 = map(sem, "qk_rest1 qk_part2 qk_part3".split())
        passed = sem("passed")
        EV, EV_TILE = [1, 2, 3, 5, 7, 9, 11], 11
        with nc.Block() as block:
            @block.sync
            def _(sp):
                for s in range(2):
                    sp.sem_inc(x_kept[s], 32)
                    sp.sem_inc(qkv_kept[s], 80)
                sp.sem_inc(x_rest, 1)
                sp.sem_inc(evacuated, EV_TILE)
                sp.sem_inc(logits_turned, 1)
                sp.sem_inc(logits_kept, 1)
                sp.sem_inc(v_turned, 2)
                sp.sem_inc(v_kept, 1)
                sp.sem_inc(rest1, 4)
                sp.sem_inc(part3, 4)
                for s in range(2):
                    sp.dma_start(xin[s][:], a["x"][s].rearrange("(b p) c -> p b c", p=P)).then_inc(x_in[s], 16)

                def tile(t, s, more):
                    if more:
                        sp.wait_ge(turned, t + 1)
                        sp.dma_start(xin[s][:], a["x"][ds(t + 2, 1)].rearrange("o (b p) c -> p (o b) c", p=P)).then_inc(x_in[s], 16)
                    sp.wait_ge(x_rest, t + 2)
                    sp.dma_start(g["x_hi"][:, :, ds(t * TT, TT)].bitcast(F32), xc_hi[s][:].bitcast(F32)).then_inc(x_kept[s], 16)
                    sp.dma_start(g["x_lo"][:, :, ds(t * TT, TT)].bitcast(F32), xc_lo[s][:].bitcast(F32)).then_inc(x_kept[s], 16)
                    sp.wait_ge(v_kept, 2 * t + 3)
                    sp.dma_start(g["v_scr"][ds(t, 1)].rearrange("b p n -> (b p) n"), vt[s][:].rearrange("p b h d -> p (b h d)")).then_inc(qkv_kept[s], 16)
                    for j in range(4):
                        wait_first(sp, passed, part3, 4 * t + j + 5)
                        sp.dma_start(g["qk_scr"][j, :, :, ds(t * TT, TT)].rearrange("s p t -> p s t"), qs[s][:, j]).then_inc(qkv_kept[s], 16)

                with sp.Fori(0, B // 2 - 1) as i:
                    for s in range(2):
                        tile(2 * i + s, s, True)
                for s in range(2):
                    tile(B - 2 + s, s, False)
                for s in range(2):
                    sp.wait_ge(x_kept[s], 16 * B + 32)
                    sp.wait_ge(qkv_kept[s], 40 * B + 80)

            @block.vector
            def _(dve):
                for s in range(2):
                    nc.vector.memset(vt[s][:, :, :, D:D + 1], 1.0)
                    nc.vector.memset(vt[s][:, :, :, D + 1:32], 0.0)

                def norm(t, i, s):
                    dve.wait_ge(x_in[s], 16 * i + 16)
                    for b in range(BLK):
                        nc.vector.bn_stats(stat[s][:, b], xin[s][:, b]).then_inc(stats, 1)
                    for b in range(BLK):
                        wait_first(dve, passed, stats, BLK * t + b + 1)
                        nc.vector.bn_aggr(mv[s][:, b], stat[s][:, b]).then_inc(aggregated, 1)
                    dve.wait_ge(aggregated, BLK * t + BLK)
                    nc.vector.tensor_scalar_add(std[s][:], mv[s][:, :, 1], EPS).then_inc(eps_added, 1)
                    dve.wait_ge(root, t + 1)
                    nc.vector.reciprocal(rstd[s][:], std[s][:]).then_inc(rooted, 1)
                    dve.wait_ge(rooted, t + 1)
                    for b in range(BLK):
                        last = nc.vector.tensor_scalar(xin[s][:, b], xin[s][:, b], mv[s][:, b, 0:1], rstd[s][:, b:b + 1],
                                                       ALU.subtract, ALU.mult)
                    last.then_inc(normed, 1)

                def x_low(t, s):
                    dve.wait_ge(x_rounded, t + 1)
                    nc.vector.tensor_tensor(xc_lo[s][:], tp[:], xc_hi[s][:].bitcast(F32), ALU.subtract).then_inc(x_rest, 1)

                def split(t, s, j):
                    dve.wait_ge(evacuated, EV_TILE * t + EV_TILE + EV[3 + j])
                    dve.wait_ge(part3, 4 * t + j + 1)
                    nc.vector.tensor_tensor(rest[j][:], qf[j][:], qs[s][:, j, 0], ALU.subtract).then_inc(rest1, 1)
                    dve.wait_ge(rest1, 4 * t + j + 5)
                    nc.vector.tensor_copy(qs[s][:, j, 1], rest[j][:]).then_inc(part2, 1)

                def tile(t, i, s, more):
                    if more:
                        norm(t + 1, i + s, 1 - s)
                    dve.wait_ge(logits_turned, t + 2)
                    nc.vector.tensor_copy(g["logits"][:, ds(t * BLK, BLK), :], lp[:]).then_inc(logits_kept, 1)
                    dve.wait_ge(qkv_kept[s], 80 * i + 80)
                    for c in range(2):
                        dve.wait_ge(v_turned, 2 * t + c + 3)
                        nc.vector.tensor_copy(vt[s][:, :, 8 * c:8 * c + 8, 0:D],
                                              vp[:].rearrange("p b (h d) -> p b h d", d=D)).then_inc(v_kept, 1)
                    split(t, s, 0)
                    split(t, s, 1)
                    if more:
                        x_low(t + 1, 1 - s)
                    split(t, s, 2)
                    split(t, s, 3)

                norm(0, 0, 0)
                x_low(0, 0)
                with dve.Fori(0, B // 2 - 1) as i:
                    for s in range(2):
                        tile(2 * i + s, i, s, True)
                for s in range(2):
                    tile(B - 2 + s, B // 2 - 1, s, s == 0)

            @block.gpsimd
            def _(pool):
                with pool.Fori(0, B // 2) as i:
                    for s in range(2):
                        for j in range(4):
                            pool.wait_ge(part2, 8 * i + 4 * s + j + 1)
                            nc.gpsimd.tensor_tensor(qs[s][:, j, 2], rest[j][:], qs[s][:, j, 1], ALU.subtract).then_inc(part3, 1)

            @block.scalar
            def _(act):
                def x_high(t, i, s):
                    act.wait_ge(turned, t + 1)
                    act.wait_ge(x_kept[s], 32 * i + 32)
                    nc.scalar.activation(xc_hi[s][:], tp[:], ACT.Copy).then_inc(x_rounded, 1)

                def take_root(t, s):
                    act.wait_ge(eps_added, t + 1)
                    nc.scalar.activation(std[s][:], std[s][:], ACT.Sqrt).then_inc(root, 1)

                def evacuate(t, i, s, n):
                    act.wait_ge(groups, GW * t + n + 1)
                    bank = gp[n % 4]
                    if n == 0:
                        act.wait_ge(logits_turned, t + 1)
                        nc.scalar.activation(lgt[:], bank[0:E], ACT.Copy).then_inc(evacuated, 1)
                    elif n <= 2:
                        act.wait_ge(v_turned, 2 * t + n)
                        nc.scalar.activation(vf[n - 1][:], bank[:], ACT.Identity, bias=g["bias"][:, n:n + 1]).then_inc(evacuated, 1)
                    else:
                        j = n - 3
                        act.wait_ge(rest1, 4 * t + j + 1)
                        act.wait_ge(qkv_kept[s], 80 * i + 80)
                        nc.scalar.activation(qf[j][:], bank[:], ACT.Identity, bias=g["bias"][:, n:n + 1]).then_inc(evacuated, 1)
                        nc.scalar.activation(qs[s][:, j, 0], bank[:], ACT.Identity, bias=g["bias"][:, n:n + 1]).then_inc(evacuated, 1)

                def tile(t, i, s, more):
                    if more:
                        take_root(t + 1, 1 - s)
                    for n in range(5):
                        evacuate(t, i, s, n)
                    if more:
                        x_high(t + 1, i + s, 1 - s)
                    for n in range(5, GW):
                        evacuate(t, i, s, n)

                take_root(0, 0)
                x_high(0, 0, 0)
                with act.Fori(0, B // 2 - 1) as i:
                    for s in range(2):
                        tile(2 * i + s, i, s, True)
                for s in range(2):
                    tile(B - 2 + s, B // 2 - 1, s, s == 0)

            @block.tensor
            def _(pe):
                def turn_x(t, s):
                    pe.wait_ge(normed, t + 1)
                    pe.wait_ge(x_rest, t + 1)
                    for c in range(KC):
                        for b in range(BLK):
                            last = nc.tensor.transpose(tp[:, c, b * P:(b + 1) * P], xin[s][:, b, c * P:(c + 1) * P], g["ident"][:])
                    last.then_inc(turned, 1)

                def group(t, s, n):
                    before = EV[n - 4] + EV_TILE if n >= 4 else EV[n + 4] if n < 3 else EV[3]
                    pe.wait_ge(evacuated, EV_TILE * t + before)
                    for c in range(KC):
                        w = slice((c * GW + n) * P, (c * GW + n + 1) * P)
                        last = three_passes(nc, gp[n % 4][:], g["pw_hi"][:, w], g["pw_lo"][:, w],
                                            xc_hi[s][:, c], xc_lo[s][:, c], c == 0, c == KC - 1)
                    last.then_inc(groups, 1)

                def turn_v(t, c):
                    pe.wait_ge(evacuated, EV_TILE * t + EV_TILE + EV[1 + c])
                    pe.wait_ge(v_kept, 2 * t + c + 1)
                    for b in range(BLK):
                        last = nc.tensor.transpose(vp[:, b], vf[c][:, b * P:(b + 1) * P], g["ident"][:])
                    last.then_inc(v_turned, 1)

                def tile(t, s, more):
                    pe.wait_ge(x_rest, t + 2)
                    for n in range(3):
                        group(t, s, n)
                    pe.wait_ge(evacuated, EV_TILE * t + EV_TILE + EV[0])
                    wait_first(pe, passed, logits_kept, t + 1)
                    for b in range(BLK):
                        last = nc.tensor.transpose(lp[:, b], lgt[:, b * P:(b + 1) * P], g["ident"][0:E, 0:E])
                    last.then_inc(logits_turned, 1)
                    group(t, s, 3)
                    turn_v(t, 0)
                    group(t, s, 4)
                    turn_v(t, 1)
                    if more:
                        turn_x(t + 1, 1 - s)
                    group(t, s, 5)
                    group(t, s, 6)

                turn_x(0, 0)
                with pe.Fori(0, B // 2 - 1) as i:
                    for s in range(2):
                        tile(2 * i + s, s, True)
                for s in range(2):
                    tile(B - 2 + s, s, s == 0)


def route(nc, a, g):
    with ExitStack() as ctx:
        sb = lambda n, s, d: ctx.enter_context(nc.sbuf_tensor(n, s, d))
        psum = lambda n, s, d: ctx.enter_context(nc.psum_tensor(n, s, d))
        sem = lambda n: ctx.enter_context(nc.semaphore(n))
        CAND = E + 8
        work = sb("route_work", [P, NBLK, E], F32)
        scores = sb("scores", [P, NBLK, CAND], F32)
        marked = sb("marked", [P, NBLK, CAND], F32)
        top = sb("top", [P, NBLK, 8], F32)
        row = sb("row", [P, NBLK], F32)
        dense_t = sb("dense_t", [E, NBLK, P], F32)
        flat = sb("flat", [P, NBLK, E], F32)
        f8 = sb("per_expert", [P, NBLK * F], F32)
        soft = sb("soft", [P, NBLK, SW], F32)
        inv_i = sb("inv_i", [E, E], I32)
        pick = sb("pick", [E, E], F32)
        sw_t = sb("soft_t", [SW, 2, TT], F32)
        sw_hi = sb("soft_hi", [E, 2, TT], F32R)
        sw_lo = sb("soft_lo", [E, 2, TT], F32R)
        turn_ps = [psum(f"route_turn{j}", [SW, BLK, P], F32) for j in range(2)]
        flat_ps = [psum(f"flat_ps{j}", [P, 8, E], F32) for j in range(4)]
        inv_in = sem("inv_in")
        kept = [sem(f"soft_kept{s}") for s in range(2)]
        chain = sem("route_step")
        act_step, dense_ready, soft_ready = sem("route_act"), sem("dense_ready"), sem("soft_ready")
        dense_turned, dense_copied, picked, soft_turned, soft_copied = map(
            sem, "dense_turned dense_copied picked soft_turned soft_copied".split())
        split_hi, split_lo = sem("soft_split_hi"), sem("soft_split_lo")
        steps = []
        with nc.Block() as block:
            @block.vector
            def _(dve):
                def step(ins):
                    steps.append(1)
                    ins.then_inc(chain, 1)
                    dve.wait_ge(chain, len(steps))

                bc = lambda v, m: v.unsqueeze(2).broadcast_to([P, v.shape[1], m])
                logits = g["logits"]
                step(nc.vector.tensor_reduce(row[:], logits[:], AX, ALU.max))
                step(nc.vector.tensor_tensor(work[:], logits[:], bc(row[:], E), ALU.subtract))
                step(nc.vector.memset(scores[:, :, E:CAND], -1.0))
                dve.wait_ge(act_step, 1)
                step(nc.vector.tensor_reduce(row[:], work[:], AX, ALU.add))
                step(nc.vector.reciprocal(row[:], row[:]))
                step(nc.vector.tensor_tensor(scores[:, :, 0:E], work[:], bc(row[:], E), ALU.mult))
                for b in range(NBLK):
                    last = nc.vector.max(top[:, b], scores[:, b, 0:E])
                step(last)
                step(nc.vector.memset(top[:, :, TOPK:8], -1.0))
                for b in range(NBLK):
                    last = nc.vector.match_replace(marked[:, b], top[:, b], scores[:, b], -2.0)
                step(last)
                step(nc.vector.scalar_tensor_tensor(work[:], marked[:, :, 0:E], -2.0, scores[:, :, 0:E], ALU.is_equal, ALU.mult))
                dve.wait_ge(inv_in, 16)
                step(nc.vector.tensor_copy(pick[:], inv_i[:]))
                nc.vector.tensor_scalar(pick[:], pick[:], g["entry"][0:E, 0:1], None, ALU.is_equal).then_inc(dense_ready, 1)
                for j in range(4):
                    dve.wait_ge(picked, j + 1)
                    last = nc.vector.tensor_copy(flat[:, 8 * j:8 * j + 8], flat_ps[j][:])
                step(last)
                v = flat[:].rearrange("p b (f k) -> p (b f) k", k=K)
                w = work[:].rearrange("p b (f k) -> p (b f) k", k=K)
                scalars = soft[:, :, E:SW]
                step(nc.vector.tensor_reduce(scalars, flat[:].rearrange("p b (f k) -> p b f k", k=K), AX, ALU.add))
                step(nc.vector.tensor_scalar(work[:], flat[:], 0.0, -1e9, ALU.is_equal, ALU.mult))
                step(nc.vector.tensor_tensor(work[:], work[:], flat[:], ALU.add))
                step(nc.vector.tensor_reduce(f8[:], w, AX, ALU.max))
                step(nc.vector.tensor_tensor(w, w, bc(f8[:], K), ALU.subtract))
                dve.wait_ge(act_step, 2)
                step(nc.vector.tensor_reduce(f8[:], w, AX, ALU.add))
                step(nc.vector.reciprocal(f8[:], f8[:]))
                nc.vector.tensor_tensor(soft[:, :, 0:E].rearrange("p b (f k) -> p b f k", k=K),
                                        work[:].rearrange("p b (f k) -> p b f k", k=K),
                                        f8[:].rearrange("p (b f) -> p b f", f=F).unsqueeze(3).broadcast_to([P, NBLK, F, K]),
                                        ALU.mult).then_inc(soft_ready, 1)
                for t in range(B):
                    dve.wait_ge(split_hi, t + 1)
                    nc.vector.tensor_tensor(sw_lo[:, t % 2], sw_t[0:E, t % 2], sw_hi[:, t % 2].bitcast(F32), ALU.subtract).then_inc(split_lo, 1)

            @block.scalar
            def _(act):
                act.wait_ge(chain, 2)
                nc.scalar.activation(work[:], work[:], ACT.Exp).then_inc(act_step, 1)
                for t in range(B):
                    act.wait_ge(dense_turned, t + 1)
                    nc.scalar.activation(dense_t[:, t * BLK:(t + 1) * BLK], turn_ps[t % 2][0:E], ACT.Copy).then_inc(dense_copied, 1)
                act.wait_ge(chain, 17)
                nc.scalar.activation(work[:], work[:], ACT.Exp).then_inc(act_step, 1)
                for t in range(B):
                    act.wait_ge(soft_turned, t + 1)
                    if t >= 2:
                        act.wait_ge(kept[t % 2], 64 * (t // 2))
                    nc.scalar.activation(sw_t[:, t % 2], turn_ps[t % 2][:].rearrange("p b t -> p (b t)"), ACT.Copy).then_inc(soft_copied, 1)
                    nc.scalar.activation(sw_hi[:, t % 2], turn_ps[t % 2][0:E].rearrange("p b t -> p (b t)"), ACT.Copy).then_inc(split_hi, 1)

            @block.tensor
            def _(pe):
                pe.wait_ge(dense_ready, 1)
                for t in range(B):
                    if t >= 2:
                        pe.wait_ge(dense_copied, t - 1)
                    for b in range(BLK):
                        last = nc.tensor.transpose(turn_ps[t % 2][0:E, b], work[:, t * BLK + b], g["ident"][:])
                    last.then_inc(dense_turned, 1)
                for j in range(4):
                    pe.wait_ge(dense_copied, 2 * j + 2)
                    for b in range(8):
                        last = nc.tensor.matmul(flat_ps[j][:, b], dense_t[:, 8 * j + b], pick[:], start=True, stop=True)
                    last.then_inc(picked, 1)
                pe.wait_ge(soft_ready, 1)
                for t in range(B):
                    if t >= 2:
                        pe.wait_ge(split_hi, t - 1)
                    for b in range(BLK):
                        last = nc.tensor.transpose(turn_ps[t % 2][:, b], soft[:, t * BLK + b], g["ident"][:])
                    last.then_inc(soft_turned, 1)

            @block.sync
            def _(sp):
                sp.dma_start(inv_i[:], a["inv"].to_broadcast([E, E])).then_inc(inv_in, 16)
                for t in range(B):
                    tok = slice(t * TT, (t + 1) * TT)
                    sp.wait_ge(soft_copied, t + 1)
                    sp.dma_start(g["sw_scr"][:, tok], sw_t[:, t % 2]).then_inc(kept[t % 2], 16)
                    sp.wait_ge(split_lo, t + 1)
                    for part, src in enumerate((sw_hi, sw_lo, sw_hi)):
                        sp.dma_start(g["cat_scr"][:, part * K:(part + 1) * K, tok], src[:, t % 2].bitcast(F32)).then_inc(kept[t % 2], 16)
                for s in range(2):
                    sp.wait_ge(kept[s], 32 * B)


def reached(eng, sem, value):
    if not isinstance(value, int) or value > 0:
        eng.wait_ge(sem, value)


def share(nc, a, g):
    with ExitStack() as ctx:
        sb = lambda n, s, d: ctx.enter_context(nc.sbuf_tensor(n, s, d))
        psum = lambda n, s, d: ctx.enter_context(nc.psum_tensor(n, s, d))
        sem = lambda n: ctx.enter_context(nc.semaphore(n))
        sh_hi, sh_lo = sb("sh_hi", [P, SG + SD], F32R), sb("sh_lo", [P, SG + SD], F32R)
        sh_in = sem("sh_in")
        sg = [sb(f"silu{s}", [P, TT], F32) for s in range(2)]
        h_hi = [sb(f"h_hi{s}", [P, TT], F32R) for s in range(3)]
        h_lo = [sb(f"h_lo{s}", [P, TT], F32R) for s in range(3)]
        gu = [[psum(f"gu{j}{s}", [P, TT], F32) for s in range(2)] for j in range(2)]
        out_ps = psum("out_ps", [P, KC, TT], F32)
        gate_up, gated, product, h_rounded, h_ready, summed, added = map(
            sem, "sh_gate_up sh_gated sh_product sh_rounded sh_ready sh_summed sh_added".split())
        W1 = lambda c, m: slice((c * 6 + m) * P, (c * 6 + m + 1) * P)
        W2 = lambda i, m: slice(SG + i * C + m * P, SG + i * C + (m + 1) * P)
        with nc.Block() as block:
            def tiles(eng, tile):
                with eng.Fori(0, B // 2) as i:
                    for s in range(2):
                        tile(2 * i + s, i, s)

            @block.sync
            def _(sp):
                sp.sem_inc(summed, 1)
                sp.sem_inc(product, 2)
                sp.sem_inc(added, 1)
                for half, v in enumerate((sh_hi, sh_lo)):
                    sp.dma_start(v[:].bitcast(F32), g["sh_scr"][:, half * SALL:half * SALL + SG + SD]).then_inc(sh_in, 16)

            @block.vector
            def _(dve):
                def tile(t, i, s):
                    for j in range(3):
                        n = 3 * t + j
                        dve.wait_ge(gated, n + 1)
                        slot = (3 * s + j) % 2
                        nc.vector.tensor_tensor(sg[slot][:], sg[slot][:], gu[slot][1][:], ALU.mult).then_inc(product, 1)
                        dve.wait_ge(h_rounded, n + 1)
                        nc.vector.tensor_tensor(h_lo[j][:], sg[slot][:], h_hi[j][:].bitcast(F32), ALU.subtract).then_inc(h_ready, 1)
                    dve.wait_ge(summed, t + 2)
                    v = g["y"][:, :, ds(t * TT, TT)]
                    nc.vector.tensor_tensor(v, out_ps[:], v, ALU.add).then_inc(added, 1)
                tiles(dve, tile)

            @block.scalar
            def _(act):
                def tile(t, i, s):
                    for j in range(3):
                        n = 3 * t + j
                        slot = (3 * s + j) % 2
                        act.wait_ge(gate_up, n + 1)
                        act.wait_ge(product, n + 1)
                        nc.scalar.activation(sg[slot][:], gu[slot][0][:], ACT.Silu).then_inc(gated, 1)
                        act.wait_ge(product, n + 3)
                        if j == 0:
                            act.wait_ge(summed, t + 1)
                        nc.scalar.activation(h_hi[j][:], sg[slot][:], ACT.Copy).then_inc(h_rounded, 1)
                tiles(act, tile)

            @block.tensor
            def _(pe):
                def gates(t, s, j):
                    n = 3 * t + j
                    slot = (3 * s + j) % 2
                    pe.wait_ge(product, n + 1)
                    for r in range(2):
                        for c in range(KC):
                            w = W1(c, 2 * j + r)
                            tok = ds(t * TT, TT)
                            last = three_passes(nc, gu[slot][r][:], sh_hi[:, w], sh_lo[:, w],
                                                g["x_hi"][:, c, tok], g["x_lo"][:, c, tok], c == 0, c == KC - 1)
                    last.then_inc(gate_up, 1)

                def down(t, j):
                    pe.wait_ge(h_ready, 3 * t + j + 1)
                    if j == 0:
                        pe.wait_ge(added, t + 1)
                    for m in range(KC):
                        last = three_passes(nc, out_ps[:, m], sh_hi[:, W2(j, m)], sh_lo[:, W2(j, m)],
                                            h_hi[j][:], h_lo[j][:], j == 0, j == 2)
                    if j == 2:
                        last.then_inc(summed, 1)

                def tile(t, i, s):
                    gates(t, s, 0)
                    gates(t, s, 1)
                    down(t, 0)
                    gates(t, s, 2)
                    down(t, 1)
                    down(t, 2)
                pe.wait_ge(sh_in, 32)
                tiles(pe, tile)


def walk(eng, tile):
    def expert(e, ws, first=False, last=False):
        for t in range(B):
            tile(e, t, ws, first and t == 0, last)

    expert(0, 0, first=True)
    with eng.Fori(0, F // 2 - 1) as i:
        expert(2 * i + 1, 1)
        expert(2 * i + 2, 0)
    expert(F - 1, 1, last=True)


def experts(nc, a, g):
    with ExitStack() as ctx:
        sb = lambda n, s, d: ctx.enter_context(nc.sbuf_tensor(n, s, d))
        psum = lambda n, s, d: ctx.enter_context(nc.psum_tensor(n, s, d))
        sem = lambda n: ctx.enter_context(nc.semaphore(n))
        w = [sb(f"expert_w{s}", [P, WALL], F32R) for s in range(2)]
        wrep = [sb(f"soft_rep{s}", [P, TT], F32) for s in range(2)]
        srep = sb("scalar_rep", [P, TT], F32)
        cat = sb("soft_stack", [P, TT], F32R)
        low, low_hi, low_lo = sb("low", [P, TT], F32), sb("low_hi", [P, TT], F32R), sb("low_lo", [P, TT], F32R)
        h = [sb(f"h{c}", [P, TT], F32) for c in range(2)]
        h_hi = [sb(f"eh_hi{c}", [P, TT], F32R) for c in range(2)]
        h_lo = [sb(f"eh_lo{c}", [P, TT], F32R) for c in range(2)]
        low2 = h[1]
        low_ps = psum("low_ps", [P, TT], F32)
        gu_ps = [psum(f"expert_gu{m}", [P, TT], F32) for m in range(3)]
        out_ps = psum("expert_out", [P, TT], F32)
        w_in = [sem(f"expert_w_in{s}") for s in range(2)]
        wrep_in = [sem(f"wrep_in{s}") for s in range(2)]
        srep_in, cat_in = sem("srep_in"), sem("cat_in")
        zeroed = sem("zeroed")
        low_done, weighted, low_rounded, low_ready = map(sem, "low_done weighted low_rounded low_ready".split())
        gu_done, gated, product, scaled, h_rounded, h_ready = map(
            sem, "gu_done gated product scaled h_rounded h_ready".split())
        low2_done, weighted2, low2_rounded, low2_ready = map(sem, "low2_done weighted2 low2_rounded low2_ready".split())
        out_done, added = sem("expert_out_done"), sem("expert_added")
        WXS = lambda c, m: slice((c * 4 + m) * P, (c * 4 + m + 1) * P)
        WSS = lambda m: slice(WX + m * P, WX + (m + 1) * P)
        WDS = lambda c, m: slice(WX + WS + (c * 3 + m) * P, WX + WS + (c * 3 + m + 1) * P)
        CATS = lambda m: slice(2 * WE + m * P, 2 * WE + (m + 1) * P)
        lo = lambda sl: slice(sl.start + WE, sl.stop + WE)
        IRP = 64
        HALVES = ((0, slice(0, P)), (1, slice(0, IR)))
        q_st = [sb(f"q_stack{s}", [P, HQ, TT], BF16) for s in range(2)]
        k_st = [sb(f"k_stack{s}", [P, HQ, TT], BF16) for s in range(2)]
        v_st = sb("v_stack", [P, BLK, HQ * 32], F32)
        mx = sb("row_max", [P, HQ * BLK], F32)
        mrest = sb("row_max_rest", [P, HQ * BLK], F32)
        mparts = sb("row_max_parts", [P, 3, HQ * BLK], BF16)
        m_t = sb("row_max_t", [3 * HQ * BLK, P], BF16)
        prob = sb("prob", [P, HQ, P_W], F32)
        y_out = sb("y_out", [P, TT], F32)
        ma_ps = psum("max_ps", [P, TT], F32)
        s_ps = psum("score_ps", [P, TT], F32)
        y_ps = psum("y_ps", [P, TT], F32)
        qk_in = [sem(f"qk_in{s}") for s in range(2)]
        v_in, m_in, y_kept, passed = sem("v_in"), sem("m_in"), sem("y_kept"), sem("passed")
        row_scored, maxed, m_part, m_turned, m_copied = map(sem, "row_scored maxed m_part m_turned m_copied".split())
        scored, exped, masked, mixed, y_copied = map(sem, "scored exped masked mixed y_copied".split())
        NLOAD = 12 * 16
        NBLOCK = HQ * BLK
        NGROUP = 5
        GROUP_AT = [[3, 4, 5, 6, 7], [0, 1, 2, 3, 4]]
        last_step = 8 * F - 1
        m_turned_out = ma_ps[0:3 * HQ * BLK, 0:P // 2].bitcast(BF16)

        with nc.Block() as block:
            @block.sync
            def _(sp):
                def load_wrep(n, e, t):
                    s, tok = t % 2, slice(t * TT, (t + 1) * TT)
                    reached(sp, weighted2, n - 1)
                    for half in range(2):
                        sp.dma_start(wrep[s][half * 64:half * 64 + 64], g["sw_scr"][ds(e * K, K), tok].unsqueeze(1).broadcast_to([K, R, TT])).then_inc(wrep_in[s], 16)

                def load_cat(n, e, t):
                    reached(sp, gu_done, 3 * n - 2)
                    sp.dma_start(cat[0:3 * K].bitcast(F32), g["cat_scr"][ds(e, 1), :, t * TT:(t + 1) * TT].rearrange("o k t -> (o k) t")).then_inc(cat_in, 16)

                def load_srep(n, e, t):
                    reached(sp, scaled, 2 * n)
                    sp.dma_start(srep[:], g["sw_scr"][ds(e + E, 1), t * TT:(t + 1) * TT].to_broadcast([P, TT])).then_inc(srep_in, 16)

                def load_qk(b, q):
                    s = q % 2
                    rows = slice((q % 2) * HQ * D, (q % 2 + 1) * HQ * D)
                    for st, j, parts in ((q_st, q // 2, Q_PART), (k_st, 2 + q // 2, K_PART)):
                        for slot, part in enumerate(parts):
                            src = g["qk_scr"][j, part, rows, ds(b * TT, TT)].rearrange("(h d) t -> d h t", d=D)
                            sp.dma_start(st[s][slot * D:(slot + 1) * D], src).then_inc(qk_in[s], 16)

                def load_v(b, q):
                    sp.dma_start(v_st[:], g["v_scr"][ds(b, 1)].rearrange("o p (k n) -> p (o k) n", k=BLK)[:, :, q * HQ * 32:(q + 1) * HQ * 32]).then_inc(v_in, 16)

                def keep_y(b, q):
                    sp.dma_start(g["y_scr"][ds(b, 1), q].rearrange("o p t -> (o p) t"), y_out[:]).then_inc(y_kept, 16)

                def step(e, t, ws, first, last):
                    n, q = 8 * e + t, t // 2
                    quad = 4 * e + q
                    more = not (last and t == B - 1)
                    following = (n + 1, e, t + 1) if t < B - 1 else (n + 1, e + 1, 0)
                    if t % 2 == 0:
                        sp.wait_ge(m_copied, quad + 1)
                        sp.dma_start(q_st[q % 2][KS:KM].rearrange("j h t -> j (h t)").rearrange("j (n t) -> j n t", t=P), m_t[:]).then_inc(m_in, 16)
                        if not first:
                            wait_first(sp, passed, y_copied, quad)
                            if t == 0:
                                keep_y(e - 1, NQ - 1)
                            else:
                                keep_y(e, q - 1)
                            load_v(e, q)
                    if more:
                        load_cat(*following)
                        load_wrep(*following)
                    if t % 2 == 1 and not (last and q >= NQ - 2):
                        wait_first(sp, passed, scored, NGROUP * n + NGROUP)
                        if q < NQ - 2:
                            load_qk(e, q + 2)
                        else:
                            load_qk(e + 1, q - 2)
                    if more:
                        load_srep(*following)

                sp.wait_ge(zeroed, 1)
                load_qk(0, 0)
                load_qk(0, 1)
                load_v(0, 0)
                load_cat(0, 0, 0)
                load_wrep(0, 0, 0)
                load_srep(0, 0, 0)
                walk(sp, step)
                sp.wait_ge(y_copied, NQUAD)
                keep_y(B - 1, NQ - 1)
                sp.wait_ge(y_kept, 16 * NQUAD)

            @block.vector
            def _(dve):
                nc.vector.memset(cat[:].bitcast(F32), 0.0)
                nc.vector.memset(h_hi[1][:].bitcast(F32), 0.0)
                nc.vector.memset(h_lo[1][:].bitcast(F32), 0.0)
                for s in range(2):
                    last_set = nc.vector.memset(k_st[s][KS:KM], 1.0)
                last_set.then_inc(zeroed, 1)

                def weight(n, e, t):
                    s = t % 2
                    dve.wait_ge(low_done, n + 1)
                    dve.wait_ge(wrep_in[s], 32 * (4 * e + t // 2) + 32)
                    nc.vector.tensor_tensor(low[:], low_ps[:], wrep[s][:], ALU.mult).then_inc(weighted, 1)

                def weight2(n, s):
                    dve.wait_ge(low2_done, n + 1)
                    nc.vector.tensor_tensor(low2[IRP:P], low_ps[IRP:P], wrep[s][IRP:P], ALU.mult).then_inc(weighted2, 1)
                    dve.wait_ge(low2_rounded, n + 1)
                    nc.vector.tensor_tensor(h_lo[1][IRP:P], low2[IRP:P], h_hi[1][IRP:P].bitcast(F32), ALU.subtract).then_inc(low2_ready, 1)

                def add(n, t, c):
                    dve.wait_ge(out_done, 2 * n + c + 1)
                    v = g["y"][:, c, t * TT:(t + 1) * TT]
                    nc.vector.tensor_tensor(v, out_ps[:], v, ALU.add).then_inc(added, 1)

                def maximum(quad, x):
                    wd = (x % BLK + 1) * P
                    wait_first(dve, passed, row_scored, NBLOCK * quad + x + 1)
                    nc.vector.tensor_tensor_reduce(out=ma_ps[:, 0:wd], in0=ma_ps[:, 0:wd], in1=g["causal_bf"][:, TT - wd:TT],
                                                   scale=1.0, scalar=NEG, op0=ALU.add, op1=ALU.max,
                                                   accum_out=mx[:, x:x + 1]).then_inc(maxed, 1)

                def split_max(quad):
                    dve.wait_ge(maxed, NBLOCK * quad + NBLOCK)
                    reached(dve, m_turned, quad)
                    nc.vector.tensor_scalar(mparts[:, 0], mx[:], -1.0, None, ALU.mult).then_inc(m_part, 1)
                    dve.wait_ge(m_part, 4 * quad + 1)
                    nc.vector.scalar_tensor_tensor(mrest[:], mx[:], -1.0, mparts[:, 0], ALU.mult, ALU.subtract).then_inc(m_part, 1)
                    dve.wait_ge(m_part, 4 * quad + 2)
                    nc.vector.tensor_copy(mparts[:, 1], mrest[:]).then_inc(m_part, 1)
                    dve.wait_ge(m_part, 4 * quad + 3)
                    nc.vector.tensor_tensor(mparts[:, 2], mrest[:], mparts[:, 1], ALU.subtract).then_inc(m_part, 1)

                def copy_y(quad):
                    dve.wait_ge(mixed, quad + 1)
                    reached(dve, y_kept, 16 * quad)
                    nc.vector.tensor_copy(y_out[:], y_ps[:]).then_inc(y_copied, 1)

                def step(e, t, ws, first, last):
                    n, q = 8 * e + t, t // 2
                    quad = 4 * e + q
                    before = (t - 1) % B
                    ahead = not (last and q == NQ - 1)
                    def attend(i):
                        if ahead:
                            maximum(quad + 1, 8 * (t % 2) + i)
                    if first:
                        weight(0, 0, 0)
                    dve.wait_ge(low_rounded, n + 1)
                    nc.vector.tensor_tensor(low_lo[:], low[:], low_hi[:].bitcast(F32), ALU.subtract).then_inc(low_ready, 1)
                    if t % 2 == 0:
                        dve.wait_ge(m_turned, quad + 1)
                        reached(dve, m_in, 16 * quad)
                        nc.vector.tensor_copy(m_t[:], m_turned_out).then_inc(m_copied, 1)
                    attend(0)
                    attend(1)
                    attend(2)
                    if t % 2 == 0 and not first:
                        copy_y(quad - 1)
                    if not first:
                        weight2(n - 1, 1 - t % 2)
                    attend(3)
                    dve.wait_ge(gated, 2 * n + 1)
                    dve.wait_ge(gu_done, 3 * n + 2)
                    nc.vector.tensor_tensor(h[0][:], h[0][:], gu_ps[1][:], ALU.mult).then_inc(product, 1)
                    dve.wait_ge(gated, 2 * n + 2)
                    nc.vector.tensor_tensor(h[1][0:IR], h[1][64:64 + IR], gu_ps[2][64:64 + IR], ALU.mult).then_inc(product, 1)
                    attend(4)
                    if not first:
                        add(n - 1, before, 0)
                    attend(5)
                    if not (last and t == B - 1):
                        weight(n + 1, e + (t + 1) // B, (t + 1) % B)
                    attend(6)
                    if not first:
                        add(n - 1, before, 1)
                    attend(7)
                    if t % 2 == 1 and ahead:
                        split_max(quad + 1)

                for x in range(NBLOCK):
                    maximum(0, x)
                split_max(0)
                walk(dve, step)
                weight2(last_step, 1)
                add(last_step, B - 1, 0)
                add(last_step, B - 1, 1)
                copy_y(NQUAD - 1)

            @block.scalar
            def _(act):
                def round_h(n, c, rows):
                    act.wait_ge(scaled, 2 * n + c + 1)
                    reached(act, out_done, 2 * n)
                    nc.scalar.activation(h_hi[c][rows], h[c][rows], ACT.Copy).then_inc(h_rounded, 1)

                def round_low2(n):
                    act.wait_ge(weighted2, n + 1)
                    nc.scalar.activation(h_hi[1][IRP:P], low2[IRP:P], ACT.Copy).then_inc(low2_rounded, 1)

                def step(e, t, ws, first, last):
                    n, q, pair = 8 * e + t, t // 2, t % 2
                    quad = 4 * e + q

                    def attend(i):
                        if i not in GROUP_AT[pair]:
                            return
                        j = GROUP_AT[pair].index(i)
                        if j == 0 and pair == 0:
                            reached(act, mixed, quad)
                        act.wait_ge(scored, NGROUP * n + j + 1)
                        if j < 4:
                            o = prob[:, 2 * pair + j // 2, (j % 2) * TT:(j % 2 + 1) * TT]
                            nc.scalar.activation(o, s_ps[:], ACT.Exp, scale=SCALE).then_inc(exped, 1)
                        else:
                            o = prob[:, 2 * pair:2 * pair + 2, 1024:P_W]
                            nc.scalar.activation(o, s_ps[:].rearrange("p (h t) -> p h t", h=2), ACT.Exp, scale=SCALE).then_inc(exped, 1)

                    act.wait_ge(weighted, n + 1)
                    nc.scalar.activation(low_hi[:], low[:], ACT.Copy).then_inc(low_rounded, 1)
                    if not first:
                        round_h(n - 1, *HALVES[0])
                    attend(0)
                    if not first:
                        round_h(n - 1, *HALVES[1])
                    attend(1)
                    attend(2)
                    if not first:
                        round_low2(n - 1)
                    attend(3)
                    act.wait_ge(gu_done, 3 * n + 1)
                    reached(act, h_ready, 2 * n)
                    nc.scalar.activation(h[0][:], gu_ps[0][:], ACT.Silu).then_inc(gated, 1)
                    act.wait_ge(gu_done, 3 * n + 3)
                    reached(act, low2_ready, n)
                    nc.scalar.activation(h[1][64:64 + IR], gu_ps[2][0:IR], ACT.Silu).then_inc(gated, 1)
                    for i in range(4, 8):
                        attend(i)
                walk(act, step)
                for half in HALVES:
                    round_h(last_step, *half)
                round_low2(last_step)

            @block.gpsimd
            def _(pool):
                def rest_h(n):
                    for c, rows in HALVES:
                        pool.wait_ge(h_rounded, 2 * n + c + 1)
                        nc.gpsimd.tensor_tensor(h_lo[c][rows], h[c][rows], h_hi[c][rows].bitcast(F32), ALU.subtract).then_inc(h_ready, 1)

                def mask(n, pair):
                    wait_first(pool, passed, exped, NGROUP * n + NGROUP)
                    for i in range(BLK):
                        v = prob[:, 2 * pair:2 * pair + 2, P_OFF[i]:P_OFF[i] + P]
                        nc.gpsimd.affine_select(out=v, in_=v, compare_op=ALU.is_ge, fill=0.0, base=0,
                                                pattern=[[0, 2], [1, P]], channel_multiplier=-1).then_inc(masked, 1)

                def step(e, t, ws, first, last):
                    n = 8 * e + t
                    if not first:
                        rest_h(n - 1)
                    if t % 2 == 1:
                        mask(n - 1, 0)
                    for c, rows in HALVES:
                        pool.wait_ge(product, 2 * n + c + 1)
                        if c == 0:
                            pool.wait_ge(srep_in, 16 * n + 16)
                        nc.gpsimd.tensor_tensor(h[c][rows], h[c][rows], srep[rows], ALU.mult).then_inc(scaled, 1)
                    if t % 2 == 1:
                        mask(n, 1)
                    if t == 0 and not last:
                        reached(pool, out_done, 2 * n)
                        pool.dma_start(w[1 - ws][:].bitcast(F32), g["wall"][ds(e + 1, 1)].rearrange("o p n -> (o p) n")).then_inc(w_in[1 - ws], 16)
                pool.dma_start(w[0][:].bitcast(F32), g["wall"][0]).then_inc(w_in[0], 16)
                walk(pool, step)
                rest_h(last_step)

            @block.tensor
            def _(pe):
                def from_x(out, m, t, ws, stop):
                    tok = slice(t * TT, (t + 1) * TT)
                    for c in range(KC):
                        three_passes(nc, out, w[ws][:, WXS(c, m)], w[ws][:, lo(WXS(c, m))], g["x_hi"][:, c, tok], g["x_lo"][:, c, tok], c == 0, False)
                    return nc.tensor.matmul(out, w[ws][:, CATS(m)], cat[:], start=False, stop=stop)

                def low_rank(n, t, ws):
                    pe.wait_ge(cat_in, 16 * n + 16)
                    reached(pe, weighted2, n - 1)
                    from_x(low_ps[:], 0, t, ws, True).then_inc(low_done, 1)

                def low_rank2(n, ws, weights_out):
                    pe.wait_ge(h_ready, 2 * n + 2)
                    pe.wait_ge(weighted, weights_out)
                    for c in range(2):
                        last = three_passes(nc, low_ps[:], w[ws][:, WDS(c, 0)], w[ws][:, lo(WDS(c, 0))], h_hi[c][:], h_lo[c][:], c == 0, c == 1)
                    last.then_inc(low2_done, 1)

                def out(n, ws, m):
                    reached(pe, added, 2 * n + m)
                    three_passes(nc, out_ps[:], w[ws][:, WDS(0, 1 + m)], w[ws][:, lo(WDS(0, 1 + m))], h_hi[0][:], h_lo[0][:], True, False)
                    pe.wait_ge(low2_ready, n + 1)
                    three_passes(nc, out_ps[:], w[ws][:, WDS(1, 1 + m)], w[ws][:, lo(WDS(1, 1 + m))], h_hi[1][:], h_lo[1][:],
                                 False, True).then_inc(out_done, 1)

                def row_scores(quad, slot, x):
                    hd, blk = x // BLK, x % BLK
                    reached(pe, maxed, NBLOCK * quad + x)
                    nc.tensor.matmul(ma_ps[:, 0:(blk + 1) * P], q_st[slot][0:KS, hd, blk * P:(blk + 1) * P],
                                     k_st[slot][0:KS, hd, 0:(blk + 1) * P], start=True, stop=True).then_inc(row_scored, 1)

                def turn_max(quad):
                    wait_first(pe, passed, m_part, 4 * quad + 4)
                    nc.tensor.transpose(m_turned_out, mparts[:].rearrange("p j n -> p (j n)"), g["ident_bf"][:]).then_inc(m_turned, 1)

                def key_scores(n, slot, pair, j):
                    reached(pe, exped, NGROUP * n + j)
                    for hd, i, at in ([(j // 2, 0, 0)], [(j // 2, 1, 0), (j // 2, 3, 384)], [(j // 2, 0, 0)], [(j // 2, 1, 0), (j // 2, 3, 384)],
                                      [(0, 2, 0), (1, 2, 256)])[j]:
                        hd += 2 * pair
                        last = nc.tensor.matmul(s_ps[:, at:at + TT - i * P], k_st[slot][0:KM, hd, i * P:(i + 1) * P],
                                                q_st[slot][0:KM, hd, i * P:TT], start=True, stop=True)
                    last.then_inc(scored, 1)

                def mix(quad):
                    pe.wait_ge(masked, 8 * quad + 8)
                    pe.wait_ge(v_in, 16 * quad + 16)
                    reached(pe, y_copied, quad)
                    for i in range(BLK):
                        for hd in range(HQ):
                            last = nc.tensor.matmul(y_ps[32 * hd:32 * hd + 32, i * P:TT], v_st[:, i, 32 * hd:32 * hd + 32],
                                                    prob[:, hd, P_OFF[i]:P_OFF[i] + TT - i * P], start=(i == 0), stop=(i == BLK - 1))
                    last.then_inc(mixed, 1)

                def step(e, t, ws, first, last):
                    n, q, pair = 8 * e + t, t // 2, t % 2
                    quad = 4 * e + q
                    wp = 1 - ws if t == 0 else ws
                    ahead = not (last and q == NQ - 1)

                    def attend(i):
                        if i == 0 and pair == 0:
                            turn_max(quad)
                        if i == 1 and pair == 0 and not first:
                            mix(quad - 1)
                        if ahead:
                            if i == 0 and pair == 0:
                                pe.wait_ge(qk_in[(q + 1) % 2], NLOAD * (2 * e + (q + 1) // 2 + 1))
                                pe.wait_ge(m_copied, quad + 1)
                            row_scores(quad + 1, (q + 1) % 2, 8 * pair + i)
                        if i in GROUP_AT[pair]:
                            j = GROUP_AT[pair].index(i)
                            if pair == 0 and j == 0:
                                pe.wait_ge(m_in, 16 * quad + 16)
                            key_scores(n, q % 2, pair, j)

                    if first:
                        pe.wait_ge(w_in[0], 16)
                        low_rank(0, 0, 0)
                    for m in range(3):
                        reached(pe, *((gated, 2 * n - 1), (product, 2 * n - 1), (product, 2 * n))[m])
                        from_x(gu_ps[m][:], m + 1, t, ws, False)
                        attend(m)
                    if not first:
                        low_rank2(n - 1, wp, n + 1)
                    attend(3)
                    pe.wait_ge(low_ready, n + 1)
                    for m in range(3):
                        three_passes(nc, gu_ps[m][:], w[ws][:, WSS(m)], w[ws][:, lo(WSS(m))], low_hi[:], low_lo[:], False, True).then_inc(gu_done, 1)
                    attend(4)
                    if not first:
                        out(n - 1, wp, 0)
                    attend(5)
                    if t < B - 1:
                        low_rank(n + 1, t + 1, ws)
                    elif not last:
                        pe.wait_ge(w_in[1 - ws], 8 * e + (16 if ws == 0 else 24))
                        low_rank(n + 1, 0, 1 - ws)
                    attend(6)
                    if not first:
                        out(n - 1, wp, 1)
                    attend(7)

                pe.wait_ge(qk_in[0], NLOAD)
                for x in range(NBLOCK):
                    row_scores(0, 0, x)
                walk(pe, step)
                mix(NQUAD - 1)
                low_rank2(last_step, 1, last_step + 1)
                out(last_step, 1, 0)
                out(last_step, 1, 1)


def project_out(nc, a, g):
    with ExitStack() as ctx:
        sb = lambda n, s, d: ctx.enter_context(nc.sbuf_tensor(n, s, d))
        psum = lambda n, s, d: ctx.enter_context(nc.psum_tensor(n, s, d))
        sem = lambda n: ctx.enter_context(nc.semaphore(n))
        wo = [sb(f"wo{s}", [P, SO], F32R) for s in range(2)]
        den = sb("sums", [P, B, H * TT // P], F32)
        yp = [sb(f"y_packed{s}", [P, KC, TT], F32) for s in range(2)]
        rden = [sb(f"sums_rep{s}", [P, KC, TT], F32) for s in range(2)]
        yn_hi = [sb(f"yn_hi{s}", [P, KC, TT], F32R) for s in range(2)]
        yn_lo = [sb(f"yn_lo{s}", [P, KC, TT], F32R) for s in range(2)]
        out_ps = [psum(f"attn_out{s}", [P, KC, TT], F32) for s in range(2)]
        wo_in, den_in, r_kept, inverted = map(sem, "wo_in sums_in r_kept sums_inverted".split())
        y_in = [sem(f"y_in{s}") for s in range(2)]
        normed, yn_rounded, yn_ready, projected, added, stored = map(
            sem, "y_normed yn_rounded yn_ready projected o_added o_stored".split())
        WO = lambda c, m: slice(c * C + m * P, c * C + (m + 1) * P)
        n_den = H * TT // P
        with nc.Block() as block:
            @block.sync
            def _(sp):
                for t in range(B):
                    sp.dma_start(den[:, t], g["y_heads"][t, :, D].rearrange("h (k n) -> h k n", n=n_den)).then_inc(den_in, 16)
                for half in range(2):
                    sp.dma_start(wo[half][:].bitcast(F32), g["sh_scr"][:, half * SALL + SG + SD:(half + 1) * SALL]).then_inc(wo_in, 16)
                sp.wait_ge(inverted, 1)
                sp.dma_start(g["r_scr"].rearrange("b h (k n) -> (h k) b n", n=n_den), den[:]).then_inc(r_kept, 16)
                sp.wait_ge(r_kept, 16)
                for t in range(B):
                    s = t % 2
                    if t >= 2:
                        sp.wait_ge(yn_ready, t - 1)
                    for c in range(KC):
                        sp.dma_start(yp[s][:, c], g["y_heads"][t, c * 8:c * 8 + 8, 0:D]).then_inc(y_in[s], 16)
                        sp.dma_start(rden[s][:, c], g["r_scr"][t, c * 8:c * 8 + 8].unsqueeze(1).broadcast_to([8, D, TT])).then_inc(y_in[s], 16)

            @block.gpsimd
            def _(pool):
                for t in range(B):
                    pool.wait_ge(added, 2 * t + 2)
                    tok = slice(t * TT, (t + 1) * TT)
                    pool.dma_start(g["out"].rearrange("(c p) t -> p c t", p=P)[:, :, tok], g["y"][:, :, tok]).then_inc(stored, 16)
                pool.wait_ge(stored, 16 * B)

            @block.vector
            def _(dve):
                def norm(t):
                    s = t % 2
                    dve.wait_ge(y_in[s], 64 * (t // 2 + 1))
                    nc.vector.tensor_tensor(yp[s][:], yp[s][:], rden[s][:], ALU.mult).then_inc(normed, 1)

                def rest(t):
                    s = t % 2
                    dve.wait_ge(yn_rounded, t + 1)
                    nc.vector.tensor_tensor(yn_lo[s][:], yp[s][:], yn_hi[s][:].bitcast(F32), ALU.subtract).then_inc(yn_ready, 1)

                def add(t):
                    s = t % 2
                    dve.wait_ge(projected, t + 1)
                    for c in range(KC):
                        v = g["y"][:, c, t * TT:(t + 1) * TT]
                        nc.vector.scalar_tensor_tensor(v, out_ps[s][:, c], g["bias"][:, GW + c:GW + c + 1], v, ALU.add, ALU.add).then_inc(added, 1)

                dve.wait_ge(den_in, 16 * B)
                nc.vector.reciprocal(den[:], den[:]).then_inc(inverted, 1)
                for t in range(B):
                    norm(t)
                    rest(t)
                    if t >= 1:
                        add(t - 1)
                add(B - 1)

            @block.scalar
            def _(act):
                for t in range(B):
                    s = t % 2
                    act.wait_ge(normed, t + 1)
                    if t >= 2:
                        act.wait_ge(projected, t - 1)
                    nc.scalar.activation(yn_hi[s][:], yp[s][:], ACT.Copy).then_inc(yn_rounded, 1)

            @block.tensor
            def _(pe):
                pe.wait_ge(wo_in, 32)
                for t in range(B):
                    s = t % 2
                    pe.wait_ge(yn_ready, t + 1)
                    if t >= 2:
                        pe.wait_ge(added, 2 * t - 2)
                    for m in range(KC):
                        for c in range(KC):
                            last = three_passes(nc, out_ps[s][:, m], wo[0][:, WO(c, m)], wo[1][:, WO(c, m)],
                                                yn_hi[s][:, c], yn_lo[s][:, c], c == 0, c == KC - 1)
                    last.then_inc(projected, 1)


def build(nc, a, out):
    g = {"out": out}
    scratch = lambda n, s, d: nc.dram_tensor(n, s, d, kind="Internal").ap()
    g["wall"] = scratch("wall_scr", [F, P, WALL], F32)
    g["sh_scr"] = scratch("sh_scr", [P, 2 * SALL], F32)
    g["qk_scr"] = scratch("qk_scr", [4, 3, P, T], BF16)
    g["v_scr"] = scratch("v_scr", [B, P, BLK * H * 32], F32)
    g["y_scr"] = scratch("y_scr", [B, NQ, P, TT], F32)
    g["y_heads"] = g["y_scr"].rearrange("b q (h d) t -> b (q h) d t", d=32)
    g["r_scr"] = scratch("r_scr", [B, H, TT], F32)
    g["sw_scr"] = scratch("sw_scr", [SW, T], F32)
    g["cat_scr"] = scratch("cat_scr", [F, 3 * K, T], F32)
    with ExitStack() as ctx:
        sb = lambda n, s, d: ctx.enter_context(nc.sbuf_tensor(n, s, d))
        for n, s, d in (("y", [P, KC, T], F32), ("x_hi", [P, KC, T], F32R), ("x_lo", [P, KC, T], F32R),
                        ("bias", [P, GW + KC], F32), ("ident_bf", [P, P], BF16), ("causal_bf", [P, TT], BF16)):
            g[n] = sb(n, s, d)
        with ExitStack() as before_attention:
            sba = lambda n, s, d: before_attention.enter_context(nc.sbuf_tensor(n, s, d))
            for n, s, d in (("logits", [P, NBLK, E], F32), ("ident", [P, P], F32), ("cat_sign", [P, 1], F32), ("entry", [P, 1], F32)):
                g[n] = sba(n, s, d)
            g["consts"] = [(g[n][:], a[n]) for n in ("bias", "ident", "cat_sign", "entry")]
            with ExitStack() as for_projection:
                sbp = lambda n, s, d: for_projection.enter_context(nc.sbuf_tensor(n, s, d))
                g["pw_hi"], g["pw_lo"] = sbp("pw_hi", [P, PW], F32R), sbp("pw_lo", [P, PW], F32R)
                prepare(nc, a, g)
                project(nc, a, g)
            route(nc, a, g)
        share(nc, a, g)
        experts(nc, a, g)
        project_out(nc, a, g)


def lay_out(inputs):
    k = {n.replace("L0_attn_", "at_").replace("L0_ffn_", ""): np.asarray(v) for n, v in inputs.items()}
    z = lambda *s: np.zeros(s, np.float32)
    chunks = lambda m: m.reshape(-1, P, m.shape[1]).transpose(1, 0, 2)
    heads = lambda m: m.transpose(1, 0, 2).reshape(C, H * D)
    pad = lambda m, cols: np.concatenate([m, z(m.shape[0], cols - m.shape[1])], 1)
    o = {"x": k["at_x"], "x_t": k["at_x"].reshape(T, C).T}
    groups = [pad(k["gate_weight"].T, P)]
    bias = [z(P)]
    for n in ("v", "q", "k"):
        m, b = heads(k["at_W" + n]), k["at_b" + n].reshape(H * D)
        groups += [m[:, c * P:(c + 1) * P] for c in range(2)]
        bias += [b[c * P:(c + 1) * P] for c in range(2)]
    o["pw"] = chunks(np.concatenate(groups, 1)).reshape(P, PW)
    bias += [k["at_bo"][c * P:(c + 1) * P] for c in range(KC)]
    o["bias"] = np.stack(bias, 1)
    pairs = []
    for i in range(3):
        pairs += [pad(k[n][i * P:(i + 1) * P].T, P) for n in ("sh_gate_W", "sh_up_W")]
    down = np.concatenate([k["sh_down_W"].T, z(3 * P - 2 * I, C)], 0)
    o["shared"] = np.concatenate([chunks(np.concatenate(pairs, 1)).reshape(P, SG), chunks(down).reshape(P, SD),
                                  chunks(k["at_Wo"]).reshape(P, SO)], 1)
    o["inv"] = k["inv_mapping"].reshape(1, E)
    third = lambda gate, up: np.concatenate([pad(gate, 64), pad(up, 64)], 1)
    ex, sc = [], []
    for f in range(F):
        gw, uw = k["gate_W"][f].T, k["up_W"][f].T
        low = np.concatenate([k["gate_qa"][f].reshape(K * R, C).T, k["up_qa"][f].reshape(K * R, C).T], 1)
        wx = chunks(np.concatenate([low, gw[:, :P], uw[:, :P], third(gw[:, P:], uw[:, P:])], 1)).reshape(P, WX)
        qb = [k[n][f].transpose(0, 2, 1).reshape(K * R, -1) for n in ("gate_qb", "up_qb", "down_qb")]
        ws = np.concatenate([
            np.concatenate([qb[0][:, :P], z(64, P), third(qb[0][:, P:], z(64, IR))], 1),
            np.concatenate([z(64, P), qb[1][:, :P], third(z(64, IR), qb[1][:, P:])], 1)], 0)
        dw, da = k["down_W"][f].T, k["down_qa"][f].reshape(K * R, I).T
        inner = np.concatenate([z(I, 64), da, dw], 1)
        wd = np.concatenate([inner, z(64 - IR, 3 * P), np.concatenate([z(64, P), qb[2]], 1)], 0)
        mu = k["mask_up_W"][f]
        spread = np.concatenate([mu, mu, mu, z(C, P - 3 * K)], 1)
        ex.append(np.concatenate([wx, ws, chunks(wd).reshape(P, WD), chunks(spread).reshape(P, WM)], 1))
        gs, us = k["gate_scale"][f][None], k["up_scale"][f][None]
        sc.append(np.concatenate([gs[:, :P], us[:, :P], third(gs[:, P:], us[:, P:]), k["down_scale"][f][None]], 1)[0])
    o["experts"], o["scales"] = np.stack(ex), np.stack(sc)
    o["ident"] = np.eye(P, dtype=np.float32)
    causal = z(P, TT)
    causal[:, TT - P:][np.triu_indices(P, 1)] = NEG
    o["causal"] = causal
    sign = z(P, 1)
    sign[2 * K:3 * K] = -1.0
    o["cat_sign"] = sign
    o["entry"] = np.arange(P, dtype=np.float32)[:, None]
    return {n: np.ascontiguousarray(v) for n, v in o.items()}


def kernel(**inputs):
    import concourse.bacc as bacc
    from concourse.bass_utils import run_bass_kernel_spmd

    nc = bacc.Bacc("TRN2", target_bir_lowering=False, num_devices=1)
    arrays = lay_out(inputs)
    a = {n: nc.dram_tensor("in_" + n, v.shape, mybir.dt.from_np(v.dtype), kind="ExternalInput").ap() for n, v in arrays.items()}
    out = nc.dram_tensor("out_t", (C, T), F32, kind="ExternalOutput").ap()
    build(nc, a, out)
    r = run_bass_kernel_spmd(nc, [{"in_" + n: v for n, v in arrays.items()}], core_ids=[0])
    return np.ascontiguousarray(r.results[0]["out_t"].T).reshape(B, TT, C)
```

```python
from contextlib import ExitStack

import numpy as np
import concourse.bass as bass
from concourse import mybir

F32 = mybir.dt.float32
F32R = mybir.dt.float32r
BF16 = mybir.dt.bfloat16
I32 = mybir.dt.int32
ALU = mybir.AluOpType
ACT = mybir.ActivationFunctionType
AX = mybir.AxisListType.X
ds = bass.ds

P = 128
C = 256
KC = C // P
B, TT = 8, 512
T = B * TT
BLK = TT // P
NBLK = T // P
H, D = 16, 16
HQ = 4
NQ = H // HQ
NQUAD = B * NQ
E, F, K, R, TOPK = 64, 8, 8, 8, 6
I = 176
IR = I - P
GW = 7
EPS = 1e-5
SCALE = float(D) ** -0.5
NEG = -3e38

WX = KC * 4 * P
WS = 4 * P
WD = 2 * 3 * P
WE = WX + WS + WD
WM = KC * P
SL = WE + WX
WALL = 2 * WE + P
SW = E + F
SG = KC * 6 * P
SD = 3 * C
SO = KC * C
SALL = SG + SD + SO
PW = KC * GW * P

PIECES = [slice(0, 4 * P), slice(4 * P, WX), slice(WX, WX + WS), slice(WX + WS, WX + WS + 3 * P), slice(WX + WS + 3 * P, WE)]
NP = len(PIECES)

Q_RUNS = [(0, 0, 3), (3, 1, 2), (5, 2, 1)]
K_RUNS = [(0, 0, 3), (3, 0, 2), (5, 0, 1)]
KS = 6 * D
KM = KS + 3
P_OFF = [0, TT, 1024, 896]
P_W = 1280
N_SUMS = H * TT // P


def wait_first(eng, passed, sem, value):
    eng.wait_ge(sem, value)
    eng.sem_inc(passed, 1)


def three_passes(nc, out, w_hi, w_lo, x_hi, x_lo, start, stop):
    nc.tensor.matmul(out, w_hi, x_hi, start=start, stop=False)
    nc.tensor.matmul(out, w_hi, x_lo, start=False, stop=False)
    return nc.tensor.matmul(out, w_lo, x_hi, start=False, stop=stop)



def fetch_qk(sp, g, b, q):
    s = q % 2
    for st, j, runs in ((g["q_st"], 0, Q_RUNS), (g["k_st"], 1, K_RUNS)):
        for slots, part, count in runs:
            src = g["qk_scr"][ds(b, 1), q, j, part:part + (1 if j == 0 else count)]
            if j == 0:
                src = src.rearrange("o s (d h) t -> (o s) d (h t)", h=HQ).broadcast_to([count, D, HQ * TT])
            else:
                src = src.rearrange("o s (d h) t -> (o s d) (h t)", h=HQ)
            sp.dma_start(st[s][slots * D:(slots + count) * D].rearrange("p h t -> p (h t)"), src).then_inc(g["qk_in"][s], 16)


def fetch_piece(sp, a, g, f, p):
    src = a["experts"][ds(f, 1), :, PIECES[p]].rearrange("e p n -> (e p) n")
    sp.dma_start(g["raw"][p % 2][:, 0:src.shape[1]], src).then_inc(g["raw_in"][p % 2], 16)


def fetch_mask(sp, a, g, f):
    sp.dma_start(g["aux"][:, 0:WM], a["experts"][ds(f, 1), :, WE:WE + WM].rearrange("e p n -> (e p) n")).then_inc(g["aux_in"], 16)


def project(nc, a, g):
    with ExitStack() as ctx:
        sb = lambda n, s, d: ctx.enter_context(nc.sbuf_tensor(n, s, d))
        psum = lambda n, s, d: ctx.enter_context(nc.psum_tensor(n, s, d))
        sem = lambda n: ctx.enter_context(nc.semaphore(n))
        xin = [sb(f"xin{s}", [P, BLK, C], F32) for s in range(2)]
        stat = [sb(f"stat{s}", [P, BLK, 6], F32) for s in range(2)]
        mv = [sb(f"mv{s}", [P, BLK, 2], F32) for s in range(2)]
        std = [sb(f"std{s}", [P, BLK], F32) for s in range(2)]
        rstd = [sb(f"rstd{s}", [P, BLK], F32) for s in range(2)]
        pw, causal = g["y"][:, 0, 0:PW], g["y"][:, 1, 0:TT]
        pw_hi, pw_lo = sb("pw_hi", [P, PW], F32R), sb("pw_lo", [P, PW], F32R)
        lgt = sb("logits_t", [E, TT], F32)
        vf = [sb(f"v_f{c}", [P, TT], F32) for c in range(2)]
        vt = [sb(f"v_tok{s}", [P, BLK, H, 32], F32) for s in range(2)]
        place = [st[s][:].rearrange("p h t -> p (h t)").bitcast(F32) for st in (g["q_st"], g["k_st"]) for s in range(2)]
        qf, rest = [v[:, 0:TT] for v in place], [v[:, TT:2 * TT] for v in place]
        qs = [sb(f"qk_split{s}", [P, 4, 3, TT], BF16) for s in range(2)]
        tp = psum("x_turned_ps", [P, KC, TT], F32)
        gp = [psum(f"group_ps{j}", [P, TT], F32) for j in range(4)]
        lp = psum("logits_ps", [P, BLK, E], F32)
        vp = psum("v_ps", [P, BLK, P], F32)
        x_in = [sem(f"x_in{s}") for s in range(2)]
        ident_in = sem("ident_in")
        PW_PARTS = [slice(0, 3 * C), slice(3 * C, PW)]
        pw_in, const_in, pw_rounded, pw_split = map(sem, "pw_in const_in pw_rounded pw_split".split())
        qkv_kept = [sem(f"qkv_kept{s}") for s in range(2)]
        stats, aggregated, eps_added, root, rooted, normed = map(sem, "stats aggregated eps_added root rooted normed".split())
        turned, x_rounded, x_rest = map(sem, "x_turned x_rounded x_rest".split())
        groups, evacuated = sem("groups_done"), sem("groups_evacuated")
        logits_turned, logits_kept, v_turned, v_kept = map(sem, "logits_turned logits_kept v_turned v_kept".split())
        rest1, part2, part3 = map(sem, "qk_rest1 qk_part2 qk_part3".split())
        passed = sem("passed")
        QKV = 9 * 16
        EV, EV_TILE = [1, 2, 3, 5, 7, 9, 11], 11
        with nc.Block() as block:
            @block.sync
            def _(sp):
                for s in range(2):
                    sp.sem_inc(qkv_kept[s], QKV)
                sp.sem_inc(x_rest, 1)
                sp.sem_inc(evacuated, EV_TILE)
                sp.sem_inc(logits_turned, 1)
                sp.sem_inc(logits_kept, 1)
                sp.sem_inc(v_turned, 2)
                sp.sem_inc(v_kept, 1)
                sp.sem_inc(rest1, 4)
                sp.sem_inc(part3, 4)
                sp.dma_start(xin[0][:], a["x"][0].rearrange("(b p) c -> p b c", p=P)).then_inc(x_in[0], 16)
                sp.dma_start(g["ident"][:], a["ident"]).then_inc(ident_in, 16)
                for cols in PW_PARTS:
                    sp.dma_start(pw[:, cols], a["pw"][:, cols]).then_inc(pw_in, 16)
                for dst, src in g["consts"] + [(causal, a["causal"])]:
                    sp.dma_start(dst, src).then_inc(const_in, 16)
                sp.dma_start(xin[1][:], a["x"][1].rearrange("(b p) c -> p b c", p=P)).then_inc(x_in[1], 16)
                sp.dma_start(g["shared"], a["shared"][:, 0:SG + SD]).then_inc(g["shared_in"], 16)

                def tile(t, s, more):
                    if more:
                        sp.wait_ge(turned, t + 1)
                        sp.dma_start(xin[s][:], a["x"][ds(t + 2, 1)].rearrange("o (b p) c -> p (o b) c", p=P)).then_inc(x_in[s], 16)
                    sp.wait_ge(v_kept, 2 * t + 3)
                    sp.dma_start(g["v_scr"][ds(t, 1)].rearrange("b p n -> (b p) n"), vt[s][:].rearrange("p b h d -> p (b h d)")).then_inc(qkv_kept[s], 16)
                    for j in range(4):
                        wait_first(sp, passed, part3, 4 * t + j + 5)
                        for half in range(2):
                            rows = slice(half * HQ * D, (half + 1) * HQ * D)
                            dst = g["qk_scr"][ds(t, 1), 2 * (j % 2) + half, j // 2].rearrange("o s p t -> (o p) s t")
                            sp.dma_start(dst, qs[s][rows, j]).then_inc(qkv_kept[s], 16)

                with sp.Fori(0, B // 2 - 1) as i:
                    for s in range(2):
                        tile(2 * i + s, s, True)
                for s in range(2):
                    tile(B - 2 + s, s, False)
                for s in range(2):
                    sp.wait_ge(qkv_kept[s], QKV * (B // 2 + 1))

            @block.vector
            def _(dve):
                for s in range(2):
                    nc.vector.memset(vt[s][:, :, :, D:D + 1], 1.0)
                    nc.vector.memset(vt[s][:, :, :, D + 1:32], 0.0)

                def norm(t, i, s):
                    dve.wait_ge(x_in[s], 16 * i + 16)
                    for b in range(BLK):
                        nc.vector.bn_stats(stat[s][:, b], xin[s][:, b]).then_inc(stats, 1)
                    for b in range(BLK):
                        wait_first(dve, passed, stats, BLK * t + b + 1)
                        nc.vector.bn_aggr(mv[s][:, b], stat[s][:, b]).then_inc(aggregated, 1)
                    dve.wait_ge(aggregated, BLK * t + BLK)
                    nc.vector.tensor_scalar_add(std[s][:], mv[s][:, :, 1], EPS).then_inc(eps_added, 1)
                    dve.wait_ge(root, t + 1)
                    nc.vector.reciprocal(rstd[s][:], std[s][:]).then_inc(rooted, 1)
                    dve.wait_ge(rooted, t + 1)
                    for b in range(BLK):
                        last = nc.vector.tensor_scalar(xin[s][:, b], xin[s][:, b], mv[s][:, b, 0:1], rstd[s][:, b:b + 1],
                                                       ALU.subtract, ALU.mult)
                    last.then_inc(normed, 1)

                def x_low(t, s):
                    dve.wait_ge(x_rounded, t + 1)
                    tok = ds(t * TT, TT)
                    nc.vector.tensor_tensor(g["x_lo"][:, :, tok], tp[:], g["x_hi"][:, :, tok].bitcast(F32), ALU.subtract).then_inc(x_rest, 1)

                def split(t, s, j):
                    dve.wait_ge(evacuated, EV_TILE * t + EV_TILE + EV[3 + j])
                    dve.wait_ge(part3, 4 * t + j + 1)
                    nc.vector.tensor_tensor(rest[j], qf[j], qs[s][:, j, 0], ALU.subtract).then_inc(rest1, 1)
                    dve.wait_ge(rest1, 4 * t + j + 5)
                    nc.vector.tensor_copy(qs[s][:, j, 1], rest[j]).then_inc(part2, 1)

                def tile(t, i, s, more):
                    if more:
                        norm(t + 1, i + s, 1 - s)
                    dve.wait_ge(logits_turned, t + 2)
                    nc.vector.tensor_copy(g["logits"][:, ds(t * BLK, BLK), :], lp[:]).then_inc(logits_kept, 1)
                    dve.wait_ge(qkv_kept[s], QKV * i + QKV)
                    for c in range(2):
                        dve.wait_ge(v_turned, 2 * t + c + 3)
                        nc.vector.tensor_copy(vt[s][:, :, 8 * c:8 * c + 8, 0:D],
                                              vp[:].rearrange("p b (h d) -> p b h d", d=D)).then_inc(v_kept, 1)
                    split(t, s, 0)
                    split(t, s, 1)
                    if more:
                        x_low(t + 1, 1 - s)
                    split(t, s, 2)
                    split(t, s, 3)

                def split_weights(part):
                    cols = PW_PARTS[part]
                    dve.wait_ge(pw_rounded, part + 1)
                    nc.vector.tensor_tensor(pw_lo[:, cols], pw[:, cols], pw_hi[:, cols].bitcast(F32), ALU.subtract).then_inc(pw_split, 1)

                norm(0, 0, 0)
                split_weights(0)
                x_low(0, 0)
                split_weights(1)
                dve.wait_ge(ident_in, 16)
                nc.vector.tensor_copy(g["ident_bf"][:], g["ident"][:])
                dve.wait_ge(const_in, 16 * len(g["consts"]) + 16)
                nc.vector.tensor_copy(g["causal_bf"][:], causal)
                with dve.Fori(0, B // 2 - 1) as i:
                    for s in range(2):
                        tile(2 * i + s, i, s, True)
                for s in range(2):
                    tile(B - 2 + s, B // 2 - 1, s, s == 0)

            @block.gpsimd
            def _(pool):
                with pool.Fori(0, B // 2) as i:
                    for s in range(2):
                        for j in range(4):
                            pool.wait_ge(part2, 8 * i + 4 * s + j + 1)
                            nc.gpsimd.tensor_tensor(qs[s][:, j, 2], rest[j], qs[s][:, j, 1], ALU.subtract).then_inc(part3, 1)

            @block.scalar
            def _(act):
                def x_high(t, i, s):
                    wait_first(act, passed, turned, t + 1)
                    nc.scalar.activation(g["x_hi"][:, :, ds(t * TT, TT)], tp[:], ACT.Copy).then_inc(x_rounded, 1)

                def take_root(t, s):
                    act.wait_ge(eps_added, t + 1)
                    nc.scalar.activation(std[s][:], std[s][:], ACT.Sqrt).then_inc(root, 1)

                def evacuate(t, i, s, n):
                    act.wait_ge(groups, GW * t + n + 1)
                    bank = gp[n % 4]
                    if n == 0:
                        act.wait_ge(logits_turned, t + 1)
                        nc.scalar.activation(lgt[:], bank[0:E], ACT.Copy).then_inc(evacuated, 1)
                    elif n <= 2:
                        act.wait_ge(v_turned, 2 * t + n)
                        nc.scalar.activation(vf[n - 1][:], bank[:], ACT.Identity, bias=g["bias"][:, n:n + 1]).then_inc(evacuated, 1)
                    else:
                        j = n - 3
                        act.wait_ge(rest1, 4 * t + j + 1)
                        act.wait_ge(qkv_kept[s], QKV * i + QKV)
                        nc.scalar.activation(qf[j], bank[:], ACT.Identity, bias=g["bias"][:, n:n + 1]).then_inc(evacuated, 1)
                        nc.scalar.activation(qs[s][:, j, 0], bank[:], ACT.Identity, bias=g["bias"][:, n:n + 1]).then_inc(evacuated, 1)

                def tile(t, i, s, more):
                    if more:
                        take_root(t + 1, 1 - s)
                    for n in range(5):
                        evacuate(t, i, s, n)
                    if more:
                        x_high(t + 1, i + s, 1 - s)
                    for n in range(5, GW):
                        evacuate(t, i, s, n)

                def round_weights(part):
                    cols = PW_PARTS[part]
                    nc.scalar.activation(pw_hi[:, cols], pw[:, cols], ACT.Copy).then_inc(pw_rounded, 1)

                take_root(0, 0)
                act.wait_ge(pw_in, 16 * len(PW_PARTS))
                round_weights(0)
                x_high(0, 0, 0)
                round_weights(1)
                act.wait_ge(const_in, 16 * len(g["consts"]) + 16)
                with act.Fori(0, B // 2 - 1) as i:
                    for s in range(2):
                        tile(2 * i + s, i, s, True)
                for s in range(2):
                    tile(B - 2 + s, B // 2 - 1, s, s == 0)

            @block.tensor
            def _(pe):
                def turn_x(t, s):
                    pe.wait_ge(normed, t + 1)
                    pe.wait_ge(x_rest, t + 1)
                    for c in range(KC):
                        for b in range(BLK):
                            last = nc.tensor.transpose(tp[:, c, b * P:(b + 1) * P], xin[s][:, b, c * P:(c + 1) * P], g["ident"][:])
                    last.then_inc(turned, 1)

                def group(t, s, n):
                    before = EV[n - 4] + EV_TILE if n >= 4 else EV[n + 4] if n < 3 else EV[3]
                    pe.wait_ge(evacuated, EV_TILE * t + before)
                    for c in range(KC):
                        w = slice((n * KC + c) * P, (n * KC + c + 1) * P)
                        tok = ds(t * TT, TT)
                        last = three_passes(nc, gp[n % 4][:], pw_hi[:, w], pw_lo[:, w],
                                            g["x_hi"][:, c, tok], g["x_lo"][:, c, tok], c == 0, c == KC - 1)
                    last.then_inc(groups, 1)

                def turn_v(t, c):
                    pe.wait_ge(evacuated, EV_TILE * t + EV_TILE + EV[1 + c])
                    pe.wait_ge(v_kept, 2 * t + c + 1)
                    for b in range(BLK):
                        last = nc.tensor.transpose(vp[:, b], vf[c][:, b * P:(b + 1) * P], g["ident"][:])
                    last.then_inc(v_turned, 1)

                def tile(t, s, more):
                    pe.wait_ge(x_rest, t + 2)
                    pe.wait_ge(pw_split, 1)
                    for n in range(3):
                        group(t, s, n)
                    pe.wait_ge(evacuated, EV_TILE * t + EV_TILE + EV[0])
                    wait_first(pe, passed, logits_kept, t + 1)
                    for b in range(BLK):
                        last = nc.tensor.transpose(lp[:, b], lgt[:, b * P:(b + 1) * P], g["ident"][0:E, 0:E])
                    last.then_inc(logits_turned, 1)
                    pe.wait_ge(pw_split, 2)
                    group(t, s, 3)
                    turn_v(t, 0)
                    group(t, s, 4)
                    turn_v(t, 1)
                    if more:
                        turn_x(t + 1, 1 - s)
                    group(t, s, 5)
                    group(t, s, 6)

                pe.wait_ge(ident_in, 16)
                turn_x(0, 0)
                with pe.Fori(0, B // 2 - 1) as i:
                    for s in range(2):
                        tile(2 * i + s, s, True)
                for s in range(2):
                    tile(B - 2 + s, s, s == 0)


def reached(eng, sem, value):
    if not isinstance(value, int) or value > 0:
        eng.wait_ge(sem, value)


def route_and_share(nc, a, g):
    with ExitStack() as ctx:
        sb = lambda n, s, d: ctx.enter_context(nc.sbuf_tensor(n, s, d))
        psum = lambda n, s, d: ctx.enter_context(nc.psum_tensor(n, s, d))
        sem = lambda n: ctx.enter_context(nc.semaphore(n))
        CAND = E + 8
        work, work2 = sb("route_work", [P, BLK, E], F32), sb("route_work2", [P, BLK, E], F32)
        scores = sb("scores", [P, BLK, CAND], F32)
        marked = sb("marked", [P, BLK, CAND], F32)
        top = sb("top", [P, BLK, 8], F32)
        row = sb("row", [P, BLK], F32)
        dense = sb("dense", [P, BLK, E], F32)
        dense_t = sb("dense_t", [E, BLK, P], F32)
        flat = sb("flat", [P, BLK, E], F32)
        f8 = sb("per_expert", [P, BLK * F], F32)
        soft = sb("soft", [P, BLK, SW], F32)
        inv_i = sb("inv_i", [E, E], I32)
        pick = sb("pick", [E, E], F32)
        sw_t = [sb(f"soft_t{s}", [SW, TT], F32) for s in range(2)]
        sw_hi = [sb(f"soft_hi{s}", [E, TT], F32R) for s in range(2)]
        sw_lo = [sb(f"soft_lo{s}", [E, TT], F32R) for s in range(2)]
        turn_ps = psum("route_turn", [SW, BLK, P], F32)
        flat_ps = psum("flat_ps", [P, BLK, E], F32)
        inv_in, prepared, prepared_k = map(sem, "inv_in route_prepared k_prepared".split())
        kept = [sem(f"soft_kept{s}") for s in range(2)]
        first_half, second_half = sem("first_half"), sem("second_half")
        exped, exped2, dense_turned, dense_copied, picked, soft_turned, soft_copied, soft_rounded, soft_split = map(
            sem, "sm_exped se_exped dense_turned dense_copied picked soft_turned soft_copied soft_rounded soft_split".split())
        passed = sem("route_passed")
        N1, N2 = 9, 8
        sh_hi, sh_lo = sb("sh_hi", [P, SG + SD], F32R), sb("sh_lo", [P, SG + SD], F32R)
        sg = [sb(f"silu{s}", [P, TT], F32) for s in range(2)]
        h_hi = [sb(f"h_hi{s}", [P, TT], F32R) for s in range(3)]
        h_lo = [sb(f"h_lo{s}", [P, TT], F32R) for s in range(3)]
        gu = [[psum(f"gu{j}{s}", [P, TT], F32) for s in range(2)] for j in range(2)]
        out_ps = psum("out_ps", [P, KC, TT], F32)
        w_rounded, w_split = sem("sh_w_rounded"), sem("sh_w_split")
        y_in = [sem(f"sh_y_in{s}") for s in range(2)]
        gate_up, gated, product, h_rounded, h_ready, summed, added = map(
            sem, "sh_gate_up sh_gated sh_product sh_rounded sh_ready sh_summed sh_added".split())
        W1 = lambda c, m: slice((m * KC + c) * P, (m * KC + c + 1) * P)
        W2 = lambda i, m: slice(SG + i * C + m * P, SG + i * C + (m + 1) * P)
        PARTS = [slice(j * SG // 3, (j + 1) * SG // 3) for j in range(3)] + [slice(SG, SG + SD)]

        def tiles(eng, tile):
            tile(0, 0, True)
            with eng.Fori(0, B // 2 - 1) as i:
                tile(2 * i + 1, 1, False)
                tile(2 * i + 2, 0, False)
            tile(B - 1, 1, False)

        slot_of = lambda s, j: (3 * s + j) % 2
        tokens = lambda t: ds(t * TT, TT)
        with nc.Block() as block:
            @block.sync
            def _(sp):
                def load_y(t, s):
                    sp.dma_start(g["y"][:, :, tokens(t)], a["x_t"].rearrange("(c p) t -> p c t", p=P)[:, :, tokens(t)]).then_inc(y_in[s], 16)

                def keep(t, s):
                    wait_first(sp, passed, soft_copied, t + 1)
                    sp.dma_start(g["sw_scr"][:, tokens(t)], sw_t[s][:]).then_inc(kept[s], 16)
                    wait_first(sp, passed, soft_split, t + 1)
                    for part, src in enumerate((sw_hi, sw_lo, sw_hi)):
                        sp.dma_start(g["cat_scr"][:, part * K:(part + 1) * K, tokens(t)], src[s][:].bitcast(F32)).then_inc(kept[s], 16)

                for s in range(2):
                    sp.sem_inc(kept[s], 64)
                sp.sem_inc(soft_rounded, 1)
                sp.sem_inc(soft_turned, 1)
                sp.dma_start(inv_i[:], a["inv"].to_broadcast([E, E])).then_inc(inv_in, 16)
                load_y(0, 0)
                load_y(1, 1)
                for q in range(2):
                    fetch_qk(sp, g, 0, q)
                    fetch_piece(sp, a, g, 0, q)
                fetch_mask(sp, a, g, 0)

                def tile(t, s, first):
                    if not first:
                        keep(t - 1, 1 - s)
                        wait_first(sp, passed, added, t)
                        if not (isinstance(t, int) and t == B - 1):
                            load_y(t + 1, 1 - s)
                tiles(sp, tile)
                keep(B - 1, 1)
                for s in range(2):
                    sp.wait_ge(kept[s], 32 * B + 64)

            @block.vector
            def _(dve):
                bc = lambda v, m: v.unsqueeze(2).broadcast_to([P, v.shape[1], m])
                split = lambda v: v.rearrange("p b (f k) -> p (b f) k", k=K)

                def softmax_a(t):
                    logits = g["logits"][:, ds(t * BLK, BLK), :]
                    base = N1 * t
                    nc.vector.tensor_reduce(row[:], logits, AX, ALU.max).then_inc(first_half, 1)
                    dve.wait_ge(first_half, base + 1)
                    nc.vector.tensor_tensor(work[:], logits, bc(row[:], E), ALU.subtract).then_inc(first_half, 1)

                def softmax_b(t):
                    base = N1 * t
                    wait_first(dve, passed, exped, t + 1)
                    nc.vector.tensor_reduce(row[:], work[:], AX, ALU.add).then_inc(first_half, 1)
                    dve.wait_ge(first_half, base + 3)
                    nc.vector.reciprocal(row[:], row[:]).then_inc(first_half, 1)
                    dve.wait_ge(first_half, base + 4)
                    nc.vector.tensor_tensor(scores[:, :, 0:E], work[:], bc(row[:], E), ALU.mult).then_inc(first_half, 1)
                    wait_first(dve, passed, first_half, base + 5)
                    for b in range(BLK):
                        last = nc.vector.max(top[:, b], scores[:, b, 0:E])
                    last.then_inc(first_half, 1)
                    wait_first(dve, passed, first_half, base + 6)
                    nc.vector.memset(top[:, :, TOPK:8], -1.0).then_inc(first_half, 1)
                    wait_first(dve, passed, first_half, base + 7)
                    for b in range(BLK):
                        last = nc.vector.match_replace(marked[:, b], top[:, b], scores[:, b], -2.0)
                    last.then_inc(first_half, 1)
                    reached(dve, dense_turned, t)
                    dve.wait_ge(first_half, base + 8)
                    nc.vector.scalar_tensor_tensor(dense[:], marked[:, :, 0:E], -2.0, scores[:, :, 0:E], ALU.is_equal, ALU.mult).then_inc(first_half, 1)

                def experts_a(t):
                    base = N2 * t
                    dve.wait_ge(picked, t + 1)
                    nc.vector.tensor_copy(flat[:], flat_ps[:]).then_inc(second_half, 1)
                    dve.wait_ge(soft_turned, t + 1)
                    wait_first(dve, passed, second_half, base + 1)
                    nc.vector.tensor_reduce(soft[:, :, E:SW], flat[:].rearrange("p b (f k) -> p b f k", k=K), AX, ALU.add)
                    nc.vector.tensor_scalar(work2[:], flat[:], 0.0, -1e9, ALU.is_equal, ALU.mult).then_inc(second_half, 1)
                    dve.wait_ge(second_half, base + 2)
                    nc.vector.tensor_tensor(work2[:], work2[:], flat[:], ALU.add).then_inc(second_half, 1)
                    wait_first(dve, passed, second_half, base + 3)
                    nc.vector.tensor_reduce(f8[:], split(work2[:]), AX, ALU.max).then_inc(second_half, 1)
                    dve.wait_ge(second_half, base + 4)
                    nc.vector.tensor_tensor(split(work2[:]), split(work2[:]), bc(f8[:], K), ALU.subtract).then_inc(second_half, 1)

                def experts_b(t):
                    base = N2 * t
                    wait_first(dve, passed, exped2, t + 1)
                    nc.vector.tensor_reduce(f8[:], split(work2[:]), AX, ALU.add).then_inc(second_half, 1)
                    dve.wait_ge(second_half, base + 6)
                    nc.vector.reciprocal(f8[:], f8[:]).then_inc(second_half, 1)
                    dve.wait_ge(second_half, base + 7)
                    nc.vector.tensor_tensor(soft[:, :, 0:E].rearrange("p b (f k) -> p b f k", k=K),
                                            work2[:].rearrange("p b (f k) -> p b f k", k=K),
                                            f8[:].rearrange("p (b f) -> p b f", f=F).unsqueeze(3).broadcast_to([P, BLK, F, K]),
                                            ALU.mult).then_inc(second_half, 1)

                def split_soft(t, s):
                    dve.wait_ge(soft_rounded, t + 2)
                    nc.vector.tensor_tensor(sw_lo[s][:], sw_t[s][0:E], sw_hi[s][:].bitcast(F32), ALU.subtract).then_inc(soft_split, 1)

                def gate(t, s, j):
                    dve.wait_ge(gated, 3 * t + j + 1)
                    slot = slot_of(s, j)
                    nc.vector.tensor_tensor(sg[slot][:], sg[slot][:], gu[slot][1][:], ALU.mult).then_inc(product, 1)

                def loaded(t, s):
                    return 8 * (t + s)

                def add(t, s, count):
                    dve.wait_ge(summed, t + 1)
                    dve.wait_ge(y_in[s], count)
                    v = g["y"][:, :, tokens(t)]
                    nc.vector.tensor_tensor(v, out_ps[:], v, ALU.add).then_inc(added, 1)

                def tile(t, s, first):
                    softmax_a(t)
                    if not first:
                        experts_a(t - 1)
                    gate(t, s, 0)
                    if not first:
                        add(t - 1, 1 - s, loaded(t, s))
                    softmax_b(t)
                    gate(t, s, 1)
                    if not first:
                        experts_b(t - 1)
                    gate(t, s, 2)
                    if not first:
                        split_soft(t - 1, 1 - s)

                for p, cols in enumerate(PARTS):
                    dve.wait_ge(w_rounded, p + 1)
                    nc.vector.tensor_tensor(sh_lo[:, cols], g["shared"][:, cols], sh_hi[:, cols].bitcast(F32), ALU.subtract).then_inc(w_split, 1)
                nc.vector.memset(scores[:, :, E:CAND], -1.0)
                dve.wait_ge(inv_in, 16)
                nc.vector.tensor_copy(pick[:], inv_i[:]).then_inc(prepared, 1)
                dve.wait_ge(prepared, 1)
                nc.vector.tensor_scalar(pick[:], pick[:], g["entry"][0:E, 0:1], None, ALU.is_equal).then_inc(prepared, 1)
                tiles(dve, tile)
                experts_a(B - 1)
                experts_b(B - 1)
                add(B - 1, 1, loaded(B, 0))
                split_soft(B - 1, 1)

            @block.scalar
            def _(act):
                def silu(t, s, j):
                    slot = slot_of(s, j)
                    act.wait_ge(gate_up, 3 * t + j + 1)
                    reached(act, h_ready, 3 * t + j - 1)
                    nc.scalar.activation(sg[slot][:], gu[slot][0][:], ACT.Silu).then_inc(gated, 1)

                def round_h(t, s, j):
                    act.wait_ge(product, 3 * t + j + 1)
                    if j == 2:
                        reached(act, summed, t)
                    nc.scalar.activation(h_hi[j][:], sg[slot_of(s, j)][:], ACT.Copy).then_inc(h_rounded, 1)

                def copy_dense(t):
                    act.wait_ge(dense_turned, t + 1)
                    reached(act, picked, t)
                    nc.scalar.activation(dense_t[:], turn_ps[0:E], ACT.Copy).then_inc(dense_copied, 1)

                def copy_soft(t, s, before):
                    act.wait_ge(soft_turned, t + 2)
                    act.wait_ge(kept[s], before + 64)
                    nc.scalar.activation(sw_t[s][:], turn_ps[:].rearrange("p b t -> p (b t)"), ACT.Copy).then_inc(soft_copied, 1)
                    nc.scalar.activation(sw_hi[s][:], turn_ps[0:E].rearrange("p b t -> p (b t)"), ACT.Copy).then_inc(soft_rounded, 1)

                def tile(t, s, first):
                    silu(t, s, 0)
                    act.wait_ge(first_half, N1 * t + 2)
                    nc.scalar.activation(work[:], work[:], ACT.Exp).then_inc(exped, 1)
                    if not first:
                        act.wait_ge(second_half, N2 * (t - 1) + 5)
                        nc.scalar.activation(work2[:], work2[:], ACT.Exp).then_inc(exped2, 1)
                    round_h(t, s, 0)
                    silu(t, s, 1)
                    round_h(t, s, 1)
                    silu(t, s, 2)
                    copy_dense(t)
                    if not first:
                        copy_soft(t - 1, 1 - s, 32 * (t - 2 + s))
                    round_h(t, s, 2)

                for p, cols in enumerate(PARTS):
                    if p == 0:
                        act.wait_ge(g["shared_in"], 16)
                    nc.scalar.activation(sh_hi[:, cols], g["shared"][:, cols], ACT.Copy).then_inc(w_rounded, 1)
                tiles(act, tile)
                act.wait_ge(second_half, N2 * (B - 1) + 5)
                nc.scalar.activation(work2[:], work2[:], ACT.Exp).then_inc(exped2, 1)
                copy_soft(B - 1, 1, 32 * (B - 2))

            @block.gpsimd
            def _(pool):
                for s in range(2):
                    nc.gpsimd.memset(g["k_st"][s][KS:KM], 1.0).then_inc(prepared_k, 1)
                pool.wait_ge(prepared_k, 2)

                def tile(t, s, first):
                    for j in range(3):
                        pool.wait_ge(h_rounded, 3 * t + j + 1)
                        nc.gpsimd.tensor_tensor(h_lo[j][:], sg[slot_of(s, j)][:], h_hi[j][:].bitcast(F32), ALU.subtract).then_inc(h_ready, 1)
                tiles(pool, tile)

            @block.tensor
            def _(pe):
                def gates(t, s, j, first):
                    slot = slot_of(s, j)
                    if first:
                        pe.wait_ge(w_split, j + 1)
                    reached(pe, product, 3 * t + j - 1)
                    for r in range(2):
                        for c in range(KC):
                            w = W1(c, 2 * j + r)
                            last = three_passes(nc, gu[slot][r][:], sh_hi[:, w], sh_lo[:, w],
                                                g["x_hi"][:, c, tokens(t)], g["x_lo"][:, c, tokens(t)], c == 0, c == KC - 1)
                    last.then_inc(gate_up, 1)

                def down(t, j, first=False):
                    if first:
                        pe.wait_ge(w_split, len(PARTS))
                    pe.wait_ge(h_ready, 3 * t + j + 1)
                    if j == 0:
                        reached(pe, added, t)
                    for m in range(KC):
                        last = three_passes(nc, out_ps[:, m], sh_hi[:, W2(j, m)], sh_lo[:, W2(j, m)],
                                            h_hi[j][:], h_lo[j][:], j == 0, j == 2)
                    if j == 2:
                        last.then_inc(summed, 1)

                def turn(v, rows):
                    for b in range(BLK):
                        last = nc.tensor.transpose(turn_ps[0:rows, b], v[:, b], g["ident"][:])
                    return last

                def turn_dense(t, first):
                    if not first:
                        pe.wait_ge(soft_rounded, t)
                    wait_first(pe, passed, first_half, N1 * t + N1)
                    turn(dense, E).then_inc(dense_turned, 1)

                def turn_soft(t, following):
                    pe.wait_ge(dense_copied, following)
                    wait_first(pe, passed, second_half, N2 * t + N2)
                    turn(soft, SW).then_inc(soft_turned, 1)

                def pick_entries(t):
                    wait_first(pe, passed, dense_copied, t + 1)
                    reached(pe, second_half, N2 * (t - 1) + 1)
                    for b in range(BLK):
                        last = nc.tensor.matmul(flat_ps[:, b], dense_t[:, b], pick[:], start=True, stop=True)
                    last.then_inc(picked, 1)

                def tile(t, s, first):
                    gates(t, s, 0, first)
                    if not first:
                        down(t - 1, 2)
                    gates(t, s, 1, first)
                    down(t, 0, first)
                    gates(t, s, 2, first)
                    turn_dense(t, first)
                    down(t, 1)
                    if not first:
                        turn_soft(t - 1, t + 1)
                    else:
                        pe.wait_ge(prepared, 2)
                    pick_entries(t)
                tiles(pe, tile)
                down(B - 1, 2)
                turn_soft(B - 1, B)


def walk(eng, tile):
    def expert(e, ws, first=False, last=False):
        for t in range(B):
            tile(e, t, ws, first and t == 0, last)

    expert(0, 0, first=True)
    with eng.Fori(0, F // 2 - 1) as i:
        expert(2 * i + 1, 1)
        expert(2 * i + 2, 0)
    expert(F - 1, 1, last=True)


def is_first(e):
    return isinstance(e, int) and e == 0


def fetch_sums(sp, g, sums, signal, b):
    sp.dma_start(sums[:], g["y_heads"][ds(b, 1), :, D].rearrange("o h (k n) -> (o h) k n", n=N_SUMS)).then_inc(signal, 16)


def keep_inverses(sp, g, sums, signal, b):
    sp.dma_start(g["r_scr"][ds(b, 1)].rearrange("o h (k n) -> (o h k) n", n=N_SUMS), sums[:]).then_inc(signal, 16)


def fetch_y(sp, g, y, sums_rep, signal, b):
    for c in range(KC):
        sp.dma_start(y[:, c], g["y_heads"][b, c * 8:c * 8 + 8, 0:D]).then_inc(signal, 16)
        sp.dma_start(sums_rep[:, c], g["r_scr"][b, c * 8:c * 8 + 8].unsqueeze(1).broadcast_to([8, D, TT])).then_inc(signal, 16)


def experts(nc, a, g):
    with ExitStack() as ctx:
        sb = lambda n, s, d: ctx.enter_context(nc.sbuf_tensor(n, s, d))
        psum = lambda n, s, d: ctx.enter_context(nc.psum_tensor(n, s, d))
        sem = lambda n: ctx.enter_context(nc.semaphore(n))
        w = [sb(f"expert_w{s}", [P, WALL], F32R) for s in range(2)]
        wrep = [sb(f"soft_rep{s}", [P, TT], F32) for s in range(2)]
        srep = sb("scalar_rep", [P, TT], F32)
        gate_pair, up_pair = sb("gate_pair", [P, TT], F32R), sb("up_pair", [P, TT], F32R)
        gate_cat, up_cat = sb("gate_cat", [P, TT], F32R), sb("up_cat", [P, TT], F32R)
        low = sb("low", [P, TT], F32)
        GATE, UP = slice(0, 64), slice(64, P)
        h = [sb(f"h{c}", [P, TT], F32) for c in range(2)]
        h_hi = [sb(f"eh_hi{c}", [P, TT], F32R) for c in range(2)]
        h_lo = [sb(f"eh_lo{c}", [P, TT], F32R) for c in range(2)]
        low2 = h[1]
        low_ps = psum("low_ps", [P, TT], F32)
        gu_ps = [psum(f"expert_gu{m}", [P, TT], F32) for m in range(3)]
        out_ps = psum("expert_out", [P, TT], F32)
        raw, aux, raw_in, aux_in = g["raw"], g["aux"], g["raw_in"], g["aux_in"]
        piece_scaled, piece_rounded, piece_split = map(sem, "piece_scaled piece_rounded piece_split".split())
        cat_mm, cat_rounded, cat_ready = map(sem, "cat_mm cat_rounded cat_ready".split())
        PER_SLOT = [(NP + 1) // 2, NP // 2]
        wrep_in = [sem(f"wrep_in{s}") for s in range(2)]
        srep_in, next_cat_in, gate_cat_in, up_cat_in = map(sem, "srep_in next_cat_in gate_cat_in up_cat_in".split())
        zeroed = sem("zeroed")
        low_done, weighted, low_rounded, low_copied, low_ready = map(
            sem, "low_done weighted low_rounded low_copied low_ready".split())
        gu_done, gated, opened, product, scaled, h_rounded, h_ready = map(
            sem, "gu_done gated opened product scaled h_rounded h_ready".split())
        low2_done, weighted2, low2_rounded, low2_ready = map(sem, "low2_done weighted2 low2_rounded low2_ready".split())
        out_done, added = sem("expert_out_done"), sem("expert_added")
        WXS = lambda c, m: slice((c * 4 + m) * P, (c * 4 + m + 1) * P)
        LOW, A, CC, BB = range(4)
        S_HI = lambda m: slice(WX + m * P, WX + (m + 1) * P)
        S_LO = lambda m: slice(SL + m * P, SL + (m + 1) * P)
        WDS = lambda c, m: slice(WX + WS + (c * 3 + m) * P, WX + WS + (c * 3 + m + 1) * P)
        lo = lambda sl: slice(sl.start + WE + (P if sl.start >= WX else 0), sl.stop + WE + (P if sl.start >= WX else 0))
        IRP = 64
        HALVES = ((0, slice(0, P)), (1, slice(0, IR)))
        q_st, k_st, qk_in = g["q_st"], g["k_st"], g["qk_in"]
        v_st = sb("v_stack", [P, BLK, HQ * 32], F32)
        mx = sb("row_max", [P, HQ * BLK], F32)
        mrest = sb("row_max_rest", [P, HQ * BLK], F32)
        mparts = sb("row_max_parts", [P, 3, HQ * BLK], BF16)
        m_t = sb("row_max_t", [3 * HQ * BLK, P], BF16)
        prob = sb("prob", [P, HQ, P_W], F32)
        y_out = low
        sums = sb("sums", [P, N_SUMS], F32)
        ma_ps = psum("max_ps", [P, TT], F32)
        s_ps = psum("score_ps", [P, TT], F32)
        y_ps = psum("y_ps", [P, TT], F32)
        sums_in, inverted, r_kept = map(sem, "sums_in sums_inverted r_kept".split())
        v_in, m_in, y_kept, passed = sem("v_in"), sem("m_in"), sem("y_kept"), sem("passed")
        row_scored, maxed, m_part, m_turned, m_copied = map(sem, "row_scored maxed m_part m_turned m_copied".split())
        scored, exped, masked, mixed, y_copied = map(sem, "scored exped masked mixed y_copied".split())
        NLOAD = (len(Q_RUNS) + len(K_RUNS)) * 16
        NBLOCK = HQ * BLK
        NGROUP = 10
        ROWS_AT = ["x0b", "x1a", "x1b", "x2a", "x2b", "L2", "LR", "O1"]
        BLOCK_OF = [0, 1, 4, 5, 2, 3, 6, 7]
        def bank_of(t, at):
            if t % 2 == 1:
                return (y_ps if at in ("x1a", "x2a") else ma_ps), (2 if at in ("x1a", "x1b", "x2a", "x2b") else 1)
            return (s_ps if at == "x2a" else ma_ps), (2 if at in ("x2a", "x2b") else 1)

        GROUP_AT = [{"L2": 0, "O0": 1, "LR": 2, "O1": 3}, {"x0a": 4, "x0b": 5, "x1b": 6, "x2b": 7, "L2": 8, "O0": 9}]
        last_step = 8 * F - 1
        CAT_PARTS = ((slice(64, 96), slice(SL + P, SL + 3 * P), slice(P, 3 * P)),
                     (slice(96, P), slice(SL, SL + P), slice(0, P)),
                     (slice(0, 64), slice(SL + 3 * P, SL + 4 * P), slice(3 * P, 4 * P)))
        ROUND_AT = [(), (0, 1), (), (), (2, 3), (), (4,), ()]
        SPLIT_AT = [(), (), (0, 1), (), (), (3,), (), (4,)]
        m_turned_out = s_ps[0:3 * HQ * BLK, 0:P // 2].bitcast(BF16)

        with nc.Block() as block:
            @block.sync
            def _(sp):
                def load_wrep(n, e, t):
                    s, tok = t % 2, slice(t * TT, (t + 1) * TT)
                    reached(sp, weighted2, n - 1)
                    for half in range(2):
                        sp.dma_start(wrep[s][half * 64:half * 64 + 64], g["sw_scr"][ds(e * K, K), tok].unsqueeze(1).broadcast_to([K, R, TT])).then_inc(wrep_in[s], 16)

                def stack_of(e, t):
                    e, t = e + t // B, t % B
                    return g["cat_scr"][ds(e, 1), :, t * TT:(t + 1) * TT].rearrange("o k t -> (o k) t")

                def load_next_cat(e, t):
                    sp.dma_start(gate_cat[96:96 + 3 * K].bitcast(F32), stack_of(e, t)).then_inc(next_cat_in, 16)

                def load_cats(n, e, t):
                    reached(sp, gu_done, 3 * n)
                    sp.dma_start(up_cat[0:3 * K].bitcast(F32), stack_of(e, t)).then_inc(up_cat_in, 16)
                    wait_first(sp, passed, low_done, n + 1)
                    sp.dma_start(gate_cat[64:64 + 3 * K].bitcast(F32), stack_of(e, t)).then_inc(gate_cat_in, 16)

                def load_srep(n, e, t):
                    reached(sp, scaled, 2 * n)
                    sp.dma_start(srep[:], g["sw_scr"][ds(e + E, 1), t * TT:(t + 1) * TT].to_broadcast([P, TT])).then_inc(srep_in, 16)

                def load_piece(f, p):
                    slot = p % 2
                    reached(sp, piece_split, NP * f + (0, 0, 1, 2, 4)[p])
                    if p == 2:
                        wait_first(sp, passed, cat_mm, f + 1)
                    fetch_piece(sp, a, g, f, p)

                def load_mask(f):
                    reached(sp, piece_scaled, 2 * f)
                    fetch_mask(sp, a, g, f)

                def load_scales(f, p):
                    cols = slice(0, 3 * P) if p == 2 else slice(3 * P, 3 * P + C)
                    if p == 2:
                        sp.wait_ge(cat_mm, f + 1)
                    else:
                        sp.wait_ge(piece_scaled, 2 * f + 1)
                    sp.dma_start(aux[:, 0:cols.stop - cols.start], a["scales"][ds(f, 1), cols].to_broadcast([P, cols.stop - cols.start])).then_inc(aux_in, 16)

                def load_weights(f, t):
                    if t == 0:
                        load_piece(f, 0)
                        load_piece(f, 1)
                        load_mask(f)
                    elif t == 2:
                        load_scales(f, 2)
                        load_piece(f, 2)
                        load_piece(f, 3)
                    elif t == 5:
                        load_scales(f, 4)
                        load_piece(f, 4)

                def load_v(b, q):
                    sp.dma_start(v_st[:], g["v_scr"][ds(b, 1)].rearrange("o p (k n) -> p (o k) n", k=BLK)[:, :, q * HQ * 32:(q + 1) * HQ * 32]).then_inc(v_in, 16)

                def keep_y(b, q):
                    sp.dma_start(g["y_scr"][ds(b, 1), q].rearrange("o p t -> (o p) t"), y_out[:]).then_inc(y_kept, 16)

                def invert_sums(b, t):
                    if t == 2:
                        wait_first(sp, passed, y_kept, 16 * NQ * (b + 1))
                        fetch_sums(sp, g, sums, sums_in, b)
                    elif t == 4:
                        wait_first(sp, passed, inverted, b + 1)
                        keep_inverses(sp, g, sums, r_kept, b)

                def step(e, t, ws, first, last):
                    n, q = 8 * e + t, t // 2
                    quad = 4 * e + q
                    if not is_first(e):
                        invert_sums(e - 1, t)
                    more = not (last and t == B - 1)
                    following = (n + 1, e, t + 1) if t < B - 1 else (n + 1, e + 1, 0)
                    if t % 2 == 0:
                        sp.wait_ge(m_copied, quad + 1)
                        sp.dma_start(q_st[q % 2][KS:KM].rearrange("j h t -> j (h t)").rearrange("j (n t) -> j n t", t=P), m_t[:]).then_inc(m_in, 16)
                        if not first:
                            wait_first(sp, passed, y_copied, quad)
                            if t == 0:
                                keep_y(e - 1, NQ - 1)
                            else:
                                keep_y(e, q - 1)
                            load_v(e, q)
                    if more:
                        load_wrep(*following)
                    if t % 2 == 1 and not (last and q >= NQ - 2):
                        wait_first(sp, passed, scored, NGROUP * quad + NGROUP)
                        if q < NQ - 2:
                            fetch_qk(sp, g, e, q + 2)
                        else:
                            fetch_qk(sp, g, e + 1, q - 2)
                    if more:
                        load_srep(*following)
                        load_cats(n + 1, e, t + 1)
                    if not (last and t >= B - 2):
                        load_next_cat(e, t + 2)
                    if not last:
                        load_weights(e + 1, t)
                    elif t == 1:
                        sp.dma_start(raw[0][:], a["shared"][:, SG + SD:SALL]).then_inc(g["wo_in"], 16)
                    elif t == 6:
                        sp.wait_ge(scored, NGROUP * (NQUAD - 1))
                        sp.wait_ge(r_kept, 16)
                        fetch_y(sp, g, g["yp0"], g["sums_rep0"], g["y_in0"], 0)

                load_weights(0, 2)
                sp.wait_ge(zeroed, 1)
                load_v(0, 0)
                load_next_cat(0, 0)
                load_wrep(0, 0, 0)
                load_srep(0, 0, 0)
                load_weights(0, 5)
                load_cats(0, 0, 0)
                load_next_cat(0, 1)
                walk(sp, step)
                sp.wait_ge(y_copied, NQUAD)
                keep_y(B - 1, NQ - 1)
                sp.wait_ge(y_kept, 16 * NQUAD)
                sp.wait_ge(r_kept, 16 * (B - 1))

            @block.vector
            def _(dve):
                def weight(n, e, t):
                    s = t % 2
                    dve.wait_ge(low_done, n + 1)
                    dve.wait_ge(wrep_in[s], 32 * (4 * e + t // 2) + 32)
                    nc.vector.tensor_tensor(low[:], low_ps[:], wrep[s][:], ALU.mult).then_inc(weighted, 1)

                def weight2(n, s, between=None):
                    dve.wait_ge(low2_done, n + 1)
                    nc.vector.tensor_tensor(low2[IRP:P], low_ps[IRP:P], wrep[s][IRP:P], ALU.mult).then_inc(weighted2, 1)
                    if between:
                        between("L2")
                    dve.wait_ge(low2_rounded, n + 1)
                    nc.vector.tensor_tensor(h_lo[1][IRP:P], low2[IRP:P], h_hi[1][IRP:P].bitcast(F32), ALU.subtract).then_inc(low2_ready, 1)

                def add(n, t, c):
                    dve.wait_ge(out_done, 2 * n + c + 1)
                    v = g["y"][:, c, t * TT:(t + 1) * TT]
                    nc.vector.tensor_tensor(v, out_ps[:], v, ALU.add).then_inc(added, 1)

                def finish_cat(f, ws):
                    dve.wait_ge(cat_rounded, f + 1)
                    for rows, dst, src in CAT_PARTS:
                        v = w[ws][rows, dst]
                        last = nc.vector.scalar_tensor_tensor(v, v.bitcast(F32), g["cat_sign"][rows, 0:1], y_ps[rows, src], ALU.mult, ALU.add)
                    last.then_inc(cat_ready, 1)

                def split_second(f, ws):
                    dve.wait_ge(piece_rounded, NP * f + 3)
                    for rows, src, dst in ((GATE, 0, 1), (UP, 2, 3)):
                        last = nc.vector.tensor_tensor(w[ws][rows, SL + dst * P:SL + (dst + 2) * P], raw[0][rows, src * P:(src + 2) * P],
                                                       w[ws][rows, WX + src * P:WX + (src + 2) * P].bitcast(F32), ALU.subtract)
                    last.then_inc(piece_split, 1)

                def scale_third(f):
                    dve.wait_ge(aux_in, 16 * (3 * f + 3))
                    dve.wait_ge(raw_in[0], 16 * (PER_SLOT[0] * f + 3))
                    v = raw[0][64:P, P:3 * P]
                    nc.vector.tensor_tensor(v, v, aux[64:P, 0:C], ALU.mult).then_inc(piece_scaled, 1)

                def maximum(quad, k, bank):
                    x = k - k % 8 + BLOCK_OF[k % 8]
                    wd = (x % BLK + 1) * P
                    wait_first(dve, passed, row_scored, NBLOCK * quad + k + 1)
                    nc.vector.tensor_tensor_reduce(out=bank[:, 0:wd], in0=bank[:, 0:wd], in1=g["causal_bf"][:, TT - wd:TT],
                                                   scale=1.0, scalar=NEG, op0=ALU.add, op1=ALU.max,
                                                   accum_out=mx[:, x:x + 1]).then_inc(maxed, 1)

                def split_max(quad):
                    dve.wait_ge(maxed, NBLOCK * quad + NBLOCK)
                    reached(dve, m_turned, quad)
                    nc.vector.tensor_scalar(mparts[:, 0], mx[:], -1.0, None, ALU.mult).then_inc(m_part, 1)
                    dve.wait_ge(m_part, 4 * quad + 1)
                    nc.vector.scalar_tensor_tensor(mrest[:], mx[:], -1.0, mparts[:, 0], ALU.mult, ALU.subtract).then_inc(m_part, 1)
                    dve.wait_ge(m_part, 4 * quad + 2)
                    nc.vector.tensor_copy(mparts[:, 1], mrest[:]).then_inc(m_part, 1)
                    dve.wait_ge(m_part, 4 * quad + 3)
                    nc.vector.tensor_tensor(mparts[:, 2], mrest[:], mparts[:, 1], ALU.subtract).then_inc(m_part, 1)

                def copy_y(quad, n):
                    dve.wait_ge(mixed, quad + 1)
                    dve.wait_ge(low_ready, 2 * n + 2)
                    reached(dve, y_kept, 16 * quad)
                    nc.vector.tensor_copy(y_out[:], y_ps[:]).then_inc(y_copied, 1)

                def step(e, t, ws, first, last):
                    n, q = 8 * e + t, t // 2
                    quad = 4 * e + q
                    before = (t - 1) % B
                    ahead = not (last and q == NQ - 1)
                    def attend(at):
                        if ahead:
                            maximum(quad + 1, 8 * (t % 2) + ROWS_AT.index(at), bank_of(t, at)[0])
                    if first:
                        weight(0, 0, 0)
                    attend("x0b")
                    attend("x1a")
                    if t % 2 == 0:
                        dve.wait_ge(m_turned, quad + 1)
                        reached(dve, m_in, 16 * quad)
                        nc.vector.tensor_copy(m_t[:], m_turned_out).then_inc(m_copied, 1)
                    attend("x1b")
                    attend("x2a")
                    if t == 5 and not last:
                        split_second(e + 1, 1 - ws)
                    if t == 6 and not last:
                        scale_third(e + 1)
                    if t % 2 == 0 and not first:
                        copy_y(quad - 1, n)
                    attend("x2b")
                    if t == 3 and not is_first(e):
                        dve.wait_ge(sums_in, 16 * e)
                        nc.vector.reciprocal(sums[:], sums[:]).then_inc(inverted, 1)
                    if first:
                        attend("L2")
                    else:
                        weight2(n - 1, 1 - t % 2, attend)
                    dve.wait_ge(gated, 2 * n + 1)
                    dve.wait_ge(gu_done, 3 * n + 2)
                    nc.vector.scalar_tensor_tensor(h[0][:], h[0][:], 1.0, gu_ps[0][:], ALU.add, ALU.mult).then_inc(opened, 1)
                    dve.wait_ge(opened, 2 * n + 1)
                    nc.vector.scalar_tensor_tensor(h[0][:], h[0][:], 0.5, gu_ps[1][:], ALU.mult, ALU.mult).then_inc(product, 1)
                    if not first:
                        add(n - 1, before, 0)
                    dve.wait_ge(gated, 2 * n + 2)
                    nc.vector.scalar_tensor_tensor(h[1][64:64 + IR], h[1][0:IR], 1.0, gu_ps[2][0:IR], ALU.add, ALU.mult).then_inc(opened, 1)
                    dve.wait_ge(opened, 2 * n + 2)
                    nc.vector.scalar_tensor_tensor(h[1][0:IR], h[1][64:64 + IR], 0.5, gu_ps[2][64:64 + IR], ALU.mult, ALU.mult).then_inc(product, 1)
                    if not (last and t == B - 1):
                        reached(dve, y_kept, 16 * quad)
                        weight(n + 1, e + (t + 1) // B, (t + 1) % B)
                    attend("LR")
                    if not first:
                        add(n - 1, before, 1)
                    attend("O1")
                    if t == 1 and not last:
                        finish_cat(e + 1, 1 - ws)
                    if t % 2 == 1 and ahead:
                        split_max(quad + 1)

                for k in range(NBLOCK):
                    maximum(0, k, (ma_ps, s_ps)[k % 2])
                    if k == 3:
                        finish_cat(0, 0)
                    elif k == 7:
                        split_second(0, 0)
                    elif k == 13:
                        scale_third(0)
                split_max(0)
                walk(dve, step)
                weight2(last_step, 1)
                add(last_step, B - 1, 0)
                add(last_step, B - 1, 1)
                copy_y(NQUAD - 1, last_step)

            @block.scalar
            def _(act):
                def round_h(n, c, rows):
                    act.wait_ge(scaled, 2 * n + c + 1)
                    reached(act, out_done, 2 * n)
                    nc.scalar.activation(h_hi[c][rows], h[c][rows], ACT.Copy).then_inc(h_rounded, 1)

                def round_piece(f, ws, p):
                    if p in (2, 4):
                        act.wait_ge(piece_scaled, 2 * f + p // 2)
                    else:
                        act.wait_ge(raw_in[p % 2], 16 * (PER_SLOT[p % 2] * f + p // 2 + 1))
                    cols = PIECES[p]
                    nc.scalar.activation(w[ws][:, cols], raw[p % 2][:, 0:cols.stop - cols.start], ACT.Copy).then_inc(piece_rounded, 1)

                def round_cat(f, ws):
                    act.wait_ge(cat_mm, f + 1)
                    for rows, dst, src in CAT_PARTS:
                        last = nc.scalar.activation(w[ws][rows, dst], y_ps[rows, src], ACT.Copy)
                    last.then_inc(cat_rounded, 1)

                def round_low(n):
                    act.wait_ge(weighted, n + 1)
                    for pair, hi in ((gate_pair, GATE), (up_pair, UP)):
                        nc.scalar.activation(pair[hi], low[hi], ACT.Copy).then_inc(low_rounded, 1)

                def copy_low(n):
                    for i, (copy, pair, hi) in enumerate(((gate_cat, gate_pair, GATE), (up_cat, up_pair, UP))):
                        act.wait_ge(low_rounded, 2 * n + i + 1)
                        nc.scalar.activation(copy[hi], pair[hi].bitcast(F32), ACT.Copy).then_inc(low_copied, 1)

                def round_low2(n):
                    act.wait_ge(weighted2, n + 1)
                    nc.scalar.activation(h_hi[1][IRP:P], low2[IRP:P], ACT.Copy).then_inc(low2_rounded, 1)

                def step(e, t, ws, first, last):
                    n, q = 8 * e + t, t // 2
                    quad = 4 * e + q

                    def attend(at):
                        if at not in GROUP_AT[t % 2]:
                            return
                        group = GROUP_AT[t % 2][at]
                        pair, j = group // 5, group % 5
                        if group == 0:
                            reached(act, mixed, quad)
                        act.wait_ge(scored, NGROUP * quad + group + 1)
                        if j < 4:
                            o = prob[:, 2 * pair + j // 2, (j % 2) * TT:(j % 2 + 1) * TT]
                            nc.scalar.activation(o, s_ps[:], ACT.Exp, scale=SCALE).then_inc(exped, 1)
                        else:
                            o = prob[:, 2 * pair:2 * pair + 2, 1024:P_W]
                            nc.scalar.activation(o, s_ps[:].rearrange("p (h t) -> p h t", h=2), ACT.Exp, scale=SCALE).then_inc(exped, 1)

                    if first:
                        round_low(0)
                    attend("x0a")
                    if not first:
                        round_h(n - 1, *HALVES[0])
                    attend("x0b")
                    if not first:
                        round_h(n - 1, *HALVES[1])
                    copy_low(n)
                    attend("x1b")
                    attend("x2b")
                    attend("L2")
                    if not first:
                        round_low2(n - 1)
                    act.wait_ge(gu_done, 3 * n + 1)
                    reached(act, h_ready, 2 * n)
                    nc.scalar.activation(h[0][:], gu_ps[0][:], ACT.Tanh, scale=0.5).then_inc(gated, 1)
                    act.wait_ge(gu_done, 3 * n + 3)
                    reached(act, low2_ready, n)
                    nc.scalar.activation(h[1][0:IR], gu_ps[2][0:IR], ACT.Tanh, scale=0.5).then_inc(gated, 1)
                    attend("O0")
                    attend("LR")
                    if not (last and t == B - 1):
                        round_low(n + 1)
                    attend("O1")
                    if not last:
                        if t == 1:
                            reached(act, out_done, 2 * 8 * e)
                            round_cat(e + 1, 1 - ws)
                        for p in ROUND_AT[t]:
                            round_piece(e + 1, 1 - ws, p)

                round_piece(0, 0, 0)
                round_piece(0, 0, 1)
                round_cat(0, 0)
                for p in range(2, NP):
                    round_piece(0, 0, p)
                walk(act, step)
                for half in HALVES:
                    round_h(last_step, *half)
                round_low2(last_step)

            @block.gpsimd
            def _(pool):
                def rest_low(n):
                    for i, (pair, hi, rest) in enumerate(((gate_pair, GATE, UP), (up_pair, UP, GATE))):
                        if i == 0:
                            reached(pool, scaled, 2 * n)
                        else:
                            pool.wait_ge(low_ready, 2 * n + 1)
                        pool.wait_ge(low_rounded, 2 * n + i + 1)
                        nc.gpsimd.tensor_tensor(pair[rest], low[hi], pair[hi].bitcast(F32), ALU.subtract).then_inc(low_ready, 1)
                    pool.wait_ge(low_ready, 2 * n + 2)

                def rest_h(n):
                    for c, rows in HALVES:
                        pool.wait_ge(h_rounded, 2 * n + c + 1)
                        nc.gpsimd.tensor_tensor(h_lo[c][rows], h[c][rows], h_hi[c][rows].bitcast(F32), ALU.subtract).then_inc(h_ready, 1)

                def scale_second(f):
                    pool.wait_ge(aux_in, 16 * (3 * f + 2))
                    pool.wait_ge(raw_in[0], 16 * (PER_SLOT[0] * f + 2))
                    nc.gpsimd.tensor_tensor(raw[0][:, 0:3 * P], raw[0][:, 0:3 * P], aux[:], ALU.mult)
                    nc.gpsimd.tensor_tensor(raw[0][:, 3 * P:WS], raw[0][:, 3 * P:WS], aux[:, P:2 * P], ALU.mult).then_inc(piece_scaled, 1)

                def split_piece(f, ws, p):
                    cols = PIECES[p]
                    pool.wait_ge(piece_rounded, NP * f + p + 1)
                    nc.gpsimd.tensor_tensor(w[ws][:, lo(cols)], raw[p % 2][:, 0:cols.stop - cols.start],
                                            w[ws][:, cols].bitcast(F32), ALU.subtract).then_inc(piece_split, 1)

                def mask(quad, pair):
                    wait_first(pool, passed, exped, NGROUP * quad + 5 * pair + 5)
                    for i in range(BLK):
                        v = prob[:, 2 * pair:2 * pair + 2, P_OFF[i]:P_OFF[i] + P]
                        nc.gpsimd.affine_select(out=v, in_=v, compare_op=ALU.is_ge, fill=0.0, base=0,
                                                pattern=[[0, 2], [1, P]], channel_multiplier=-1).then_inc(masked, 1)

                def step(e, t, ws, first, last):
                    n = 8 * e + t
                    if first:
                        rest_low(0)
                    else:
                        rest_h(n - 1)
                    if t % 2 == 1:
                        mask(4 * e + t // 2, 0)
                    if not last:
                        if t == 3:
                            scale_second(e + 1)
                        for p in SPLIT_AT[t]:
                            split_piece(e + 1, 1 - ws, p)
                    for c, rows in HALVES:
                        pool.wait_ge(product, 2 * n + c + 1)
                        if c == 0:
                            pool.wait_ge(srep_in, 16 * n + 16)
                        nc.gpsimd.tensor_tensor(h[c][rows], h[c][rows], srep[rows], ALU.mult).then_inc(scaled, 1)
                    if t % 2 == 1:
                        mask(4 * e + t // 2, 1)
                    if not (last and t == B - 1):
                        if t % 2 == 1:
                            pool.wait_ge(masked, 8 * (4 * e + t // 2) + 8)
                        rest_low(n + 1)

                nc.gpsimd.memset(gate_cat[:].bitcast(F32), 0.0)
                nc.gpsimd.memset(up_cat[0:64].bitcast(F32), 0.0)
                for s in range(2):
                    nc.gpsimd.memset(w[s][0:96, S_LO(0)].bitcast(F32), 0.0)
                    nc.gpsimd.memset(w[s][0:64, S_LO(4)].bitcast(F32), 0.0)
                nc.gpsimd.memset(h_hi[1][:].bitcast(F32), 0.0)
                last_set = nc.gpsimd.memset(h_lo[1][:].bitcast(F32), 0.0)
                last_set.then_inc(zeroed, 1)
                for p in range(NP):
                    if p == 2:
                        scale_second(0)
                    else:
                        split_piece(0, 0, p)
                walk(pool, step)
                rest_h(last_step)

            @block.tensor
            def _(pe):
                def from_x(out, m, t, ws, between=None, at=None):
                    tok = slice(t * TT, (t + 1) * TT)
                    for c in range(KC):
                        three_passes(nc, out, w[ws][:, WXS(c, m)], w[ws][:, lo(WXS(c, m))], g["x_hi"][:, c, tok], g["x_lo"][:, c, tok], c == 0, False)
                        if between and c == 0:
                            between(at + "a")

                def low_rank(n, t, ws):
                    pe.wait_ge(next_cat_in, 16 * n + 16)
                    reached(pe, gate_cat_in, 16 * n)
                    reached(pe, weighted2, n - 1)
                    from_x(low_ps[:], LOW, t, ws)
                    nc.tensor.matmul(low_ps[:], w[ws][:, S_LO(0)], gate_cat[:], start=False, stop=True).then_inc(low_done, 1)

                def from_low(n, ws):
                    def add(m, weights, x, stop=False, rows=P):
                        return nc.tensor.matmul(gu_ps[m][:], w[ws][0:rows, weights], x[0:rows], start=False, stop=stop)

                    pe.wait_ge(low_ready, 2 * n + 2)
                    pe.wait_ge(low_copied, 2 * n + 2)
                    add(0, S_HI(0), gate_pair)
                    pe.wait_ge(gate_cat_in, 16 * n + 16)
                    add(0, S_LO(1), gate_cat, True, 96).then_inc(gu_done, 1)
                    add(2, S_LO(2), gate_cat, False, 96)
                    pe.wait_ge(up_cat_in, 16 * n + 16)
                    add(1, S_LO(3), up_cat)
                    add(1, S_HI(2), up_pair, True).then_inc(gu_done, 1)
                    add(2, S_HI(1), gate_pair)
                    add(2, S_HI(3), up_pair)
                    add(2, S_LO(4), up_cat, True).then_inc(gu_done, 1)

                def low_rank2(n, ws, weights_out):
                    pe.wait_ge(h_ready, 2 * n + 2)
                    pe.wait_ge(weighted, weights_out)
                    for c in range(2):
                        last = three_passes(nc, low_ps[:], w[ws][:, WDS(c, 0)], w[ws][:, lo(WDS(c, 0))], h_hi[c][:], h_lo[c][:], c == 0, c == 1)
                    last.then_inc(low2_done, 1)

                def out(n, ws, m):
                    reached(pe, added, 2 * n + m)
                    three_passes(nc, out_ps[:], w[ws][:, WDS(0, 1 + m)], w[ws][:, lo(WDS(0, 1 + m))], h_hi[0][:], h_lo[0][:], True, False)
                    pe.wait_ge(low2_ready, n + 1)
                    three_passes(nc, out_ps[:], w[ws][:, WDS(1, 1 + m)], w[ws][:, lo(WDS(1, 1 + m))], h_hi[1][:], h_lo[1][:],
                                 False, True).then_inc(out_done, 1)

                def row_scores(quad, slot, k, bank, banks):
                    x = k - k % 8 + BLOCK_OF[k % 8]
                    hd, blk = x // BLK, x % BLK
                    reached(pe, maxed, NBLOCK * quad + k + 1 - banks)
                    nc.tensor.matmul(bank[:, 0:(blk + 1) * P], q_st[slot][0:KS, hd, blk * P:(blk + 1) * P],
                                     k_st[slot][0:KS, hd, 0:(blk + 1) * P], start=True, stop=True).then_inc(row_scored, 1)

                def turn_max(quad):
                    reached(pe, exped, NGROUP * quad)
                    wait_first(pe, passed, m_part, 4 * quad + 4)
                    nc.tensor.transpose(m_turned_out, mparts[:].rearrange("p j n -> p (j n)"), g["ident_bf"][:]).then_inc(m_turned, 1)

                def key_scores(quad, slot, group):
                    pair, j = group // 5, group % 5
                    reached(pe, exped, NGROUP * quad + group)
                    for hd, i, at in ([(j // 2, 0, 0)], [(j // 2, 1, 0), (j // 2, 3, 384)], [(j // 2, 0, 0)], [(j // 2, 1, 0), (j // 2, 3, 384)],
                                      [(0, 2, 0), (1, 2, 256)])[j]:
                        hd += 2 * pair
                        last = nc.tensor.matmul(s_ps[:, at:at + TT - i * P], k_st[slot][0:KM, hd, i * P:(i + 1) * P],
                                                q_st[slot][0:KM, hd, i * P:TT], start=True, stop=True)
                    last.then_inc(scored, 1)

                def stack(f):
                    for c in range(KC):
                        pe.wait_ge(raw_in[c], 16 * (PER_SLOT[c] * f + 1))
                        last = nc.tensor.matmul(y_ps[:], aux[:, c * P:(c + 1) * P], raw[c][:], start=(c == 0), stop=(c == KC - 1))
                    last.then_inc(cat_mm, 1)

                def mix(quad, stacked):
                    pe.wait_ge(masked, 8 * quad + 8)
                    pe.wait_ge(v_in, 16 * quad + 16)
                    reached(pe, y_copied, quad)
                    pe.wait_ge(cat_ready, stacked)
                    for i in range(BLK):
                        for hd in range(HQ):
                            last = nc.tensor.matmul(y_ps[32 * hd:32 * hd + 32, i * P:TT], v_st[:, i, 32 * hd:32 * hd + 32],
                                                    prob[:, hd, P_OFF[i]:P_OFF[i] + TT - i * P], start=(i == 0), stop=(i == BLK - 1))
                    last.then_inc(mixed, 1)

                def step(e, t, ws, first, last):
                    n, q = 8 * e + t, t // 2
                    quad = 4 * e + q
                    wp = 1 - ws if t == 0 else ws
                    ahead = not (last and q == NQ - 1)

                    def attend(at):
                        if at in ROWS_AT and ahead:
                            k = 8 * (t % 2) + ROWS_AT.index(at)
                            if k == 0:
                                pe.wait_ge(qk_in[(q + 1) % 2], NLOAD * (2 * e + (q + 1) // 2 + 1))
                            if at == "x2a" and t % 2 == 0:
                                pe.wait_ge(m_copied, quad + 1)
                            row_scores(quad + 1, (q + 1) % 2, k, *bank_of(t, at))
                        if at == "x1a" and t % 2 == 0:
                            turn_max(quad)
                        if at in GROUP_AT[t % 2]:
                            group = GROUP_AT[t % 2][at]
                            if group == 0:
                                pe.wait_ge(m_in, 16 * quad + 16)
                            key_scores(quad, q % 2, group)
                        if at == "x1b" and t % 2 == 0 and not first:
                            mix(quad - 1, e + 1 if t == 0 or last else e + 2)

                    if first:
                        pe.wait_ge(piece_split, NP)
                        pe.wait_ge(cat_ready, 1)
                        low_rank(0, 0, 0)
                    for m in range(3):
                        reached(pe, product, 2 * n - (1 if m < 2 else 0))
                        from_x(gu_ps[m][:], (A, BB, CC)[m], t, ws, attend, f"x{m}")
                        attend(f"x{m}b")
                    if not first:
                        low_rank2(n - 1, wp, n + 1)
                    attend("L2")
                    if t == 1 and not last:
                        pe.wait_ge(aux_in, 16 * (3 * e + 4))
                        reached(pe, y_copied, quad)
                        stack(e + 1)
                    from_low(n, ws)
                    if not first:
                        out(n - 1, wp, 0)
                    attend("O0")
                    if t < B - 1:
                        low_rank(n + 1, t + 1, ws)
                    elif not last:
                        pe.wait_ge(piece_split, NP * (e + 2))
                        pe.wait_ge(cat_ready, e + 2)
                        low_rank(n + 1, 0, 1 - ws)
                    attend("LR")
                    if not first:
                        out(n - 1, wp, 1)
                    attend("O1")

                pe.wait_ge(aux_in, 16)
                stack(0)
                pe.wait_ge(qk_in[0], NLOAD)
                for k in range(NBLOCK):
                    row_scores(0, 0, k, (ma_ps, s_ps)[k % 2], 2)
                walk(pe, step)
                mix(NQUAD - 1, F)
                low_rank2(last_step, 1, last_step + 1)
                out(last_step, 1, 0)
                out(last_step, 1, 1)


def project_out(nc, a, g):
    with ExitStack() as ctx:
        sb = lambda n, s, d: ctx.enter_context(nc.sbuf_tensor(n, s, d))
        psum = lambda n, s, d: ctx.enter_context(nc.psum_tensor(n, s, d))
        sem = lambda n: ctx.enter_context(nc.semaphore(n))
        wo_raw, wo_in = g["raw"][0], g["wo_in"]
        wo = [sb(f"wo{s}", [P, SO], F32R) for s in range(2)]
        wo_rounded, wo_split = sem("wo_rounded"), sem("wo_split")
        sums = sb("last_sums", [P, N_SUMS], F32)
        DEPTH = 4
        yp = [g["yp0"]] + [sb(f"y_packed{s}", [P, KC, TT], F32)[:] for s in range(1, DEPTH)]
        rden = [g["sums_rep0"]] + [sb(f"sums_rep{s}", [P, KC, TT], F32)[:] for s in range(1, DEPTH)]
        yn_hi = [sb(f"yn_hi{s}", [P, KC, TT], F32R) for s in range(2)]
        yn_lo = [sb(f"yn_lo{s}", [P, KC, TT], F32R) for s in range(2)]
        out_ps = [psum(f"attn_out{s}", [P, KC, TT], F32) for s in range(2)]
        sums_in, r_kept, inverted = map(sem, "last_sums_in last_r_kept last_inverted".split())
        y_in = [g["y_in0"]] + [sem(f"y_in{s}") for s in range(1, DEPTH)]
        normed, yn_rounded, yn_ready, projected, added, stored = map(
            sem, "y_normed yn_rounded yn_ready projected o_added o_stored".split())
        WO = lambda c, m: slice(c * C + m * P, c * C + (m + 1) * P)
        with nc.Block() as block:
            @block.sync
            def _(sp):
                fetch_sums(sp, g, sums, sums_in, B - 1)
                for t in range(1, B):
                    s = t % DEPTH
                    if t >= DEPTH:
                        sp.wait_ge(yn_ready, t - DEPTH + 1)
                    if t == DEPTH:
                        sp.wait_ge(inverted, 1)
                        keep_inverses(sp, g, sums, r_kept, B - 1)
                    if t == B - 1:
                        sp.wait_ge(r_kept, 16)
                    fetch_y(sp, g, yp[s], rden[s], y_in[s], t)

            @block.gpsimd
            def _(pool):
                def rest(t):
                    s = t % 2
                    pool.wait_ge(yn_rounded, t + 1)
                    nc.gpsimd.tensor_tensor(yn_lo[s][:], yp[t % DEPTH], yn_hi[s][:].bitcast(F32), ALU.subtract).then_inc(yn_ready, 1)

                for t in range(B + 2):
                    if t < B:
                        rest(t)
                    if t >= 2:
                        pool.wait_ge(added, 2 * t - 2)
                        tok = slice((t - 2) * TT, (t - 1) * TT)
                        pool.dma_start(g["out"].rearrange("(c p) t -> p c t", p=P)[:, :, tok], g["y"][:, :, tok]).then_inc(stored, 16)
                pool.wait_ge(stored, 16 * B)

            @block.vector
            def _(dve):
                def norm(t):
                    s = t % DEPTH
                    dve.wait_ge(y_in[s], 64 * (t // DEPTH + 1))
                    nc.vector.tensor_tensor(yp[s], yp[s], rden[s], ALU.mult).then_inc(normed, 1)

                def add(t):
                    s = t % 2
                    dve.wait_ge(projected, t + 1)
                    for c in range(KC):
                        v = g["y"][:, c, t * TT:(t + 1) * TT]
                        nc.vector.scalar_tensor_tensor(v, out_ps[s][:, c], g["bias"][:, GW + c:GW + c + 1], v, ALU.add, ALU.add).then_inc(added, 1)

                norm(0)
                dve.wait_ge(wo_rounded, 1)
                nc.vector.tensor_tensor(wo[1][:], wo_raw[:], wo[0][:].bitcast(F32), ALU.subtract).then_inc(wo_split, 1)
                dve.wait_ge(sums_in, 16)
                nc.vector.reciprocal(sums[:], sums[:]).then_inc(inverted, 1)
                norm(1)
                for t in range(2, B):
                    norm(t)
                    add(t - 2)
                add(B - 2)
                add(B - 1)

            @block.scalar
            def _(act):
                act.wait_ge(wo_in, 16)
                nc.scalar.activation(wo[0][:], wo_raw[:], ACT.Copy).then_inc(wo_rounded, 1)
                for t in range(B):
                    s = t % 2
                    act.wait_ge(normed, t + 1)
                    if t >= 2:
                        act.wait_ge(projected, t - 1)
                    nc.scalar.activation(yn_hi[s][:], yp[t % DEPTH], ACT.Copy).then_inc(yn_rounded, 1)

            @block.tensor
            def _(pe):
                pe.wait_ge(wo_split, 1)
                for t in range(B):
                    s = t % 2
                    pe.wait_ge(yn_ready, t + 1)
                    if t >= 2:
                        pe.wait_ge(added, 2 * t - 2)
                    for m in range(KC):
                        for c in range(KC):
                            last = three_passes(nc, out_ps[s][:, m], wo[0][:, WO(c, m)], wo[1][:, WO(c, m)],
                                                yn_hi[s][:, c], yn_lo[s][:, c], c == 0, c == KC - 1)
                    last.then_inc(projected, 1)


def build(nc, a, out):
    g = {"out": out}
    scratch = lambda n, s, d: nc.dram_tensor(n, s, d, kind="Internal").ap()
    g["qk_scr"] = scratch("qk_scr", [B, NQ, 2, 3, D * HQ, TT], BF16)
    g["v_scr"] = scratch("v_scr", [B, P, BLK * H * 32], F32)
    g["y_scr"] = scratch("y_scr", [B, NQ, P, TT], F32)
    g["y_heads"] = g["y_scr"].rearrange("b q (h d) t -> b (q h) d t", d=32)
    g["r_scr"] = scratch("r_scr", [B, H, TT], F32)
    g["sw_scr"] = scratch("sw_scr", [SW, T], F32)
    g["cat_scr"] = scratch("cat_scr", [F, 3 * K, T], F32)
    with ExitStack() as ctx:
        sb = lambda n, s, d: ctx.enter_context(nc.sbuf_tensor(n, s, d))
        for n, s, d in (("y", [P, KC, T], F32), ("x_hi", [P, KC, T], F32R), ("x_lo", [P, KC, T], F32R), ("bias", [P, GW + KC], F32),
                        ("ident_bf", [P, P], BF16), ("causal_bf", [P, TT], BF16), ("cat_sign", [P, 1], F32)):
            g[n] = sb(n, s, d)
        g["q_st"], g["k_st"] = ([sb(f"{n}_stack{s}", [P, HQ, TT], BF16) for s in range(2)] for n in "qk")
        g["raw"], g["aux"] = [sb(f"piece_raw{s}", [P, 4 * P], F32) for s in range(2)], sb("piece_aux", [P, 3 * P], F32)
        sem = lambda n: ctx.enter_context(nc.semaphore(n))
        g["qk_in"], g["raw_in"] = ([sem(f"{n}{s}") for s in range(2)] for n in ("qk_in", "piece_in"))
        g["aux_in"] = sem("aux_in")
        g["wo_in"], g["y_in0"] = sem("wo_in"), sem("y_in0")
        as_batch = lambda v: v[:].rearrange("p h t -> p (h t)").bitcast(F32).rearrange("p (c t) -> p c t", t=TT)
        g["yp0"], g["sums_rep0"] = as_batch(g["q_st"][0]), as_batch(g["k_st"][0])
        with ExitStack() as before_attention:
            sba = lambda n, s, d: before_attention.enter_context(nc.sbuf_tensor(n, s, d))
            for n, s, d in (("logits", [P, NBLK, E], F32), ("ident", [P, P], F32), ("entry", [P, 1], F32)):
                g[n] = sba(n, s, d)
            g["shared"] = g["y"][:, 0, PW:PW + SG + SD]
            g["consts"] = [(g[n][:], a[n]) for n in ("bias", "cat_sign", "entry")]
            g["shared_in"] = ctx.enter_context(nc.semaphore("shared_in"))
            project(nc, a, g)
            route_and_share(nc, a, g)
        experts(nc, a, g)
        project_out(nc, a, g)


def lay_out(inputs):
    k = {n.replace("L0_attn_", "at_").replace("L0_ffn_", ""): np.asarray(v) for n, v in inputs.items()}
    z = lambda *s: np.zeros(s, np.float32)
    chunks = lambda m: m.reshape(-1, P, m.shape[1]).transpose(1, 0, 2)
    heads = lambda m: m.transpose(1, 0, 2).reshape(C, H * D)
    pad = lambda m, cols: np.concatenate([m, z(m.shape[0], cols - m.shape[1])], 1)
    o = {"x": k["at_x"], "x_t": k["at_x"].reshape(T, C).T}
    groups = [pad(k["gate_weight"].T, P)]
    bias = [z(P)]
    for n in ("v", "q", "k"):
        m, b = heads(k["at_W" + n]), k["at_b" + n].reshape(H * D)
        if n != "v":
            order = np.arange(H * D).reshape(NQ, HQ, D).transpose(0, 2, 1).reshape(-1)
            m, b = m[:, order], b[order]
        groups += [m[:, c * P:(c + 1) * P] for c in range(2)]
        bias += [b[c * P:(c + 1) * P] for c in range(2)]
    o["pw"] = chunks(np.concatenate(groups, 1)).reshape(P, KC, GW, P).transpose(0, 2, 1, 3).reshape(P, PW)
    bias += [k["at_bo"][c * P:(c + 1) * P] for c in range(KC)]
    o["bias"] = np.stack(bias, 1)
    pairs = []
    for i in range(3):
        pairs += [pad(k[n][i * P:(i + 1) * P].T, P) for n in ("sh_gate_W", "sh_up_W")]
    down = np.concatenate([k["sh_down_W"].T, z(3 * P - 2 * I, C)], 0)
    gate_up = chunks(np.concatenate(pairs, 1)).reshape(P, KC, 6, P).transpose(0, 2, 1, 3)
    o["shared"] = np.concatenate([gate_up.reshape(P, SG), chunks(down).reshape(P, SD),
                                  chunks(k["at_Wo"]).reshape(P, SO)], 1)
    o["inv"] = k["inv_mapping"].reshape(1, E)
    third = lambda gate, up: np.concatenate([pad(gate, 64), pad(up, 64)], 1)
    ex, sc = [], []
    for f in range(F):
        gw, uw = k["gate_W"][f].T, k["up_W"][f].T
        low = np.concatenate([k["gate_qa"][f].reshape(K * R, C).T, k["up_qa"][f].reshape(K * R, C).T], 1)
        wx = chunks(np.concatenate([low, gw[:, :P], third(gw[:, P:], uw[:, P:]), uw[:, :P]], 1)).reshape(P, WX)
        qb = [k[n][f].transpose(0, 2, 1).reshape(K * R, -1) for n in ("gate_qb", "up_qb", "down_qb")]
        ws = np.concatenate([qb[0][:, :P], third(qb[0][:, P:], z(64, IR)), qb[1][:, :P], third(z(64, IR), qb[1][:, P:])], 1)
        ws = np.concatenate([ws, ws], 0)
        dw, da = k["down_W"][f].T, k["down_qa"][f].reshape(K * R, I).T
        inner = np.concatenate([z(I, 64), da, dw], 1)
        wd = np.concatenate([inner, z(64 - IR, 3 * P), np.concatenate([z(64, P), qb[2]], 1)], 0)
        mu = k["mask_up_W"][f]
        mu = np.concatenate([mu, mu, mu], 1)
        spread = np.concatenate([pad(mu, 64), pad(mu, 32), pad(mu, 32)], 1)
        ex.append(np.concatenate([wx, ws, chunks(wd).reshape(P, WD), chunks(spread).reshape(P, WM)], 1))
        gs, us = k["gate_scale"][f][None], k["up_scale"][f][None]
        sc.append(np.concatenate([gs[:, :P], third(gs[:, P:], us[:, P:]), us[:, :P], k["down_scale"][f][None]], 1)[0])
    o["experts"], o["scales"] = np.stack(ex), np.stack(sc)
    o["ident"] = np.eye(P, dtype=np.float32)
    causal = z(P, TT)
    causal[:, TT - P:][np.triu_indices(P, 1)] = NEG
    o["causal"] = causal
    sign = z(P, 1)
    sign[2 * K:3 * K] = sign[64 + 2 * K:64 + 3 * K] = sign[96 + 2 * K:96 + 3 * K] = -1.0
    o["cat_sign"] = sign
    o["entry"] = np.arange(P, dtype=np.float32)[:, None]
    return {n: np.ascontiguousarray(v) for n, v in o.items()}


def kernel(**inputs):
    import concourse.bacc as bacc
    from concourse.bass_utils import run_bass_kernel_spmd

    nc = bacc.Bacc("TRN2", target_bir_lowering=False, num_devices=1)
    arrays = lay_out(inputs)
    a = {n: nc.dram_tensor("in_" + n, v.shape, mybir.dt.from_np(v.dtype), kind="ExternalInput").ap() for n, v in arrays.items()}
    out = nc.dram_tensor("out_t", (C, T), F32, kind="ExternalOutput").ap()
    build(nc, a, out)
    r = run_bass_kernel_spmd(nc, [{"in_" + n: v for n, v in arrays.items()}], core_ids=[0])
    return np.ascontiguousarray(r.results[0]["out_t"].T).reshape(B, TT, C)
```
